# Optimizing a Trainium2 kernel written in Bass

```python
import numpy as np
import jax
import jax.numpy as jnp

def _softmax(x, axis=-1):
    return jax.nn.softmax(x, axis=axis)

def _gelu(x):
    return jax.nn.gelu(x, approximate=True)

def _silu(x):
    return jax.nn.silu(x)

def _sigmoid(x):
    return jax.nn.sigmoid(x)

def _layernorm(x, axis=-1, eps=1e-05):
    m = jnp.mean(x, axis=axis, keepdims=True)
    v = jnp.var(x, axis=axis, keepdims=True)
    return (x - m) / jnp.sqrt(v + eps)

def _scatter_add(tgt, idx, src, axis=0):
    return tgt.at[idx].add(src)

def _segment_sum(src, seg, n):
    return jax.ops.segment_sum(src, seg, n)
kernel_name = 'mk_early_fusion_d1_tok_img256_r4_db2d3b'

def setup_inputs(seed: int=0):
    np.random.seed(seed)
    _w = jnp.asarray

    def _rec_inputs():
        import jax
        import jax.numpy as jnp
        _rk = jax.random.key(seed)
        x = -0.000125008 + 0.999885 * jax.random.normal(jax.random.fold_in(_rk, 1), (4, 64, 64, 64), jnp.float32)
        txt = -0.000576576 + 0.0605146 * jax.random.normal(jax.random.fold_in(_rk, 2), (4, 128, 64), jnp.float32)
        return (x, txt)
    x, txt = _rec_inputs()

    def _L0_tok_setup():
        import jax, jax.numpy as jnp
        import numpy as np
        DIM = 64
        NH = 8
        WH, WW = (8, 8)

        def _rope_axis(x, axis):
            half = x.shape[-1]
            inv_freq = 1.0 / 10000.0 ** (jnp.arange(0, half, 2, dtype=jnp.float32) / half)
            pos = jnp.arange(x.shape[axis], dtype=jnp.float32)
            ang = pos[:, None] * inv_freq
            cos, sin = (jnp.cos(ang), jnp.sin(ang))
            shape = [1, 1, 1, ang.shape[-1]]
            shape[axis] = ang.shape[0]
            cos = cos.reshape(shape).astype(x.dtype)
            sin = sin.reshape(shape).astype(x.dtype)
            x1, x2 = (x[..., 0::2], x[..., 1::2])
            r1 = x1 * cos - x2 * sin
            r2 = x1 * sin + x2 * cos
            return jnp.stack([r1, r2], axis=-1).reshape(x.shape)

        def _rope2(x):
            half = x.shape[-1] // 2
            return jnp.concatenate([_rope_axis(x[..., :half], 1), _rope_axis(x[..., half:], 2)], axis=-1)
        key = jax.random.key(seed)
        ks = jax.random.split(key, 5)
        B, H, W, C = (32, 64, 64, DIM)
        s = 1.0 / np.sqrt(C)
        return {'x': jax.random.normal(ks[0], (B, H, W, C), dtype=jnp.float32), 'qkv_w': jax.random.uniform(ks[1], (3 * C, C), jnp.float32, -s, s), 'qkv_b': jax.random.uniform(ks[2], (3 * C,), jnp.float32, -s, s), 'proj_w': jax.random.uniform(ks[3], (C, C), jnp.float32, -s, s), 'proj_b': jax.random.uniform(ks[4], (C,), jnp.float32, -s, s)}
    _L0_tok_all = _L0_tok_setup()
    _L0_tok_in = {k: v for k, v in _L0_tok_all.items() if k in ('qkv_w', 'qkv_b', 'proj_w', 'proj_b')}
    del _L0_tok_all

    def _L0_attn_setup():
        import jax, jax.numpy as jnp
        import numpy as np
        key = jax.random.key(seed)
        k1, k2 = jax.random.split(key)
        B, N, F = (4, 1024, 64)
        nodes = jax.random.normal(k1, (B, N, F), dtype=jnp.float32)
        limit = np.sqrt(6.0 / (F + F)).astype(np.float32)
        W = jax.random.uniform(k2, (F, F), dtype=jnp.float32, minval=-limit, maxval=limit)
        return {'nodes': nodes, 'W': W}
    _L0_attn_all = _L0_attn_setup()
    _L0_attn_in = {k: v for k, v in _L0_attn_all.items() if k in ('W',)}
    del _L0_attn_all

    def _L0_ffn_setup():
        import jax, jax.numpy as jnp
        import numpy as np
        B, S, H, F, E, K = (8, 1024, 64, 128, 16, 2)
        EPS = 1e-05
        key = jax.random.key(seed)
        ks = jax.random.split(key, 9)
        sc = 0.02
        return {'x': jax.random.normal(ks[0], (B, S, H), dtype=jnp.float32), 'gate_w': jax.random.normal(ks[1], (H, E), dtype=jnp.float32) * sc, 'gate_b': jnp.zeros((E,), dtype=jnp.float32), 'w1': jax.random.normal(ks[2], (E, H, F), dtype=jnp.float32) * sc, 'b1': jnp.zeros((E, F), dtype=jnp.float32), 'w2': jax.random.normal(ks[3], (E, F, H), dtype=jnp.float32) * sc, 'b2': jnp.zeros((E, H), dtype=jnp.float32), 'gamma': jnp.ones((H,), dtype=jnp.float32), 'beta': jnp.zeros((H,), dtype=jnp.float32)}
    _L0_ffn_all = _L0_ffn_setup()
    _L0_ffn_in = {k: v for k, v in _L0_ffn_all.items() if k in ('gate_w', 'gate_b', 'w1', 'b1', 'w2', 'b2', 'gamma', 'beta')}
    del _L0_ffn_all
    return {'x': x, 'txt': txt, 'L0_tok_qkv_w': _L0_tok_in['qkv_w'], 'L0_tok_qkv_b': _L0_tok_in['qkv_b'], 'L0_tok_proj_w': _L0_tok_in['proj_w'], 'L0_tok_proj_b': _L0_tok_in['proj_b'], 'L0_attn_W': _L0_attn_in['W'], 'L0_ffn_gate_w': _L0_ffn_in['gate_w'], 'L0_ffn_gate_b': _L0_ffn_in['gate_b'], 'L0_ffn_w1': _L0_ffn_in['w1'], 'L0_ffn_b1': _L0_ffn_in['b1'], 'L0_ffn_w2': _L0_ffn_in['w2'], 'L0_ffn_b2': _L0_ffn_in['b2'], 'L0_ffn_gamma': _L0_ffn_in['gamma'], 'L0_ffn_beta': _L0_ffn_in['beta']}

def reference(x, txt, L0_tok_qkv_w, L0_tok_qkv_b, L0_tok_proj_w, L0_tok_proj_b, L0_attn_W, L0_ffn_gate_w, L0_ffn_gate_b, L0_ffn_w1, L0_ffn_b1, L0_ffn_w2, L0_ffn_b2, L0_ffn_gamma, L0_ffn_beta):
    import jax
    import jax.numpy as jnp

    def _L0_tok_ref(x, qkv_w, qkv_b, proj_w, proj_b):
        import jax, jax.numpy as jnp
        import numpy as np
        DIM = 64
        NH = 8
        WH, WW = (8, 8)

        def _rope_axis(x, axis):
            half = x.shape[-1]
            inv_freq = 1.0 / 10000.0 ** (jnp.arange(0, half, 2, dtype=jnp.float32) / half)
            pos = jnp.arange(x.shape[axis], dtype=jnp.float32)
            ang = pos[:, None] * inv_freq
            cos, sin = (jnp.cos(ang), jnp.sin(ang))
            shape = [1, 1, 1, ang.shape[-1]]
            shape[axis] = ang.shape[0]
            cos = cos.reshape(shape).astype(x.dtype)
            sin = sin.reshape(shape).astype(x.dtype)
            x1, x2 = (x[..., 0::2], x[..., 1::2])
            r1 = x1 * cos - x2 * sin
            r2 = x1 * sin + x2 * cos
            return jnp.stack([r1, r2], axis=-1).reshape(x.shape)

        def _rope2(x):
            half = x.shape[-1] // 2
            return jnp.concatenate([_rope_axis(x[..., :half], 1), _rope_axis(x[..., half:], 2)], axis=-1)
        B, H, W, C = x.shape
        hd = C // NH
        N = WH * WW
        xw = x.reshape(B, H // WH, WH, W // WW, WW, C).transpose(0, 1, 3, 2, 4, 5).reshape(-1, N, C)
        qkv = xw @ qkv_w.T + qkv_b
        qkv = qkv.reshape(-1, N, 3, NH, hd).transpose(2, 0, 3, 1, 4)
        q, k, v = (qkv[0], qkv[1], qkv[2])
        q = _rope2(q.reshape(-1, WH, WW, hd)).reshape(-1, NH, N, hd)
        k = _rope2(k.reshape(-1, WH, WW, hd)).reshape(-1, NH, N, hd)
        scale = hd ** (-0.5)
        attn = jax.nn.softmax(q * scale @ jnp.swapaxes(k, -2, -1), axis=-1)
        out = (attn @ v).transpose(0, 2, 1, 3).reshape(-1, N, C)
        out = out.reshape(B, H // WH, W // WW, WH, WW, C).transpose(0, 1, 3, 2, 4, 5).reshape(B, H * W, C)
        return out @ proj_w.T + proj_b

    def _L0_attn_ref(nodes, W):
        import jax, jax.numpy as jnp
        import numpy as np
        F = nodes.shape[-1]
        norm_const = 1.0 / jnp.sqrt(jnp.asarray(F, dtype=nodes.dtype))
        x = jnp.einsum('bnf,fg->bng', nodes, W)
        prods = jnp.einsum('bnf,bmf->bnm', x, nodes)
        att_scores = jax.nn.softmax(prods * norm_const, axis=-1)
        messgs = jnp.einsum('bnm,bmf->bnf', att_scores, nodes)
        return messgs

    def _L0_ffn_ref(x, gate_w, gate_b, w1, b1, w2, b2, gamma, beta):
        import jax, jax.numpy as jnp
        import numpy as np
        B, S, H, F, E, K = (8, 1024, 64, 128, 16, 2)
        EPS = 1e-05
        gate_logits = x @ gate_w + gate_b
        topk_vals, topk_idx = jax.lax.top_k(gate_logits, K)
        topk_w = jax.nn.softmax(topk_vals, axis=-1)
        h = jax.nn.relu(jnp.einsum('bsh,ehf->bsef', x, w1) + b1)
        expert_out = jnp.einsum('bsef,efh->bseh', h, w2) + b2
        sel = jnp.take_along_axis(expert_out, topk_idx[:, :, :, None], axis=2)
        moe = jnp.sum(topk_w[..., None] * sel, axis=2)
        y = x + moe
        mu = jnp.mean(y, axis=-1, keepdims=True)
        var = jnp.var(y, axis=-1, keepdims=True)
        return (y - mu) / jnp.sqrt(var + EPS) * gamma + beta
    h = _L0_tok_ref(x, L0_tok_qkv_w, L0_tok_qkv_b, L0_tok_proj_w, L0_tok_proj_b)
    h = jnp.concatenate([h, txt], axis=1)
    h = h + _L0_attn_ref(_layernorm(h, axis=-1), L0_attn_W)
    h = h + _L0_ffn_ref(_layernorm(h, axis=-1), L0_ffn_gate_w, L0_ffn_gate_b, L0_ffn_w1, L0_ffn_b1, L0_ffn_w2, L0_ffn_b2, L0_ffn_gamma, L0_ffn_beta)
    return h

_drawn_inputs = setup_inputs


def setup_inputs(seed=0):
    import zlib

    import numpy as np

    out = dict(_drawn_inputs(seed))
    spreads = {'L0_ffn_gate_b': (0.0, 0.1),
     'L0_ffn_b1': (0.0, 0.8),
     'L0_ffn_b2': (0.0, 0.348),
     'L0_ffn_gamma': (1.0, 0.2),
     'L0_ffn_beta': (0.0, 0.1)}
    factors = {'txt': 3.319, 'L0_ffn_gate_w': 8.0, 'L0_ffn_w1': 6.884, 'L0_ffn_w2': 6.152}
    for name, (base, spread) in spreads.items():
        noise = np.random.default_rng([zlib.crc32(name.encode()), seed]).standard_normal(out[name].shape)
        drawn = base * np.exp(spread * noise) if base else spread * noise
        out[name] = jnp.asarray(drawn.astype(out[name].dtype))
    for name, factor in factors.items():
        out[name] = (out[name] * factor).astype(out[name].dtype)
    return out
```

```python
from contextlib import ExitStack

import numpy as np
import concourse.bass as bass
from concourse import mybir

F32 = mybir.dt.float32
F32R = mybir.dt.float32r
ALU = mybir.AluOpType
ACT = mybir.ActivationFunctionType
AX = mybir.AxisListType
ds = bass.ds

P = 128
B, SIDE, C = 4, 64, 64
WIN = 8
NH, HD = 8, 8
WTOK = WIN * WIN
NPAIR = B * (SIDE // WIN) ** 2 // 2
QUAD = 4
NQUAD = NPAIR // QUAD
PER = 2 * QUAD
TXT = 128
HEAD_SCALE = HD ** -0.5


def wait_above_zero(eng, sem, count):
    if not isinstance(count, int) or count > 0:
        eng.wait_ge(sem, count)


def run_turns(eng, turn):
    turns = NPAIR // PER
    turn(0, "first")
    with eng.Fori(1, turns - 1) as i:
        turn(i, "mid")
    turn(turns - 1, "last")
    turn(turns, "tail")


def runs(kind, k, lag):
    return k >= lag if kind == "first" else k < lag if kind == "tail" else True


def window_attention(nc, xw, txt, wqk, wv, wp, cols, trig, hmask, vmask, omask, ident, tokens):
    with ExitStack() as ctx:
        def sb(name, shape, dt=F32):
            return ctx.enter_context(nc.sbuf_tensor(name, shape, dt))

        def ps(name, shape):
            return ctx.enter_context(nc.psum_tensor(name, shape, F32))

        def sem(name):
            return ctx.enter_context(nc.semaphore(name))

        wqk_s = sb("wqk_s", [P, 4, P])
        wv_s = sb("wv_s", [P, P])
        wp_s = sb("wp_s", [P, P])
        cols_s = sb("cols_s", [P, 8])
        trig_s = sb("trig_s", [P, 2, WTOK])
        hmask_s = sb("hmask_s", [P, NH])
        vmask_s = sb("vmask_s", [P, P])
        omask_s = sb("omask_s", [P, P])
        ident_s = sb("ident_s", [P, P])
        x_s = sb("x_s", [P, 2, QUAD, 2, WTOK])
        turned = sb("turned", [P, 4, QUAD * WTOK])
        k_rot = sb("k_rot", [P, 2, QUAD, WTOK])
        q_diag = sb("q_diag", [P, 2, QUAD, P])
        k_heads = sb("k_heads", [P, 2, QUAD, NH, WTOK])
        v_heads = sb("v_heads", [P, 2, QUAD, P])
        s_max = sb("s_max", [P, 2, NH])
        s_low = sb("s_low", [P, 2, NH, WTOK])
        probs = sb("probs", [P, 2, NH, WTOK])
        p_sum = sb("p_sum", [P, 2, NH])
        p_inv = sb("p_inv", [P, 2, NH])
        p_norm = sb("p_norm", [P, 2, NH, WTOK])
        p_turn = sb("p_turn", [P, 2, 4, P])
        o_own = sb("o_own", [P, QUAD, P])
        h_cols = sb("h_cols", [P, QUAD, P])

        proj_a = ps("proj_a", [P, 2, QUAD * WTOK])
        proj_b = ps("proj_b", [P, 2, QUAD * WTOK])
        scores = [ps(f"scores{i}", [P, NH, WTOK]) for i in range(2)]
        p_t = [ps(f"p_t{i}", [P, 4, P]) for i in range(2)]
        o_t = ps("o_t", [P, QUAD, P])
        h_t = ps("h_t", [P, QUAD, P])
        v_ps = proj_a[:].rearrange("p a b -> p (a b)").rearrange("p (q c) -> p q c", q=QUAD)
        rows_ps = proj_b[:].rearrange("p a b -> p (a b)").rearrange("p (q c) -> p q c", q=QUAD)

        consts_loaded = sem("consts_loaded")
        x_loaded = [sem(f"x_loaded{half}") for half in range(2)]
        text_loaded = sem("text_loaded")
        diag_zero = sem("diag_zero")
        qk_projected = sem("qk_projected")
        v_projected = sem("v_projected")
        turned_ready = sem("turned_ready")
        rotated = sem("rotated")
        k_ready = sem("k_ready")
        v_ready = sem("v_ready")
        scores_ready = sem("scores_ready")
        max_ready = sem("max_ready")
        low_ready = sem("low_ready")
        probs_ready = sem("probs_ready")
        sum_ready = sem("sum_ready")
        inv_ready = sem("inv_ready")
        norm_ready = sem("norm_ready")
        pt_ready = sem("pt_ready")
        pt_copied = sem("pt_copied")
        pv_ready = sem("pv_ready")
        o_ready = sem("o_ready")
        h_ready = sem("h_ready")
        h_copied = sem("h_copied")
        rows_ready = sem("rows_ready")
        rows_copied = sem("rows_copied")

        consts = [(wqk_s[:].rearrange("p a b -> p (a b)"), wqk), (wv_s[:], wv), (wp_s[:], wp), (cols_s[:], cols),
                  (trig_s[:].rearrange("p a b -> p (a b)"), trig), (hmask_s[:], hmask), (vmask_s[:], vmask),
                  (omask_s[:], omask), (ident_s[:], ident)]
        ALL_CONSTS = 16 * len(consts)

        block = ctx.enter_context(nc.Block())

        @block.sync
        def _(sp):
            def load_x(u, half):
                for copy in range(2):
                    sp.dma_start(x_s[:, half, :, copy, :],
                                 xw[ds(u, 1)].rearrange("a p (q t) -> (a p) q t", q=QUAD)).then_inc(x_loaded[half], 16)

            load_x(0, 0)
            for dst, src in consts:
                sp.dma_start(dst, src).then_inc(consts_loaded, 16)
            load_x(1, 1)
            sp.dma_start(tokens[:, NPAIR:NPAIR + B, :], txt.rearrange("b p c -> p b c")).then_inc(text_loaded, 16)

            def refill(i):
                sp.wait_ge(v_projected, 2 * i + 1)
                load_x(2 * i + 2, 0)
                sp.wait_ge(v_projected, 2 * i + 2)
                load_x(2 * i + 3, 1)

            with sp.Fori(0, NQUAD // 2 - 1) as i:
                refill(i)
            sp.wait_ge(text_loaded, 16)

        @block.tensor
        def _(pe):
            def project_qk(u, half, nth):
                pe.wait_ge(x_loaded[half], 32 * nth + 32)
                wait_above_zero(pe, v_ready, u)
                wait_above_zero(pe, rows_copied, u - 3)
                for m in range(4):
                    bank = proj_a if m < 2 else proj_b
                    last = nc.tensor.matmul(bank[:, m % 2, :], wqk_s[:, m, :],
                                            x_s[:, half, :, 0, :], start=True, stop=True)
                last.then_inc(qk_projected, 1)

            def project_v(u, half):
                pe.wait_ge(turned_ready, 4 * u + 4)
                for p in range(QUAD):
                    last = nc.tensor.matmul(v_ps[:, p, :], x_s[:, half, p].rearrange("p a t -> p (a t)"), wv_s[:],
                                            start=True, stop=True)
                last.then_inc(v_projected, 1)

            def score(n, k):
                pe.wait_ge(k_ready, n + 1)
                pe.wait_ge(rotated, 3 * ((n - k) // QUAD + k // QUAD) + 3)
                wait_above_zero(pe, low_ready, n - 1)
                half, p = k // QUAD, k % QUAD
                nc.tensor.matmul(scores[k % 2][:].rearrange("p h t -> p (h t)"), q_diag[:, half, p, :],
                                 k_heads[:, half, p].rearrange("p h t -> p (h t)"),
                                 start=True, stop=True).then_inc(scores_ready, 1)

            def turn_probs(n, k):
                pe.wait_ge(norm_ready, n + 1)
                wait_above_zero(pe, pt_copied, n - 1)
                for j in range(4):
                    last = nc.tensor.transpose(p_t[k % 2][:, j, :],
                                               p_norm[:, k % 2, 2 * j:2 * j + 2, :].rearrange("p h t -> p (h t)"),
                                               ident_s[:])
                last.then_inc(pt_ready, 1)

            def values(n, k, u):
                pe.wait_ge(pt_copied, n + 1)
                half, p = k // QUAD, k % QUAD
                if p == 0:
                    pe.wait_ge(v_ready, u + 1)
                    wait_above_zero(pe, o_ready, u)
                for j in range(4):
                    last = nc.tensor.matmul(o_t[32 * j:32 * j + 32, p, :], v_heads[:, half, p, 32 * j:32 * j + 32],
                                            p_turn[:, k % 2, j, :], start=True, stop=True)
                last.then_inc(pv_ready, 1)

            def project_out(u):
                pe.wait_ge(o_ready, u + 1)
                wait_above_zero(pe, h_copied, u)
                nc.tensor.matmul(h_t[:].rearrange("p q t -> p (q t)"), wp_s[:],
                                 o_own[:].rearrange("p q t -> p (q t)"), start=True, stop=True).then_inc(h_ready, 1)

            def to_rows(u, k, kind):
                pe.wait_ge(h_copied, u + 1)
                if kind in ("first", "mid") or kind == "last" and k == 1:
                    pe.wait_ge(turned_ready, 4 * (u + 3) + 4)
                wait_above_zero(pe, rows_copied, u)
                for p in range(QUAD):
                    last = nc.tensor.transpose(rows_ps[:, p, :], h_cols[:, p, :], ident_s[:])
                last.then_inc(rows_ready, 1)

            def turn(i, kind):
                for k in range(PER):
                    n = i * PER + k
                    if k == 0 and kind != "tail":
                        project_qk(2 * i + 1, 1, i)
                    if k == QUAD and kind in ("first", "mid"):
                        project_qk(2 * i + 2, 0, i + 1)
                    if kind != "tail":
                        score(n, k)
                    if runs(kind, k, 2):
                        turn_probs(n - 2, (k - 2) % PER)
                    if runs(kind, k, 3):
                        values(n - 3, (k - 3) % PER, 2 * i + (k - 3) // QUAD)
                    if k == 3 and kind != "tail":
                        project_v(2 * i + 1, 1)
                    if k == 7 and kind in ("first", "mid"):
                        project_v(2 * i + 2, 0)
                    if kind != "first" and k in (0, 4):
                        project_out(2 * i - 2 + k // 4)
                    if kind != "first" and k in (1, 5):
                        to_rows(2 * i - 2 + k // 4, k, kind)

            pe.wait_ge(consts_loaded, ALL_CONSTS)
            project_qk(0, 0, 0)
            project_v(0, 0)
            run_turns(pe, turn)

        @block.vector
        def _(dve):
            def rotate(u, half):
                dve.wait_ge(qk_projected, u + 1)
                wait_above_zero(dve, rotated, 3 * u)
                for m in range(4):
                    bank = proj_a if m < 2 else proj_b
                    nc.vector.scalar_tensor_tensor(
                        out=turned[:, m, :].rearrange("p (q t) -> p q t", q=QUAD),
                        in0=bank[:, m % 2, :].rearrange("p (q t) -> p q t", q=QUAD),
                        scalar=cols_s[:, m:m + 1],
                        in1=trig_s[:, m % 2:m % 2 + 1, :].broadcast_to([P, QUAD, WTOK]),
                        op0=ALU.add, op1=ALU.mult).then_inc(turned_ready, 1)
                dve.wait_ge(turned_ready, 4 * u + 4)
                wait_above_zero(dve, scores_ready, QUAD * (u - 1))
                wait_above_zero(dve, k_ready, QUAD * (u - 1))
                q1 = turned[:, 0, :].rearrange("p (q t) -> p q t", q=QUAD)
                q2 = turned[:, 1, :].rearrange("p (q t) -> p q t", q=QUAD)
                for w in range(2):
                    r = slice(64 * w, 64 * w + 64)
                    nc.vector.tensor_tensor(q_diag[r, half, :, r], q1[r], q2[r], ALU.add).then_inc(rotated, 1)
                nc.vector.tensor_tensor(k_rot[:, half].rearrange("p q t -> p (q t)"), turned[:, 2, :],
                                        turned[:, 3, :], ALU.add).then_inc(rotated, 1)

            def mask_v(u, half):
                dve.wait_ge(v_projected, u + 1)
                wait_above_zero(dve, pv_ready, QUAD * (u - 1))
                nc.vector.tensor_tensor(v_heads[:, half], v_ps,
                                        vmask_s[:].rearrange("p (a c) -> p a c", a=1).broadcast_to([P, QUAD, P]),
                                        ALU.mult).then_inc(v_ready, 1)

            def lower(n, k):
                dve.wait_ge(scores_ready, n + 1)
                wait_above_zero(dve, low_ready, n - 1)
                nc.vector.tensor_reduce(s_max[:, k % 2, :], scores[k % 2][:], AX.X, ALU.max).then_inc(max_ready, 1)
                dve.wait_ge(max_ready, n + 1)
                wait_above_zero(dve, probs_ready, n - 1)
                nc.vector.tensor_tensor(s_low[:, k % 2], scores[k % 2][:],
                                        s_max[:, k % 2, :].rearrange("p (h a) -> p h a", a=1).broadcast_to([P, NH, WTOK]),
                                        ALU.subtract).then_inc(low_ready, 1)

            def invert(n, k):
                dve.wait_ge(probs_ready, n + 1)
                wait_above_zero(dve, inv_ready, n - 1)
                nc.vector.tensor_reduce(p_sum[:, k % 2, :], probs[:, k % 2], AX.X, ALU.add).then_inc(sum_ready, 1)
                dve.wait_ge(sum_ready, n + 1)
                wait_above_zero(dve, norm_ready, n - 1)
                nc.vector.reciprocal(p_inv[:, k % 2, :], p_sum[:, k % 2, :]).then_inc(inv_ready, 1)

            def own_window(u):
                dve.wait_ge(pv_ready, QUAD * (u + 1))
                wait_above_zero(dve, h_ready, u)
                nc.vector.scalar_tensor_tensor(
                    out=o_own[:], in0=o_t[:], scalar=cols_s[:, 4:5],
                    in1=omask_s[:].rearrange("p (a c) -> p a c", a=1).broadcast_to([P, QUAD, P]),
                    op0=ALU.add, op1=ALU.mult).then_inc(o_ready, 1)

            def keep_rows(u):
                dve.wait_ge(rows_ready, u + 1)
                nc.vector.tensor_copy(tokens[:, ds(QUAD * u, QUAD), :], rows_ps[:, :, 0:C]).then_inc(rows_copied, 1)

            def turn(i, kind):
                for k in range(PER):
                    n = i * PER + k
                    if k == 0 and kind != "tail":
                        rotate(2 * i + 1, 1)
                    if k == QUAD and kind in ("first", "mid"):
                        rotate(2 * i + 2, 0)
                    if kind != "tail":
                        lower(n, k)
                    if runs(kind, k, 1):
                        invert(n - 1, (k - 1) % PER)
                    if k == 3 and kind != "first":
                        own_window(2 * i - 1)
                    if k == 7 and kind != "tail":
                        own_window(2 * i)
                    if k == 3 and kind != "tail":
                        mask_v(2 * i + 1, 1)
                    if k == 7 and kind in ("first", "mid"):
                        mask_v(2 * i + 2, 0)
                    if kind != "first" and k in (2, 6):
                        keep_rows(2 * i - 2 + k // 4)

            nc.vector.memset(q_diag[:], 0.0).then_inc(diag_zero, 1)
            dve.wait_ge(diag_zero, 1)
            dve.wait_ge(consts_loaded, ALL_CONSTS)
            rotate(0, 0)
            mask_v(0, 0)
            run_turns(dve, turn)

        @block.gpsimd
        def _(pool):
            def split_heads(n, k, u):
                half, p = k // QUAD, k % QUAD
                if p == 0:
                    pool.wait_ge(rotated, 3 * u + 3)
                wait_above_zero(pool, scores_ready, n - PER + 1)
                nc.gpsimd.tensor_tensor(k_heads[:, half, p], k_rot[:, half, p:p + 1, :].broadcast_to([P, NH, WTOK]),
                                        hmask_s[:].rearrange("p (h a) -> p h a", a=1).broadcast_to([P, NH, WTOK]),
                                        ALU.mult).then_inc(k_ready, 1)

            def normalize(n, k):
                pool.wait_ge(inv_ready, n + 1)
                wait_above_zero(pool, pt_ready, n - 1)
                nc.gpsimd.tensor_tensor(p_norm[:, k % 2], probs[:, k % 2],
                                        p_inv[:, k % 2, :].rearrange("p (h a) -> p h a", a=1).broadcast_to([P, NH, WTOK]),
                                        ALU.mult).then_inc(norm_ready, 1)

            def turn(i, kind):
                for k in range(PER):
                    n = i * PER + k
                    if kind != "tail":
                        if not (kind == "last" and k >= PER - 2):
                            split_heads(n + 2, (k + 2) % PER, 2 * i + (k + 2) // QUAD)
                    if runs(kind, k, 1):
                        normalize(n - 1, (k - 1) % PER)

            pool.wait_ge(consts_loaded, ALL_CONSTS)
            for k in range(2):
                split_heads(k, k, 0)
            run_turns(pool, turn)

        @block.scalar
        def _(act):
            def exponent(n, k):
                act.wait_ge(low_ready, n + 1)
                wait_above_zero(act, norm_ready, n - 1)
                nc.scalar.activation(probs[:, k % 2], s_low[:, k % 2], ACT.Exp, scale=HEAD_SCALE).then_inc(probs_ready, 1)

            def copy_turned(n, k):
                act.wait_ge(pt_ready, n + 1)
                wait_above_zero(act, pv_ready, n - 1)
                nc.scalar.copy(p_turn[:, k % 2], p_t[k % 2][:]).then_inc(pt_copied, 1)

            def add_bias(u):
                act.wait_ge(h_ready, u + 1)
                wait_above_zero(act, rows_ready, u)
                nc.scalar.activation(h_cols[:], h_t[:], ACT.Identity, bias=cols_s[:, 5:6]).then_inc(h_copied, 1)

            def turn(i, kind):
                for k in range(PER):
                    n = i * PER + k
                    if kind != "tail":
                        exponent(n, k)
                    if runs(kind, k, 2):
                        copy_turned(n - 2, (k - 2) % PER)
                    if kind != "first" and k in (0, 4):
                        add_bias(2 * i - 2 + k // 4)

            act.wait_ge(consts_loaded, ALL_CONSTS)
            run_turns(act, turn)


def window_layout(x, qkv_w, qkv_b, proj_w, proj_b):
    f = np.float32
    nw = SIDE // WIN
    xw = x.reshape(B, nw, WIN, nw // 2, 2, WIN, C)
    xw = xw.transpose(0, 1, 3, 4, 6, 2, 5).reshape(NQUAD, QUAD, 2, C, WTOK)
    xw = xw.transpose(0, 2, 3, 1, 4).reshape(NQUAD, P, QUAD * WTOK)
    swap = np.arange(C) ^ 1
    wq, wk, wv = qkv_w[0:C], qkv_w[C:2 * C], qkv_w[2 * C:3 * C]
    bq, bk, bv = qkv_b[0:C], qkv_b[C:2 * C], qkv_b[2 * C:3 * C]
    wqk = np.zeros((P, 4, P), f)
    for m, w in enumerate((wq, wq[swap], wk, wk[swap])):
        for s in (slice(0, 64), slice(64, 128)):
            wqk[s, m, s] = w.T
    wvx = np.zeros((2, C, 4, 2, 16), f)
    for w in range(2):
        wvx[w, :, :, w, :] = wv.T.reshape(C, 4, 16)
    wpx = np.zeros((4, 2, 16, C), f)
    for w in range(2):
        wpx[:, w] = proj_w.T.reshape(4, 16, C)
    cols = np.zeros((P, 8), f)
    for m, b in enumerate((bq, bq[swap], bk, bk[swap])):
        cols[:, m] = np.concatenate([b, b])
    bvx = np.zeros((4, 2, 16), f)
    for w in range(2):
        bvx[:, w] = bv.reshape(4, 16)
    cols[:, 4] = bvx.reshape(P)
    cols[:, 5] = np.concatenate([proj_b, proj_b])
    half = HD // 2
    freq = (1.0 / 10000.0 ** (np.arange(0, half, 2, dtype=f) / f(half))).astype(f)
    cos, sin = np.zeros((C, WIN, WIN), f), np.zeros((C, WIN, WIN), f)
    for c in range(C):
        d = c % HD
        ang = np.arange(WIN, dtype=f) * freq[(d % half) // 2]
        ang = ang[:, None] + np.zeros((1, WIN), f) if d < half else ang[None, :] + np.zeros((WIN, 1), f)
        cos[c] = np.cos(ang)
        sin[c] = np.sin(ang) if d % 2 else -np.sin(ang)
    trig = np.stack([cos.reshape(C, WTOK), sin.reshape(C, WTOK)], 1)
    trig = np.concatenate([trig, trig]).reshape(P, 2 * WTOK)
    rows = np.arange(P)
    hmask = (((rows % C) // HD)[:, None] == np.arange(NH)[None, :]).astype(f)
    vmask = ((rows // 64)[:, None] == ((rows % 16) // HD)[None, :]).astype(f)
    omask = (((rows % 32) // 16)[:, None] == (rows // 64)[None, :]).astype(f)
    return dict(xw=xw, wqk=wqk.reshape(P, 4 * P), wv=wvx.reshape(P, P), wp=np.tile(wpx.reshape(P, C), (1, 2)), cols=cols, trig=trig,
                hmask=hmask, vmask=vmask, omask=omask, ident=np.eye(P, dtype=f))


TT = 384
CH = TT // P
NT = (SIDE * SIDE + TXT) // P
TILES = NT // CH
KEYS = NT * P
GROUPS = [2] * 13 + [1] * 7
NG = len(GROUPS)
FIRST = [sum(GROUPS[:g]) for g in range(NG)]
LAG = 3
RING = 4
assert NG % RING == 0
NMAX = CH * TILES
MAX_PER = [2] * 9 + [3] * 4 + [1] * 3 + [0] * 4
MAX_FROM = [sum(MAX_PER[:g]) for g in range(NG)]
SHIFT_AT, SHIFT_OUT = 17, 18
OUT_AT = 4
DVE_HIGH = [g for g in range(NG) if g % 3 == 1]
ACT_HIGH = [g for g in range(NG) if g % 3 != 1]
DVE_LOW = 3 / 8
LN_EPS = 1e-5
NORM = C ** -0.5


def above(eng, sem, count):
    if not isinstance(count, int) or count > 0:
        eng.wait_ge(sem, count)


def full_attention(nc, w2x, ident, fold, tokens):
    with ExitStack() as ctx:
        def sb(name, shape, dt=F32):
            return ctx.enter_context(nc.sbuf_tensor(name, shape, dt))

        def ps(name, shape):
            return ctx.enter_context(nc.psum_tensor(name, shape, F32))

        def sem(name):
            return ctx.enter_context(nc.semaphore(name))

        w2x_s = sb("w2x_s", [P, P])
        ident_b = sb("ident_b", [P, P])
        stat = sb("stat", [P, 4, NT])
        fold_s = sb("fold_s", [P, C + 1])
        values_s = sb("values_s", [P, NT, 2 * C], F32R)
        residue = sb("residue", [P, NT, 1])
        keys_t = sb("keys_t", [P, KEYS])
        k_hi = sb("k_hi", [P, KEYS], F32R)
        k_lo = sb("k_lo", [P, KEYS], F32R)
        q_both = sb("q_both", [P, KEYS], F32R)
        centred = keys_t[:, 0:NT * C].rearrange("p (n c) -> p n c", n=NT)
        q_hi = sb("q_hi", [P, KEYS], F32R)
        q_own = sb("q_own", [P, TT], F32R)
        cmax = sb("cmax", [P, CH, TILES])
        neg_max = sb("neg_max", [P, CH, C + 1])
        shared = sb("shared", [P, KEYS])
        probs = shared[:, 0:RING * 2 * TT].rearrange("p (g w) -> p g w", g=RING)
        nodes2 = shared[:].rearrange("p (n a c) -> p n a c", n=NT, a=2)
        p_hi = sb("p_hi", [P, RING, 2 * TT], F32R)
        p_lo = sb("p_lo", [P, RING, 2 * TT], F32R)
        out_cols = sb("out_cols", [P, TT])
        sum_inv = sb("sum_inv", [P, CH, 1])

        s_ps = [ps(f"s_ps{i}", [P, 2, 512]) for i in range(2)]
        max_ps = [ps(f"max_ps{i}", [P, 512]) for i in range(2)]
        o_ps = ps("o_ps", [P, 512])
        turn_ps = ps("turn_ps", [P, 512])

        loaded = sem("b_loaded")
        filled = sem("filled")
        sum_ready = sem("b_sum_ready")
        mean_ready = sem("mean_ready")
        centred_ready = sem("centred_ready")
        square_ready = sem("square_ready")
        var_ready = sem("var_ready")
        std_ready = sem("std_ready")
        rstd_ready = sem("rstd_ready")
        nodes_ready = sem("nodes_ready")
        values_ready = sem("values_ready")
        keys_turned = sem("keys_turned")
        keys_copied = sem("keys_copied")
        k_hi_ready = sem("k_hi_ready")
        k_lo_ready = sem("k_lo_ready")
        q_made = sem("q_made")
        q_rounded = sem("q_rounded")
        q_hi_ready = sem("q_hi_ready")
        q_both_ready = sem("q_both_ready")
        own_ready = sem("own_ready")
        max_made = sem("max_made")
        max_read = sem("max_read")
        neg_ready = sem("neg_ready")
        shift_turned = sem("shift_turned")
        shift_ready = sem("shift_ready")
        s_ready = sem("s_ready")
        p_ready = sem("p_ready")
        act_high = sem("act_high")
        dve_high = sem("dve_high")
        dve_low = sem("dve_low")
        pool_low = sem("pool_low")
        v_high = sem("v_high")
        residue_ready = sem("residue_ready")
        pv_done = sem("pv_done")
        out_copied = sem("out_copied")
        out_turned = sem("out_turned")
        inv_ready = sem("b_inv_ready")
        out_added = sem("out_added")

        block = ctx.enter_context(nc.Block())

        TR = (NT + 3) // 4

        @block.sync
        def _(sp):
            sp.dma_start(w2x_s[:], w2x).then_inc(loaded, 16)
            sp.dma_start(ident_b[:], ident).then_inc(loaded, 16)
            sp.dma_start(fold_s[:], fold).then_inc(loaded, 16)
            sp.wait_ge(loaded, 48)

        def high_ready(eng, b, t, g):
            own, done = (DVE_HIGH, dve_high) if g in DVE_HIGH else (ACT_HIGH, act_high)
            eng.wait_ge(done, len(own) * (TILES * b + t) + own.index(g) + 1)

        def batches(eng, body):
            body(0)
            with eng.Fori(1, B) as b:
                body(b)

        def turns(eng, b, turn):
            turn(b, 0, "first")
            with eng.Fori(1, TILES - 2) as t:
                turn(b, t, "mid")
            turn(b, TILES - 2, "late")
            turn(b, TILES - 1, "last")
            turn(b, TILES, "tail")

        @block.tensor
        def _(pe):
            def prepare(b):
                pe.wait_ge(nodes_ready, b + 1)
                above(pe, p_ready, NG * TILES * b)
                for g in range(TR):
                    if g >= 2:
                        pe.wait_ge(keys_copied, TR * b + g - 1)
                    for m in range(4 * g, min(4 * g + 4, NT)):
                        last = nc.tensor.transpose(s_ps[g % 2][:, 0, (m % 4) * P:(m % 4 + 1) * P],
                                                   nodes2[:, m].rearrange("p a c -> p (a c)"), ident_b[:])
                    last.then_inc(keys_turned, 1)
                for c in range(TILES):
                    pe.wait_ge(keys_copied, TR * b + min(TR, (c + 1) * CH // 4 + 1))
                    if c >= 2:
                        pe.wait_ge(q_both_ready, TILES * b + c - 1)
                        pe.wait_ge(q_hi_ready, TILES * b + c - 1)
                    nc.tensor.matmul(s_ps[c % 2][:, 1, 0:TT], w2x_s[:], keys_t[:, c * TT:(c + 1) * TT],
                                     start=True, stop=True).then_inc(q_made, 1)

            def maximum(b, t, idx):
                made = (TILES * b + t) * NMAX + idx
                j, c = idx // TILES, idx % TILES
                if idx == 0:
                    pe.wait_ge(own_ready, TILES * b + t + 1)
                above(pe, max_read, made if idx == 0 else made - 1)
                nc.tensor.matmul(max_ps[idx % 2][:, 0:TT], q_own[:, j * P:(j + 1) * P], k_hi[:, c * TT:(c + 1) * TT],
                                 start=True, stop=True).then_inc(max_made, 1)

            def turn_shift(b, t):
                pe.wait_ge(neg_ready, TILES * b + t + 1)
                for j in range(CH):
                    last = nc.tensor.transpose(turn_ps[0:C + 1, j * P:(j + 1) * P], neg_max[:, j, :], ident_b[:])
                last.then_inc(shift_turned, 1)

            def scores(b, t, g, kind):
                at = NG * (TILES * b + t) + g
                if g == 0:
                    pe.wait_ge(shift_ready, TILES * b + t + 1)
                above(pe, p_ready, at if kind == "first" and g == 0 else at - 1)
                q = ds(t * TT, TT)
                for r in range(GROUPS[g]):
                    m = FIRST[g] + r
                    if r == 1 and kind in ("first", "mid", "late") and MAX_PER[g]:
                        maximum(b, t + 1, MAX_FROM[g])
                    out = s_ps[g % 2][:, r, 0:TT]
                    nc.tensor.matmul(out, k_hi[:, m * P:(m + 1) * P], q_both[:, q], start=True, stop=False)
                    last = nc.tensor.matmul(out, k_lo[:, m * P:(m + 1) * P], q_hi[:, q], start=False, stop=True)
                last.then_inc(s_ready, 1)

            def gather(b, t, g):
                at = NG * (TILES * b + t) + g
                pe.wait_ge(dve_low, at + 1)
                pe.wait_ge(pool_low, at + 1)
                high_ready(pe, b, t, g)
                if g == 0:
                    above(pe, out_copied, TILES * b + t)
                for r in range(GROUPS[g]):
                    m = FIRST[g] + r
                    for part in (p_hi, p_lo):
                        last = nc.tensor.matmul(o_ps[:, 0:TT], values_s[:, m, :], part[:, g % RING, r * TT:(r + 1) * TT],
                                                start=(m == 0 and part is p_hi), stop=(m == NT - 1 and part is p_lo))
                last.then_inc(pv_done, 1)

            def turn_out(b, t):
                pe.wait_ge(out_copied, TILES * b + t + 1)
                above(pe, out_added, CH * (TILES * b + t))
                for j in range(CH):
                    last = nc.tensor.matmul(turn_ps[:, j * (C + 1):(j + 1) * (C + 1)],
                                            out_cols[:, j * P:(j + 1) * P], fold_s[:], start=True, stop=True)
                last.then_inc(out_turned, 1)

            def turn(b, t, kind):
                for g in range(LAG + 2 if kind == "tail" else NG):
                    if kind != "tail":
                        scores(b, t, g, kind)
                    if kind in ("first", "mid", "late"):
                        for idx in range(MAX_FROM[g] + (GROUPS[g] == 2 and MAX_PER[g] > 0), MAX_FROM[g] + MAX_PER[g]):
                            maximum(b, t + 1, idx)
                    if g < LAG and kind != "first":
                        gather(b, t - 1, g + NG - LAG)
                    if g >= LAG and kind != "tail":
                        gather(b, t, g - LAG)
                    if g == OUT_AT and kind != "first":
                        turn_out(b, t - 1)
                    if g == SHIFT_AT and kind in ("first", "mid", "late"):
                        above(pe, out_added, CH * (TILES * b + t))
                        turn_shift(b, t + 1)

            def batch(b):
                prepare(b)
                pe.wait_ge(k_hi_ready, b + 1)
                for idx in range(NMAX):
                    maximum(b, 0, idx)
                above(pe, out_added, CH * TILES * b)
                turn_shift(b, 0)
                pe.wait_ge(k_lo_ready, b + 1)
                pe.wait_ge(values_ready, b + 1)
                turns(pe, b, turn)

            pe.wait_ge(loaded, 48)
            batches(pe, batch)

        @block.scalar
        def _(act):
            def copy_out(b, t):
                act.wait_ge(pv_done, NG * (TILES * b + t + 1))
                above(act, out_turned, TILES * b + t)
                nc.scalar.copy(out_cols[:], o_ps[:, 0:TT]).then_inc(out_copied, 1)

            def copy_shift(b, t):
                act.wait_ge(shift_turned, TILES * b + t + 1)
                nc.scalar.copy(q_hi[C:C + 1, ds(t * TT, TT)], turn_ps[C:C + 1, 0:TT]).then_inc(shift_ready, 1)

            def turn(b, t, kind):
                for g in range(LAG if kind == "tail" else NG):
                    at = NG * (TILES * b + t) + g
                    n = GROUPS[g]
                    if kind != "tail":
                        act.wait_ge(s_ready, at + 1)
                        if kind == "first" and g == 0:
                            act.wait_ge(values_ready, b + 1)
                        above(act, dve_low, at + 1 - RING)
                        above(act, pool_low, at + 1 - RING)
                        nc.scalar.activation(probs[:, g % RING, 0:n * TT].rearrange("p (r q) -> p r q", r=n),
                                             s_ps[g % 2][:, 0:n, 0:TT], ACT.Exp, scale=NORM).then_inc(p_ready, 1)
                    if kind != "tail" and g in ACT_HIGH:
                        act.wait_ge(p_ready, at + 1)
                        above(act, pv_done, at + 1 - RING)
                        nc.scalar.copy(p_hi[:, g % RING, 0:n * TT], probs[:, g % RING, 0:n * TT]).then_inc(act_high, 1)
                    if g == LAG - 1 and kind != "first":
                        copy_out(b, t - 1)
                    if g == SHIFT_OUT and kind in ("first", "mid", "late"):
                        copy_shift(b, t + 1)

            def batch(b):
                act.wait_ge(centred_ready, 2 * b + 2)
                above(act, dve_low, NG * TILES * b)
                above(act, pool_low, NG * TILES * b)
                nc.scalar.activation(nodes2.rearrange("p n a c -> p (n a c)")[:, 0:NT * C].rearrange("p (n c) -> p n c", n=NT),
                                     centred, ACT.Square).then_inc(square_ready, 1)
                act.wait_ge(var_ready, 2 * b + 2)
                nc.scalar.activation(stat[:, 3, :], stat[:, 2, :], ACT.Sqrt).then_inc(std_ready, 1)
                act.wait_ge(residue_ready, b + 1)
                above(act, pv_done, NG * TILES * b)
                nc.scalar.copy(values_s[:, :, 0:C - 1], nodes2[:, :, 0, 0:C - 1])
                nc.scalar.copy(values_s[:, :, C - 1:C], residue[:]).then_inc(v_high, 1)
                for g in range(TR):
                    act.wait_ge(keys_turned, TR * b + g + 1)
                    w = min(4, NT - 4 * g) * P
                    nc.scalar.copy(keys_t[:, 4 * g * P:4 * g * P + w], s_ps[g % 2][:, 0, 0:w]).then_inc(keys_copied, 1)
                act.wait_ge(values_ready, b + 1)
                for c in range(TILES):
                    act.wait_ge(q_made, TILES * b + c + 1)
                    q = slice(c * TT, (c + 1) * TT)
                    nc.scalar.copy(q_both[:, q], s_ps[c % 2][:, 1, 0:TT]).then_inc(q_rounded, 1)
                    nc.scalar.copy(q_hi[0:C, q], s_ps[c % 2][0:C, 1, 0:TT]).then_inc(q_hi_ready, 1)
                copy_shift(b, 0)
                turns(act, b, turn)

            batches(act, batch)

        @block.gpsimd
        def _(pool):
            def turn(b, t, kind):
                for g in range(0 if kind == "tail" else NG):
                    w = GROUPS[g] * TT
                    own = slice(int(w * DVE_LOW), w)
                    high_ready(pool, b, t, g)
                    nc.gpsimd.tensor_tensor(p_lo[:, g % RING, own], probs[:, g % RING, own],
                                            p_hi[:, g % RING, own].bitcast(F32), ALU.subtract).then_inc(pool_low, 1)

            batches(pool, lambda b: turns(pool, b, turn))

        @block.vector
        def _(dve):
            def per_token(row):
                return stat[:, row, :].rearrange("p (n a) -> p n a", a=1)

            def normalize(b):
                above(dve, q_made, TILES * b)
                above(dve, k_lo_ready, b)
                parts = [(slice(0, NT - 1), ds(b * (NT - 1), NT - 1)), (slice(NT - 1, NT), ds(NPAIR + b, 1))]
                for own, at in parts:
                    nc.vector.tensor_reduce(stat[:, 0, own], tokens[:, at, :], AX.X, ALU.add).then_inc(sum_ready, 1)
                dve.wait_ge(sum_ready, 2 * b + 2)
                nc.vector.tensor_scalar(stat[:, 1, :], stat[:, 0, :], 1.0 / C, None, ALU.mult).then_inc(mean_ready, 1)
                dve.wait_ge(mean_ready, b + 1)
                for own, at in parts:
                    n = own.stop - own.start
                    nc.vector.tensor_tensor(centred[:, own, :], tokens[:, at, :],
                                            per_token(1)[:, own, :].broadcast_to([P, n, C]),
                                            ALU.subtract).then_inc(centred_ready, 1)
                dve.wait_ge(square_ready, b + 1)
                sq = nodes2[:].rearrange("p n a c -> p (n a c)")[:, 0:NT * C].rearrange("p (n c) -> p n c", n=NT)
                nc.vector.tensor_reduce(stat[:, 0, :], sq, AX.X, ALU.add).then_inc(var_ready, 1)
                dve.wait_ge(var_ready, 2 * b + 1)
                nc.vector.tensor_scalar(stat[:, 2, :], stat[:, 0, :], 1.0 / C, LN_EPS, ALU.mult, ALU.add)\
                    .then_inc(var_ready, 1)
                dve.wait_ge(std_ready, b + 1)
                nc.vector.reciprocal(stat[:, 0, :], stat[:, 3, :]).then_inc(rstd_ready, 1)
                dve.wait_ge(rstd_ready, b + 1)
                nc.vector.tensor_tensor(nodes2, centred.rearrange("p n (a c) -> p n a c", a=1).broadcast_to([P, NT, 2, C]),
                                        stat[:, 0, :].rearrange("p (n a c) -> p n a c", a=1, c=1).broadcast_to([P, NT, 2, C]),
                                        ALU.mult).then_inc(nodes_ready, 1)
                dve.wait_ge(nodes_ready, b + 1)
                nc.vector.tensor_reduce(residue[:, :, 0], nodes2[:, :, 0, :], AX.X, ALU.add).then_inc(residue_ready, 1)
                dve.wait_ge(v_high, b + 1)
                nc.vector.tensor_tensor(values_s[:, :, C:2 * C - 1], nodes2[:, :, 0, 0:C - 1],
                                        values_s[:, :, 0:C - 1].bitcast(F32), ALU.subtract).then_inc(values_ready, 1)

            def split(b):
                dve.wait_ge(keys_copied, TR * (b + 1))
                above(dve, s_ready, NG * TILES * b)
                nc.vector.tensor_copy(k_hi[:], keys_t[:]).then_inc(k_hi_ready, 1)
                dve.wait_ge(k_hi_ready, b + 1)
                nc.vector.tensor_tensor(k_lo[0:C, :], keys_t[0:C, :], k_hi[0:C, :].bitcast(F32),
                                        ALU.subtract).then_inc(k_lo_ready, 1)
                for c in range(TILES):
                    dve.wait_ge(q_rounded, TILES * b + c + 1)
                    q = slice(c * TT, (c + 1) * TT)
                    nc.vector.tensor_tensor(q_both[C:P, q], s_ps[c % 2][C:P, 1, 0:TT], q_both[C:P, q].bitcast(F32),
                                            ALU.subtract).then_inc(q_both_ready, 1)

            def take_own(b, t):
                dve.wait_ge(q_both_ready, TILES * b + TILES)
                above(dve, max_made, NMAX * (TILES * b + t))
                nc.vector.tensor_copy(q_own[:], q_both[:, ds(t * TT, TT)].bitcast(F32)).then_inc(own_ready, 1)

            def high(b, t, g):
                at = NG * (TILES * b + t) + g
                w = GROUPS[g] * TT
                dve.wait_ge(p_ready, at + 1)
                above(dve, pv_done, at + 1 - RING)
                nc.vector.tensor_copy(p_hi[:, g % RING, 0:w], probs[:, g % RING, 0:w]).then_inc(dve_high, 1)

            def low(b, t, g):
                own = slice(0, int(GROUPS[g] * TT * DVE_LOW))
                high_ready(dve, b, t, g)
                nc.vector.tensor_tensor(p_lo[:, g % RING, own], probs[:, g % RING, own],
                                        p_hi[:, g % RING, own].bitcast(F32), ALU.subtract).then_inc(dve_low, 1)

            def read_max(b, t, idx):
                made = (TILES * b + t) * NMAX + idx
                j, c = idx // TILES, idx % TILES
                dve.wait_ge(max_made, made + 1)
                nc.vector.tensor_reduce(cmax[:, j, c:c + 1], max_ps[idx % 2][:, 0:TT], AX.X, ALU.max).then_inc(max_read, 1)

            def negate(b, t):
                dve.wait_ge(max_read, NMAX * (TILES * b + t + 1))
                above(dve, shift_turned, TILES * b + t)
                nc.vector.tensor_reduce(neg_max[:, :, C:C + 1], cmax[:], AX.X, ALU.max, negate=True).then_inc(neg_ready, 1)

            def add_out(b, t, kind):
                dve.wait_ge(out_turned, TILES * b + t + 1)
                turned = turn_ps[:, 0:CH * (C + 1)].rearrange("p (j c) -> p j c", j=CH)
                nc.vector.reciprocal(sum_inv[:], turned[:, :, C:C + 1]).then_inc(inv_ready, 1)
                dve.wait_ge(inv_ready, TILES * b + t + 1)
                for j in range(CH):
                    if kind == "tail" and j == CH - 1:
                        at = ds(NPAIR + b, 1)
                    else:
                        at = ds((NT - 1) * b + CH * t + j, 1)
                    nc.vector.scalar_tensor_tensor(out=tokens[:, at, :].rearrange("p a c -> p (a c)"),
                                                   in0=turned[:, j, 0:C], scalar=sum_inv[:, j, :],
                                                   in1=tokens[:, at, :].rearrange("p a c -> p (a c)"),
                                                   op0=ALU.mult, op1=ALU.add).then_inc(out_added, 1)

            def turn(b, t, kind):
                for g in range(OUT_AT + 1 if kind == "tail" else NG):
                    reads = MAX_PER[g] if kind in ("first", "mid", "late") else 0
                    for k in range(max(reads, 1)):
                        if k < reads:
                            read_max(b, t + 1, MAX_FROM[g] + k)
                        if k == 0 and not (kind == "tail" or (kind == "first" and g == 0)):
                            split_at(b, t, g - 1)
                    if g == 0 and kind == "tail":
                        split_at(b, t, g - 1)
                    if g == OUT_AT and kind != "first":
                        add_out(b, t - 1, kind)
                    if MAX_FROM[g] == NMAX and MAX_FROM[g - 1] < NMAX and kind in ("first", "mid", "late"):
                        negate(b, t + 1)
                        if kind != "late":
                            take_own(b, t + 2)

            def split_at(b, t, g):
                if g < 0:
                    t, g = t - 1, NG - 1
                if g in DVE_HIGH:
                    high(b, t, g)
                low(b, t, g)

            def batch(b):
                normalize(b)
                split(b)
                take_own(b, 0)
                for idx in range(NMAX):
                    read_max(b, 0, idx)
                negate(b, 0)
                take_own(b, 1)
                turns(dve, b, turn)

            nc.vector.memset(k_lo[C:P, :].bitcast(F32), 0.0).then_inc(filled, 1)
            nc.vector.memset(q_hi[C:P, :].bitcast(F32), 0.0)
            nc.vector.memset(neg_max[:], 0.0)
            nc.vector.memset(values_s[:, :, 2 * C - 1:2 * C].bitcast(F32), 1.0)
            dve.wait_ge(filled, 1)
            nc.vector.memset(k_lo[C:C + 1, :].bitcast(F32), 1.0)
            batches(dve, batch)


def attention_layout(w):
    w2x = np.zeros((P, P), np.float32)
    w2x[0:C, 0:C] = w
    w2x[0:C, C:P] = w
    fold = np.zeros((P, C + 1), np.float32)
    for c in range(C - 1):
        for row in (c, C + c):
            fold[row, c] = 1.0
            fold[row, C - 1] = -1.0
    fold[C - 1, C - 1] = 1.0
    fold[P - 1, C] = 1.0
    return w2x, fold


U32 = mybir.dt.uint32
E, F = 16, 128
BT = 4
BW = BT * P
NTILES = NPAIR + B
NBLOCK = NTILES // BT
LO = 32


def experts(nc, gate_w, w1, w2, sel, b2, b1, gate_b, rows, ident, tokens, out):
    with ExitStack() as ctx:
        def sb(name, shape, dt=F32):
            return ctx.enter_context(nc.sbuf_tensor(name, shape, dt))

        def ps(name, shape):
            return ctx.enter_context(nc.psum_tensor(name, shape, F32))

        def sem(name):
            return ctx.enter_context(nc.semaphore(name))

        ident_c = sb("ident_c", [P, P])
        gate_w_s = sb("gate_w_s", [P, P])
        w1_s = sb("w1_s", [P, E, F])
        w1_hi = sb("w1_hi", [P, E, F], F32R)
        w1_lo = sb("w1_lo", [P, E, F], F32R)
        w2_s = sb("w2_s", [P, E, 2, C])
        sel_s = sb("sel_s", [P, E, P])
        sel_r = sb("sel_r", [P, E, P], F32R)
        b2_s = sb("b2_s", [P, P])
        b2_hi = sb("b2_hi", [P, P], F32R)
        b2_lo = sb("b2_lo", [P, P], F32R)
        b1_s = sb("b1_s", [P, E])
        gate_b_s = sb("gate_b_s", [P, 1])
        rows_s = sb("rows_s", [P, 2, C])
        places = sb("places", [P, E])

        stat = sb("c_stat", [P, 4, BT])
        centred = sb("c_centred", [P, BT, C])
        square = sb("c_square", [P, BT, C])
        y = sb("y", [P, BT, 2, C])
        y_kept = sb("y_kept", [P, 2, BT, C])
        y_t = sb("y_t", [P, BW])
        y_both = sb("y_both", [P, 2, BW], F32R)
        logit_cols = sb("logit_cols", [P, BW])
        logits = sb("logits", [P, BT, E])
        top = sb("top", [P, BT, 8])
        top_at = sb("top_at", [P, BT, 8], U32)
        at_f = sb("at_f", [P, BT, 2])
        is_top = sb("is_top", [P, 2, BT, E])
        gap = sb("gap", [P, 4, BT])
        gates = sb("gates", [P, BT, P // LO, LO])
        gates_t = sb("gates_t", [P, 2, BW], F32R)
        hidden = sb("hidden", [P, 2, BW])
        gated = sb("gated", [P, 2, BW])
        moe_cols = sb("moe_cols", [P, BW])
        total = sb("total", [P, BT, C])
        f_stat = sb("f_stat", [P, 4, BT])
        f_centred = sb("f_centred", [P, BT, C])
        f_square = sb("f_square", [P, BT, C])
        f_norm = sb("f_norm", [P, BT, C])
        f_scaled = sb("f_scaled", [P, BT, C])
        f_shift = sb("f_shift", [P, BT, C])
        result = sb("result", [P, 2, BT, C])

        z_ps = [ps(f"z_ps{i}", [P, BW]) for i in range(2)]
        gate_ps = [ps(f"gate_ps{i}", [P, BW]) for i in range(2)]
        moe_ps = ps("moe_ps", [P, BW])
        prep_a = ps("prep_a", [P, BW])
        prep_b = ps("prep_b", [P, BW])
        back_ps = ps("back_ps", [P, BW])

        loaded = sem("c_loaded")
        filled = sem("c_filled")
        rounded = sem("c_rounded")
        weights_ready = sem("weights_ready")
        sum_ready = sem("c_sum_ready")
        mean_ready = sem("c_mean_ready")
        centred_ready = sem("c_centred_ready")
        square_ready = sem("c_square_ready")
        square_sum = sem("c_square_sum")
        var_ready = sem("c_var_ready")
        std_ready = sem("c_std_ready")
        rstd_ready = sem("c_rstd_ready")
        y_ready = sem("y_ready")
        y_kept_ready = sem("y_kept_ready")
        y_turned = sem("y_turned")
        y_copied = sem("y_copied")
        y_rounded = sem("y_rounded")
        y_both_ready = sem("y_both_ready")
        logits_made = sem("logits_made")
        logits_biased = sem("logits_biased")
        logits_turned = sem("logits_turned")
        logits_ready = sem("logits_ready")
        top_ready = sem("top_ready")
        top_at_ready = sem("top_at_ready")
        at_ready = sem("at_ready")
        is_top_ready = sem("is_top_ready")
        gap_ready = sem("gap_ready")
        gap_exp = sem("gap_exp")
        gap_sum = sem("gap_sum")
        first_ready = sem("first_ready")
        second_ready = sem("second_ready")
        weighed = sem("weighed")
        gates_ready = sem("gates_ready")
        gates_turned = sem("gates_turned")
        gates_rounded = sem("gates_rounded")
        gates_t_ready = sem("gates_t_ready")
        gate_spread = sem("gate_spread")
        z_ready = sem("z_ready")
        hidden_ready = sem("hidden_ready")
        gated_ready = sem("gated_ready")
        moe_step = sem("moe_step")
        moe_copied = sem("moe_copied")
        moe_turned = sem("moe_turned")
        total_ready = sem("total_ready")
        f_sum_ready = sem("f_sum_ready")
        f_mean_ready = sem("f_mean_ready")
        f_centred_ready = sem("f_centred_ready")
        f_square_ready = sem("f_square_ready")
        f_square_sum = sem("f_square_sum")
        f_var_ready = sem("f_var_ready")
        f_std_ready = sem("f_std_ready")
        f_rstd_ready = sem("f_rstd_ready")
        f_norm_ready = sem("f_norm_ready")
        f_scaled_ready = sem("f_scaled_ready")
        f_shift_ready = sem("f_shift_ready")
        result_ready = sem("result_ready")
        stored = [sem(f"stored{h}") for h in range(2)]

        consts = [(ident_c[:], ident), (gate_w_s[:], gate_w), (w1_s[:].rearrange("p e f -> p (e f)"), w1),
                  (w2_s[:].rearrange("p e a c -> p (e a c)"), w2), (sel_s[:].rearrange("p e c -> p (e c)"), sel),
                  (b2_s[:], b2), (b1_s[:], b1), (gate_b_s[:], gate_b),
                  (rows_s[:].rearrange("p a c -> p (a c)"), rows[:, 0:2 * C]), (places[:], rows[:, 2 * C:2 * C + E])]
        ALL_CONSTS = 16 * len(consts)

        block = ctx.enter_context(nc.Block())

        def run_blocks(eng, step):
            step(0, 0, "first")
            with eng.Fori(0, (NBLOCK - 3) // 2) as i:
                step(2 * i + 1, 1, "mid")
                step(2 * i + 2, 0, "mid")
            step(NBLOCK - 2, 1, "mid")
            step(NBLOCK - 1, 0, "last")
            step(NBLOCK, 1, "tail")

        @block.sync
        def _(sp):
            for dst, src in consts:
                sp.dma_start(dst, src).then_inc(loaded, 16)

            def store(n, half):
                sp.wait_ge(result_ready, n + 1)
                sp.dma_start(out[ds(BT * n, BT)].rearrange("n p c -> p n c"), result[:, half]).then_inc(stored[half], 16)

            with sp.Fori(0, NBLOCK // 2) as i:
                store(2 * i, 0)
                store(2 * i + 1, 1)
            store(NBLOCK - 1, 0)
            sp.wait_ge(stored[0], 16 * (NBLOCK // 2 + 1))
            sp.wait_ge(stored[1], 16 * (NBLOCK // 2))

        @block.tensor
        def _(pe):
            def turn_y(n, half):
                pe.wait_ge(y_ready, n + 1)
                wait_above_zero(pe, top_ready, BT * n)
                for j in range(BT):
                    last = nc.tensor.transpose(prep_a[:, j * P:(j + 1) * P], y[:, j].rearrange("p a c -> p (a c)"),
                                               ident_c[:])
                last.then_inc(y_turned, 1)

            def make_logits(n):
                pe.wait_ge(y_copied, n + 1)
                wait_above_zero(pe, gates_t_ready, n)
                nc.tensor.matmul(prep_b[:], gate_w_s[:], y_t[:], start=True, stop=True).then_inc(logits_made, 1)

            def turn_logits(n):
                pe.wait_ge(logits_biased, n + 1)
                pe.wait_ge(y_both_ready, n + 1)
                for j in range(BT):
                    last = nc.tensor.transpose(prep_a[:, j * P:(j + 1) * P], logit_cols[:, j * P:(j + 1) * P],
                                               ident_c[:])
                last.then_inc(logits_turned, 1)

            def turn_gates(n):
                pe.wait_ge(gates_ready, n + 1)
                for j in range(BT):
                    last = nc.tensor.transpose(prep_b[:, j * P:(j + 1) * P],
                                               gates[:, j].rearrange("p a c -> p (a c)"), ident_c[:])
                last.then_inc(gates_turned, 1)

            def spread(n, half, e):
                wait_above_zero(pe, gated_ready, E * n + e - 1)
                nc.tensor.matmul(gate_ps[e % 2][:], sel_r[:, e, :], gates_t[:, half, :],
                                 start=True, stop=True).then_inc(gate_spread, 1)

            def first_layer(n, half, e):
                wait_above_zero(pe, hidden_ready, E * n + e - 1)
                nc.tensor.matmul(z_ps[e % 2][:], w1_hi[:, e, :], y_both[:, half, :], start=True, stop=False)
                nc.tensor.matmul(z_ps[e % 2][:], w1_lo[:, e, :], y_both[:, half, :],
                                 start=False, stop=True).then_inc(z_ready, 1)

            def second_layer(n, e):
                pe.wait_ge(gated_ready, E * n + e + 1)
                nc.tensor.matmul(moe_ps[:], w2_s[:, e].rearrange("p a c -> p (a c)"), gated[:, e % 2, :], start=False,
                                 stop=(e == E - 1)).then_inc(moe_step, 1)

            def second_bias(n, half):
                wait_above_zero(pe, moe_copied, n)
                nc.tensor.matmul(moe_ps[:], b2_hi[:], gates_t[:, half, :], start=True, stop=False)
                nc.tensor.matmul(moe_ps[:], b2_lo[:], gates_t[:, half, :], start=False, stop=False)

            def turn_back(n):
                pe.wait_ge(moe_copied, n + 1)
                wait_above_zero(pe, total_ready, n)
                for j in range(BT):
                    last = nc.tensor.transpose(back_ps[:, j * P:(j + 1) * P], moe_cols[:, j * P:(j + 1) * P],
                                               ident_c[:])
                last.then_inc(moe_turned, 1)

            def prepare(n, half, e):
                if e == 2:
                    turn_y(n, half)
                if e == 4:
                    make_logits(n)
                if e == 6:
                    turn_logits(n)
                if e == 12:
                    turn_gates(n)

            def step(n, half, kind):
                if kind != "tail":
                    pe.wait_ge(y_both_ready, n + 1)
                    pe.wait_ge(gates_t_ready, n + 1)
                for e in range(E):
                    if kind != "tail":
                        spread(n, half, e)
                        first_layer(n, half, e)
                    if e == 2 and kind != "tail":
                        second_bias(n, half)
                    if e >= 2 and kind != "tail":
                        second_layer(n, e - 2)
                    if e < 2 and kind != "first":
                        second_layer(n - 1, E - 2 + e)
                    if e == 3 and kind != "first":
                        turn_back(n - 1)
                    if kind in ("first", "mid"):
                        prepare(n + 1, 1 - half, e)

            pe.wait_ge(loaded, ALL_CONSTS)
            pe.wait_ge(weights_ready, 3)
            for e in range(E):
                prepare(0, 0, e)
            run_blocks(pe, step)

        @block.scalar
        def _(act):
            def squares(n):
                act.wait_ge(centred_ready, n + 1)
                wait_above_zero(act, square_sum, n)
                nc.scalar.activation(square[:], centred[:], ACT.Square).then_inc(square_ready, 1)

            def deviation(n):
                act.wait_ge(var_ready, n + 1)
                wait_above_zero(act, rstd_ready, n)
                nc.scalar.activation(stat[:, 3, :], stat[:, 2, :], ACT.Sqrt).then_inc(std_ready, 1)

            def copy_y(n, half):
                act.wait_ge(y_turned, n + 1)
                wait_above_zero(act, logits_made, n)
                nc.scalar.copy(y_t[:], prep_a[:]).then_inc(y_copied, 1)
                wait_above_zero(act, z_ready, E * (n - 1))
                nc.scalar.copy(y_both[:, half, :], prep_a[:]).then_inc(y_rounded, 1)

            def add_gate_bias(n):
                act.wait_ge(logits_made, n + 1)
                wait_above_zero(act, logits_turned, n)
                nc.scalar.activation(logit_cols[:], prep_b[:], ACT.Identity, bias=gate_b_s[:])\
                    .then_inc(logits_biased, 1)

            def gap_exponent(n):
                act.wait_ge(gap_ready, n + 1)
                wait_above_zero(act, second_ready, n)
                nc.scalar.activation(gap[:, 1, :], gap[:, 0, :], ACT.Exp).then_inc(gap_exp, 1)

            def round_gates(n, half):
                act.wait_ge(gates_turned, n + 1)
                wait_above_zero(act, gate_spread, E * (n - 1))
                nc.scalar.copy(gates_t[0:2 * LO, half, :], prep_b[0:2 * LO, :]).then_inc(gates_rounded, 1)

            def relu(n, e):
                act.wait_ge(z_ready, E * n + e + 1)
                wait_above_zero(act, gated_ready, E * n + e - 1)
                nc.scalar.activation(hidden[:, e % 2, :], z_ps[e % 2][:], ACT.Relu, bias=b1_s[:, e:e + 1])\
                    .then_inc(hidden_ready, 1)

            def copy_moe(n):
                act.wait_ge(moe_step, E * (n + 1))
                wait_above_zero(act, moe_turned, n)
                nc.scalar.copy(moe_cols[:], moe_ps[:]).then_inc(moe_copied, 1)

            def f_squares(n):
                act.wait_ge(f_centred_ready, n + 1)
                wait_above_zero(act, f_square_sum, n)
                nc.scalar.activation(f_square[:], f_centred[:], ACT.Square).then_inc(f_square_ready, 1)

            def f_deviation(n):
                act.wait_ge(f_var_ready, n + 1)
                wait_above_zero(act, f_rstd_ready, n)
                nc.scalar.activation(f_stat[:, 3, :], f_stat[:, 2, :], ACT.Sqrt).then_inc(f_std_ready, 1)

            def prepare(n, half, e):
                if e == 0:
                    squares(n)
                if e == 1:
                    deviation(n)
                if e == 3:
                    copy_y(n, half)
                if e == 5:
                    add_gate_bias(n)
                if e == 10:
                    gap_exponent(n)
                if e == 13:
                    round_gates(n, half)

            def step(n, half, kind):
                for e in range(E):
                    if kind != "tail":
                        relu(n, e)
                    if kind in ("first", "mid"):
                        prepare(n + 1, 1 - half, e)
                    if kind != "first":
                        if e == 1:
                            copy_moe(n - 1)
                        if e == 5:
                            f_squares(n - 1)
                        if e == 7:
                            f_deviation(n - 1)

            act.wait_ge(loaded, ALL_CONSTS)
            for e in range(E):
                prepare(0, 0, e)
            run_blocks(act, step)

        @block.vector
        def _(dve):
            def spread_rows(ap):
                return ap.rearrange("p (n a) -> p n a", a=1)

            def centre(n):
                at = ds(BT * n, BT)
                nc.vector.tensor_reduce(stat[:, 0, :], tokens[:, at, :], AX.X, ALU.add).then_inc(sum_ready, 1)
                dve.wait_ge(sum_ready, n + 1)
                nc.vector.tensor_scalar(stat[:, 1, :], stat[:, 0, :], 1.0 / C, None, ALU.mult).then_inc(mean_ready, 1)
                dve.wait_ge(mean_ready, n + 1)
                nc.vector.tensor_tensor(centred[:], tokens[:, at, :],
                                        spread_rows(stat[:, 1, :]).broadcast_to([P, BT, C]),
                                        ALU.subtract).then_inc(centred_ready, 1)

            def variance(n):
                dve.wait_ge(square_ready, n + 1)
                nc.vector.tensor_reduce(stat[:, 0, :], square[:], AX.X, ALU.add).then_inc(square_sum, 1)
                dve.wait_ge(square_sum, n + 1)
                nc.vector.tensor_scalar(stat[:, 2, :], stat[:, 0, :], 1.0 / C, LN_EPS, ALU.mult, ALU.add)\
                    .then_inc(var_ready, 1)

            def normalize(n, half):
                dve.wait_ge(std_ready, n + 1)
                nc.vector.reciprocal(stat[:, 1, :], stat[:, 3, :]).then_inc(rstd_ready, 1)
                dve.wait_ge(rstd_ready, n + 1)
                wait_above_zero(dve, y_turned, n)
                wait_above_zero(dve, y_kept_ready, n)
                nc.vector.tensor_tensor(
                    y[:], centred[:].rearrange("p n (a c) -> p n a c", a=1).broadcast_to([P, BT, 2, C]),
                    stat[:, 1, :].rearrange("p (n a c) -> p n a c", a=1, c=1).broadcast_to([P, BT, 2, C]),
                    ALU.mult).then_inc(y_ready, 1)

            def keep_y(n, half):
                dve.wait_ge(y_ready, n + 1)
                nc.vector.tensor_copy(y_kept[:, half], y[:, :, 0, :]).then_inc(y_kept_ready, 1)

            def low_y(n, half):
                dve.wait_ge(y_rounded, n + 1)
                nc.vector.tensor_tensor(y_both[C:P, half, :], prep_a[C:P, :], y_both[C:P, half, :].bitcast(F32),
                                        ALU.subtract).then_inc(y_both_ready, 1)

            def choose(n):
                dve.wait_ge(logits_turned, n + 1)
                in_bank = prep_a[:].rearrange("p (n e) -> p n e", n=BT)[:, :, 0:E]
                nc.vector.tensor_copy(logits[:], in_bank).then_inc(logits_ready, 1)
                for j in range(BT):
                    nc.vector.max(top[:, j, :], in_bank[:, j, :]).then_inc(top_ready, 1)
                dve.wait_ge(logits_ready, n + 1)
                dve.wait_ge(top_ready, BT * (n + 1))
                nc.vector.tensor_tensor(spread_rows(gap[:, 0, :]), top[:, :, 1:2], top[:, :, 0:1],
                                        ALU.subtract).then_inc(gap_ready, 1)
                for j in range(BT):
                    nc.vector.max_index(top_at[:, j, :], top[:, j, :], logits[:, j, :]).then_inc(top_at_ready, 1)

            def mark(n):
                dve.wait_ge(top_at_ready, BT * (n + 1))
                nc.vector.tensor_copy(at_f[:], top_at[:, :, 0:2]).then_inc(at_ready, 1)
                dve.wait_ge(at_ready, n + 1)
                for r in range(2):
                    nc.vector.tensor_tensor(is_top[:, r], places[:].rearrange("p (a e) -> p a e", a=1).broadcast_to([P, BT, E]),
                                            at_f[:, :, r:r + 1].broadcast_to([P, BT, E]), ALU.is_equal)\
                        .then_inc(is_top_ready, 1)

            def weigh(n):
                dve.wait_ge(gap_exp, n + 1)
                nc.vector.tensor_scalar(gap[:, 2, :], gap[:, 1, :], 1.0, None, ALU.add).then_inc(gap_sum, 1)
                dve.wait_ge(gap_sum, n + 1)
                nc.vector.reciprocal(gap[:, 3, :], gap[:, 2, :]).then_inc(first_ready, 1)
                dve.wait_ge(first_ready, n + 1)
                nc.vector.tensor_tensor(gap[:, 2, :], gap[:, 1, :], gap[:, 3, :], ALU.mult).then_inc(second_ready, 1)
                dve.wait_ge(second_ready, n + 1)
                dve.wait_ge(is_top_ready, 2 * (n + 1))
                for r in range(2):
                    nc.vector.tensor_tensor(is_top[:, r], is_top[:, r],
                                            spread_rows(gap[:, 3 - r, :]).broadcast_to([P, BT, E]), ALU.mult)\
                        .then_inc(weighed, 1)
                dve.wait_ge(weighed, 2 * (n + 1))
                nc.vector.tensor_tensor(gates[:, :, 0:2, 0:E],
                                        is_top[:, 0].rearrange("p n (a e) -> p n a e", a=1).broadcast_to([P, BT, 2, E]),
                                        is_top[:, 1].rearrange("p n (a e) -> p n a e", a=1).broadcast_to([P, BT, 2, E]),
                                        ALU.add).then_inc(gates_ready, 1)

            def low_gates(n, half):
                dve.wait_ge(gates_rounded, n + 1)
                nc.vector.tensor_tensor(gates_t[LO:2 * LO, half, :], prep_b[LO:2 * LO, :],
                                        gates_t[LO:2 * LO, half, :].bitcast(F32), ALU.subtract).then_inc(gates_t_ready, 1)

            def gate(n, e):
                dve.wait_ge(hidden_ready, E * n + e + 1)
                dve.wait_ge(gate_spread, E * n + e + 1)
                wait_above_zero(dve, moe_step, E * n + e - 1)
                nc.vector.tensor_tensor(gated[:, e % 2, :], gate_ps[e % 2][:], hidden[:, e % 2, :],
                                        ALU.mult).then_inc(gated_ready, 1)

            def f_centre(n, half):
                dve.wait_ge(moe_turned, n + 1)
                nc.vector.tensor_tensor(total[:], back_ps[:].rearrange("p (n c) -> p n c", n=BT)[:, :, 0:C],
                                        y_kept[:, half], ALU.add).then_inc(total_ready, 1)
                dve.wait_ge(total_ready, n + 1)
                nc.vector.tensor_reduce(f_stat[:, 0, :], total[:], AX.X, ALU.add).then_inc(f_sum_ready, 1)
                dve.wait_ge(f_sum_ready, n + 1)
                nc.vector.tensor_scalar(f_stat[:, 1, :], f_stat[:, 0, :], 1.0 / C, None, ALU.mult).then_inc(f_mean_ready, 1)
                dve.wait_ge(f_mean_ready, n + 1)
                nc.vector.tensor_tensor(f_centred[:], total[:], spread_rows(f_stat[:, 1, :]).broadcast_to([P, BT, C]),
                                        ALU.subtract).then_inc(f_centred_ready, 1)

            def f_variance(n):
                dve.wait_ge(f_square_ready, n + 1)
                nc.vector.tensor_reduce(f_stat[:, 0, :], f_square[:], AX.X, ALU.add).then_inc(f_square_sum, 1)
                dve.wait_ge(f_square_sum, n + 1)
                nc.vector.tensor_scalar(f_stat[:, 2, :], f_stat[:, 0, :], 1.0 / C, LN_EPS, ALU.mult, ALU.add)\
                    .then_inc(f_var_ready, 1)

            def f_normalize(n):
                dve.wait_ge(f_std_ready, n + 1)
                nc.vector.reciprocal(f_stat[:, 1, :], f_stat[:, 3, :]).then_inc(f_rstd_ready, 1)
                dve.wait_ge(f_rstd_ready, n + 1)
                wait_above_zero(dve, f_scaled_ready, n)
                nc.vector.tensor_tensor(f_norm[:], f_centred[:], spread_rows(f_stat[:, 1, :]).broadcast_to([P, BT, C]),
                                        ALU.mult).then_inc(f_norm_ready, 1)

            def prepare(n, half, e):
                if e == 0:
                    centre(n)
                if e == 1:
                    variance(n)
                if e == 2:
                    normalize(n, half)
                if e == 4:
                    low_y(n, half)
                if e == 5:
                    keep_y(n, half)
                if e == 7:
                    choose(n)
                if e == 9:
                    mark(n)
                if e == 11:
                    weigh(n)
                if e == 14:
                    low_gates(n, half)

            def step(n, half, kind):
                for e in range(E):
                    if kind != "tail":
                        gate(n, e)
                    if kind in ("first", "mid"):
                        prepare(n + 1, 1 - half, e)
                    if kind != "first":
                        if e == 4:
                            f_centre(n - 1, 1 - half)
                        if e == 6:
                            f_variance(n - 1)
                        if e == 8:
                            f_normalize(n - 1)

            nc.vector.memset(gates[:], 0.0).then_inc(filled, 1)
            nc.vector.memset(gates_t[:].bitcast(F32), 0.0).then_inc(filled, 1)
            dve.wait_ge(loaded, ALL_CONSTS)
            dve.wait_ge(filled, 2)
            nc.vector.tensor_copy(w1_hi[:], w1_s[:]).then_inc(rounded, 1)
            nc.vector.tensor_copy(b2_hi[:], b2_s[:]).then_inc(rounded, 1)
            nc.vector.tensor_copy(sel_r[:], sel_s[:]).then_inc(weights_ready, 1)
            dve.wait_ge(rounded, 2)
            nc.vector.tensor_tensor(w1_lo[:], w1_s[:], w1_hi[:].bitcast(F32), ALU.subtract).then_inc(weights_ready, 1)
            nc.vector.tensor_tensor(b2_lo[:], b2_s[:], b2_hi[:].bitcast(F32), ALU.subtract).then_inc(weights_ready, 1)
            for e in range(E):
                prepare(0, 0, e)
            run_blocks(dve, step)

        @block.gpsimd
        def _(pool):
            def finish(n, half, nth):
                pool.wait_ge(f_norm_ready, n + 1)
                wait_above_zero(pool, result_ready, n)
                gamma = rows_s[:, 0:1, :].broadcast_to([P, BT, C])
                beta = rows_s[:, 1:2, :].broadcast_to([P, BT, C])
                nc.gpsimd.tensor_tensor(f_scaled[:], f_norm[:], gamma, ALU.mult).then_inc(f_scaled_ready, 1)
                nc.gpsimd.tensor_tensor(f_shift[:], tokens[:, ds(BT * n, BT), :], beta, ALU.add).then_inc(f_shift_ready, 1)
                pool.wait_ge(f_scaled_ready, n + 1)
                pool.wait_ge(f_shift_ready, n + 1)
                wait_above_zero(pool, stored[half], 16 * nth)
                nc.gpsimd.tensor_tensor(result[:, half], f_scaled[:], f_shift[:], ALU.add).then_inc(result_ready, 1)

            pool.wait_ge(loaded, ALL_CONSTS)
            with pool.Fori(0, NBLOCK // 2) as i:
                finish(2 * i, 0, i)
                finish(2 * i + 1, 1, i)
            finish(NBLOCK - 1, 0, NBLOCK // 2)


def expert_layout(gate_w, gate_b, w1, b1, w2, b2, gamma, beta):
    f = np.float32
    gw = np.zeros((P, P), f)
    gw[0:C, 0:E] = gate_w
    gb = np.zeros((P, 1), f)
    gb[0:E, 0] = gate_b
    w1t = w1.transpose(1, 0, 2).reshape(C, E * F)
    sel = np.zeros((P, E, P), f)
    b2x = np.zeros((P, C), f)
    for e in range(E):
        sel[e, e] = sel[LO + e, e] = 1.0
    b2x[0:E] = b2
    b2x[LO:LO + E] = b2
    rows = np.concatenate([gamma, beta, np.arange(E, dtype=f)])
    return dict(gate_w=gw, w1=np.concatenate([w1t, w1t]), w2=np.tile(w2.transpose(1, 0, 2)[:, :, None], (1, 1, 2, 1)).reshape(F, 2 * E * C),
                sel=sel.reshape(P, E * P), b2=np.tile(b2x, (1, 2)), b1=np.ascontiguousarray(b1.T), gate_b=gb,
                rows=np.tile(rows, (P, 1)))


def fused_layer(nc, xw, txt, wqk, wv, wp, cols, trig, hmask, vmask, omask, ident, w2x, fold,
                gate_w, w1, w2, sel, b2, b1, gate_b, rows, out):
    with nc.sbuf_tensor("tokens", [P, NPAIR + B, C], F32) as tokens:
        window_attention(nc, xw, txt, wqk, wv, wp, cols, trig, hmask, vmask, omask, ident, tokens)
        full_attention(nc, w2x, ident, fold, tokens)
        experts(nc, gate_w, w1, w2, sel, b2, b1, gate_b, rows, ident, tokens, out)


def kernel(x, txt, L0_tok_qkv_w, L0_tok_qkv_b, L0_tok_proj_w, L0_tok_proj_b, L0_attn_W, L0_ffn_gate_w,
           L0_ffn_gate_b, L0_ffn_w1, L0_ffn_b1, L0_ffn_w2, L0_ffn_b2, L0_ffn_gamma, L0_ffn_beta):
    import concourse.bacc as bacc
    from concourse.bass_utils import run_bass_kernel_spmd

    a = [np.asarray(v) for v in (x, L0_tok_qkv_w, L0_tok_qkv_b, L0_tok_proj_w, L0_tok_proj_b)]
    laid = window_layout(*a)
    laid["txt"] = np.asarray(txt)
    laid["w2x"], laid["fold"] = attention_layout(np.asarray(L0_attn_W))
    laid.update(expert_layout(*[np.asarray(v) for v in (
        L0_ffn_gate_w, L0_ffn_gate_b, L0_ffn_w1, L0_ffn_b1, L0_ffn_w2, L0_ffn_b2, L0_ffn_gamma, L0_ffn_beta)]))
    order = ["xw", "txt", "wqk", "wv", "wp", "cols", "trig", "hmask", "vmask", "omask", "ident", "w2x", "fold",
             "gate_w", "w1", "w2", "sel", "b2", "b1", "gate_b", "rows"]

    nc = bacc.Bacc("TRN2", target_bir_lowering=False, num_devices=1)
    arrays, args = {}, []
    for name in order:
        v = np.ascontiguousarray(laid[name])
        arrays[f"in_{name}_dram"] = v
        args.append(nc.dram_tensor(f"in_{name}_dram", v.shape, mybir.dt.from_np(v.dtype), kind="ExternalInput").ap())
    args.append(nc.dram_tensor("out_0_dram", (NPAIR + B, P, C), F32, kind="ExternalOutput").ap())
    fused_layer(nc, *args)
    got = run_bass_kernel_spmd(nc, [arrays], core_ids=[0]).results[0]["out_0_dram"]

    nw = SIDE // WIN
    img = got[:NPAIR].reshape(B, nw, nw // 2, 2, WIN, WIN, C).transpose(0, 1, 4, 2, 3, 5, 6)
    return np.concatenate([img.reshape(B, SIDE * SIDE, C), got[NPAIR:]], axis=1)
```

```python
from contextlib import ExitStack

import numpy as np
import concourse.bass as bass
from concourse import mybir

F32 = mybir.dt.float32
F32R = mybir.dt.float32r
ALU = mybir.AluOpType
ACT = mybir.ActivationFunctionType
AX = mybir.AxisListType
ds = bass.ds

P = 128
B, SIDE, C = 4, 64, 64
WIN = 8
NH, HD = 8, 8
WTOK = WIN * WIN
NPAIR = B * (SIDE // WIN) ** 2 // 2
QUAD = 4
NQUAD = NPAIR // QUAD
PER = 2 * QUAD
TXT = 128
HEAD_SCALE = HD ** -0.5


def wait_above_zero(eng, sem, count):
    if not isinstance(count, int) or count > 0:
        eng.wait_ge(sem, count)


def run_turns(eng, turn):
    turns = NPAIR // PER
    turn(0, "first")
    with eng.Fori(1, turns - 1) as i:
        turn(i, "mid")
    turn(turns - 1, "last")
    turn(turns, "tail")


def runs(kind, k, lag):
    return k >= lag if kind == "first" else k < lag if kind == "tail" else True


def window_attention(nc, xw, txt, wqk, wv, wp, cols, trig, hmask, vmask, omask, ident, tokens):
    with ExitStack() as ctx:
        def sb(name, shape, dt=F32):
            return ctx.enter_context(nc.sbuf_tensor(name, shape, dt))

        def ps(name, shape):
            return ctx.enter_context(nc.psum_tensor(name, shape, F32))

        def sem(name):
            return ctx.enter_context(nc.semaphore(name))

        wqk_s = sb("wqk_s", [P, 4, P])
        wv_s = sb("wv_s", [P, P])
        wp_s = sb("wp_s", [P, P])
        cols_s = sb("cols_s", [P, 8])
        trig_s = sb("trig_s", [P, 2, WTOK])
        hmask_s = sb("hmask_s", [P, NH])
        vmask_s = sb("vmask_s", [P, P])
        omask_s = sb("omask_s", [P, P])
        ident_s = sb("ident_s", [P, P])
        x_s = sb("x_s", [P, 2, QUAD, 2, WTOK])
        turned = sb("turned", [P, 4, QUAD * WTOK])
        k_rot = sb("k_rot", [P, 2, QUAD, WTOK])
        q_diag = sb("q_diag", [P, 2, QUAD, P])
        k_heads = sb("k_heads", [P, 2, QUAD, NH, WTOK])
        v_heads = sb("v_heads", [P, 2, QUAD, P])
        s_max = sb("s_max", [P, 2, NH])
        s_low = sb("s_low", [P, 2, NH, WTOK])
        probs = sb("probs", [P, 2, NH, WTOK])
        p_sum = sb("p_sum", [P, 2, NH])
        p_inv = sb("p_inv", [P, 2, NH])
        p_norm = sb("p_norm", [P, 2, NH, WTOK])
        p_turn = sb("p_turn", [P, 2, 4, P])
        o_own = sb("o_own", [P, QUAD, P])
        h_cols = sb("h_cols", [P, QUAD, P])

        proj_a = ps("proj_a", [P, 2, QUAD * WTOK])
        proj_b = ps("proj_b", [P, 2, QUAD * WTOK])
        scores = [ps(f"scores{i}", [P, NH, WTOK]) for i in range(2)]
        p_t = [ps(f"p_t{i}", [P, 4, P]) for i in range(2)]
        o_t = ps("o_t", [P, QUAD, P])
        h_t = ps("h_t", [P, QUAD, P])
        v_ps = proj_a[:].rearrange("p a b -> p (a b)").rearrange("p (q c) -> p q c", q=QUAD)
        rows_ps = proj_b[:].rearrange("p a b -> p (a b)").rearrange("p (q c) -> p q c", q=QUAD)

        consts_loaded = sem("consts_loaded")
        x_loaded = [sem(f"x_loaded{half}") for half in range(2)]
        text_loaded = sem("text_loaded")
        diag_zero = sem("diag_zero")
        qk_projected = sem("qk_projected")
        v_projected = sem("v_projected")
        turned_ready = sem("turned_ready")
        rotated = sem("rotated")
        k_ready = sem("k_ready")
        v_ready = sem("v_ready")
        scores_ready = sem("scores_ready")
        max_ready = sem("max_ready")
        low_ready = sem("low_ready")
        probs_ready = sem("probs_ready")
        sum_ready = sem("sum_ready")
        inv_ready = sem("inv_ready")
        norm_ready = sem("norm_ready")
        pt_ready = sem("pt_ready")
        pt_copied = sem("pt_copied")
        pv_ready = sem("pv_ready")
        o_ready = sem("o_ready")
        h_ready = sem("h_ready")
        h_copied = sem("h_copied")
        rows_ready = sem("rows_ready")
        rows_copied = sem("rows_copied")

        consts = [(wqk_s[:].rearrange("p a b -> p (a b)"), wqk), (wv_s[:], wv), (wp_s[:], wp), (cols_s[:], cols),
                  (trig_s[:].rearrange("p a b -> p (a b)"), trig), (hmask_s[:], hmask), (vmask_s[:], vmask),
                  (omask_s[:], omask), (ident_s[:], ident)]
        ALL_CONSTS = 16 * len(consts)

        block = ctx.enter_context(nc.Block())

        @block.sync
        def _(sp):
            def load_x(u, half):
                for copy in range(2):
                    sp.dma_start(x_s[:, half, :, copy, :],
                                 xw[ds(u, 1)].rearrange("a p (q t) -> (a p) q t", q=QUAD)).then_inc(x_loaded[half], 16)

            load_x(0, 0)
            for dst, src in consts:
                sp.dma_start(dst, src).then_inc(consts_loaded, 16)
            load_x(1, 1)
            sp.dma_start(tokens[:, NPAIR:NPAIR + B, :], txt.rearrange("b p c -> p b c")).then_inc(text_loaded, 16)

            def refill(i):
                sp.wait_ge(v_projected, 2 * i + 1)
                load_x(2 * i + 2, 0)
                sp.wait_ge(v_projected, 2 * i + 2)
                load_x(2 * i + 3, 1)

            with sp.Fori(0, NQUAD // 2 - 1) as i:
                refill(i)
            sp.wait_ge(text_loaded, 16)

        @block.tensor
        def _(pe):
            def project_qk(u, half, nth):
                pe.wait_ge(x_loaded[half], 32 * nth + 32)
                wait_above_zero(pe, v_ready, u)
                wait_above_zero(pe, rows_copied, u - 3)
                for m in range(4):
                    bank = proj_a if m < 2 else proj_b
                    last = nc.tensor.matmul(bank[:, m % 2, :], wqk_s[:, m, :],
                                            x_s[:, half, :, 0, :], start=True, stop=True)
                last.then_inc(qk_projected, 1)

            def project_v(u, half):
                pe.wait_ge(turned_ready, 4 * u + 4)
                for p in range(QUAD):
                    last = nc.tensor.matmul(v_ps[:, p, :], x_s[:, half, p].rearrange("p a t -> p (a t)"), wv_s[:],
                                            start=True, stop=True)
                last.then_inc(v_projected, 1)

            def score(n, k):
                pe.wait_ge(k_ready, n + 1)
                pe.wait_ge(rotated, 3 * ((n - k) // QUAD + k // QUAD) + 3)
                wait_above_zero(pe, low_ready, n - 1)
                half, p = k // QUAD, k % QUAD
                nc.tensor.matmul(scores[k % 2][:].rearrange("p h t -> p (h t)"), q_diag[:, half, p, :],
                                 k_heads[:, half, p].rearrange("p h t -> p (h t)"),
                                 start=True, stop=True).then_inc(scores_ready, 1)

            def turn_probs(n, k):
                pe.wait_ge(norm_ready, n + 1)
                wait_above_zero(pe, pt_copied, n - 1)
                for j in range(4):
                    last = nc.tensor.transpose(p_t[k % 2][:, j, :],
                                               p_norm[:, k % 2, 2 * j:2 * j + 2, :].rearrange("p h t -> p (h t)"),
                                               ident_s[:])
                last.then_inc(pt_ready, 1)

            def values(n, k, u):
                pe.wait_ge(pt_copied, n + 1)
                half, p = k // QUAD, k % QUAD
                if p == 0:
                    pe.wait_ge(v_ready, u + 1)
                    wait_above_zero(pe, o_ready, u)
                for j in range(4):
                    last = nc.tensor.matmul(o_t[32 * j:32 * j + 32, p, :], v_heads[:, half, p, 32 * j:32 * j + 32],
                                            p_turn[:, k % 2, j, :], start=True, stop=True)
                last.then_inc(pv_ready, 1)

            def project_out(u):
                pe.wait_ge(o_ready, u + 1)
                wait_above_zero(pe, h_copied, u)
                nc.tensor.matmul(h_t[:].rearrange("p q t -> p (q t)"), wp_s[:],
                                 o_own[:].rearrange("p q t -> p (q t)"), start=True, stop=True).then_inc(h_ready, 1)

            def to_rows(u, k, kind):
                pe.wait_ge(h_copied, u + 1)
                if kind in ("first", "mid") or kind == "last" and k == 1:
                    pe.wait_ge(turned_ready, 4 * (u + 3) + 4)
                wait_above_zero(pe, rows_copied, u)
                for p in range(QUAD):
                    last = nc.tensor.transpose(rows_ps[:, p, :], h_cols[:, p, :], ident_s[:])
                last.then_inc(rows_ready, 1)

            def turn(i, kind):
                for k in range(PER):
                    n = i * PER + k
                    if k == 0 and kind != "tail":
                        project_qk(2 * i + 1, 1, i)
                    if k == QUAD and kind in ("first", "mid"):
                        project_qk(2 * i + 2, 0, i + 1)
                    if kind != "tail":
                        score(n, k)
                    if runs(kind, k, 2):
                        turn_probs(n - 2, (k - 2) % PER)
                    if runs(kind, k, 3):
                        values(n - 3, (k - 3) % PER, 2 * i + (k - 3) // QUAD)
                    if k == 3 and kind != "tail":
                        project_v(2 * i + 1, 1)
                    if k == 7 and kind in ("first", "mid"):
                        project_v(2 * i + 2, 0)
                    if kind != "first" and k in (0, 4):
                        project_out(2 * i - 2 + k // 4)
                    if kind != "first" and k in (1, 5):
                        to_rows(2 * i - 2 + k // 4, k, kind)

            pe.wait_ge(consts_loaded, ALL_CONSTS)
            project_qk(0, 0, 0)
            project_v(0, 0)
            run_turns(pe, turn)

        @block.vector
        def _(dve):
            def rotate(u, half):
                dve.wait_ge(qk_projected, u + 1)
                wait_above_zero(dve, rotated, 3 * u)
                for m in range(4):
                    bank = proj_a if m < 2 else proj_b
                    nc.vector.scalar_tensor_tensor(
                        out=turned[:, m, :].rearrange("p (q t) -> p q t", q=QUAD),
                        in0=bank[:, m % 2, :].rearrange("p (q t) -> p q t", q=QUAD),
                        scalar=cols_s[:, m:m + 1],
                        in1=trig_s[:, m % 2:m % 2 + 1, :].broadcast_to([P, QUAD, WTOK]),
                        op0=ALU.add, op1=ALU.mult).then_inc(turned_ready, 1)
                dve.wait_ge(turned_ready, 4 * u + 4)
                wait_above_zero(dve, scores_ready, QUAD * (u - 1))
                wait_above_zero(dve, k_ready, QUAD * (u - 1))
                q1 = turned[:, 0, :].rearrange("p (q t) -> p q t", q=QUAD)
                q2 = turned[:, 1, :].rearrange("p (q t) -> p q t", q=QUAD)
                for w in range(2):
                    r = slice(64 * w, 64 * w + 64)
                    nc.vector.tensor_tensor(q_diag[r, half, :, r], q1[r], q2[r], ALU.add).then_inc(rotated, 1)
                nc.vector.tensor_tensor(k_rot[:, half].rearrange("p q t -> p (q t)"), turned[:, 2, :],
                                        turned[:, 3, :], ALU.add).then_inc(rotated, 1)

            def mask_v(u, half):
                dve.wait_ge(v_projected, u + 1)
                wait_above_zero(dve, pv_ready, QUAD * (u - 1))
                nc.vector.tensor_tensor(v_heads[:, half], v_ps,
                                        vmask_s[:].rearrange("p (a c) -> p a c", a=1).broadcast_to([P, QUAD, P]),
                                        ALU.mult).then_inc(v_ready, 1)

            def lower(n, k):
                dve.wait_ge(scores_ready, n + 1)
                wait_above_zero(dve, low_ready, n - 1)
                nc.vector.tensor_reduce(s_max[:, k % 2, :], scores[k % 2][:], AX.X, ALU.max).then_inc(max_ready, 1)
                dve.wait_ge(max_ready, n + 1)
                wait_above_zero(dve, probs_ready, n - 1)
                nc.vector.tensor_tensor(s_low[:, k % 2], scores[k % 2][:],
                                        s_max[:, k % 2, :].rearrange("p (h a) -> p h a", a=1).broadcast_to([P, NH, WTOK]),
                                        ALU.subtract).then_inc(low_ready, 1)

            def invert(n, k):
                dve.wait_ge(probs_ready, n + 1)
                wait_above_zero(dve, inv_ready, n - 1)
                nc.vector.tensor_reduce(p_sum[:, k % 2, :], probs[:, k % 2], AX.X, ALU.add).then_inc(sum_ready, 1)
                dve.wait_ge(sum_ready, n + 1)
                wait_above_zero(dve, norm_ready, n - 1)
                nc.vector.reciprocal(p_inv[:, k % 2, :], p_sum[:, k % 2, :]).then_inc(inv_ready, 1)

            def own_window(u):
                dve.wait_ge(pv_ready, QUAD * (u + 1))
                wait_above_zero(dve, h_ready, u)
                nc.vector.scalar_tensor_tensor(
                    out=o_own[:], in0=o_t[:], scalar=cols_s[:, 4:5],
                    in1=omask_s[:].rearrange("p (a c) -> p a c", a=1).broadcast_to([P, QUAD, P]),
                    op0=ALU.add, op1=ALU.mult).then_inc(o_ready, 1)

            def keep_rows(u):
                dve.wait_ge(rows_ready, u + 1)
                nc.vector.tensor_copy(tokens[:, ds(QUAD * u, QUAD), :], rows_ps[:, :, 0:C]).then_inc(rows_copied, 1)

            def turn(i, kind):
                for k in range(PER):
                    n = i * PER + k
                    if k == 0 and kind != "tail":
                        rotate(2 * i + 1, 1)
                    if k == QUAD and kind in ("first", "mid"):
                        rotate(2 * i + 2, 0)
                    if kind != "tail":
                        lower(n, k)
                    if runs(kind, k, 1):
                        invert(n - 1, (k - 1) % PER)
                    if k == 3 and kind != "first":
                        own_window(2 * i - 1)
                    if k == 7 and kind != "tail":
                        own_window(2 * i)
                    if k == 3 and kind != "tail":
                        mask_v(2 * i + 1, 1)
                    if k == 7 and kind in ("first", "mid"):
                        mask_v(2 * i + 2, 0)
                    if kind != "first" and k in (2, 6):
                        keep_rows(2 * i - 2 + k // 4)

            nc.vector.memset(q_diag[:], 0.0).then_inc(diag_zero, 1)
            dve.wait_ge(diag_zero, 1)
            dve.wait_ge(consts_loaded, ALL_CONSTS)
            rotate(0, 0)
            mask_v(0, 0)
            run_turns(dve, turn)

        @block.gpsimd
        def _(pool):
            def split_heads(n, k, u):
                half, p = k // QUAD, k % QUAD
                if p == 0:
                    pool.wait_ge(rotated, 3 * u + 3)
                wait_above_zero(pool, scores_ready, n - PER + 1)
                nc.gpsimd.tensor_tensor(k_heads[:, half, p], k_rot[:, half, p:p + 1, :].broadcast_to([P, NH, WTOK]),
                                        hmask_s[:].rearrange("p (h a) -> p h a", a=1).broadcast_to([P, NH, WTOK]),
                                        ALU.mult).then_inc(k_ready, 1)

            def normalize(n, k):
                pool.wait_ge(inv_ready, n + 1)
                wait_above_zero(pool, pt_ready, n - 1)
                nc.gpsimd.tensor_tensor(p_norm[:, k % 2], probs[:, k % 2],
                                        p_inv[:, k % 2, :].rearrange("p (h a) -> p h a", a=1).broadcast_to([P, NH, WTOK]),
                                        ALU.mult).then_inc(norm_ready, 1)

            def turn(i, kind):
                for k in range(PER):
                    n = i * PER + k
                    if kind != "tail":
                        if not (kind == "last" and k >= PER - 2):
                            split_heads(n + 2, (k + 2) % PER, 2 * i + (k + 2) // QUAD)
                    if runs(kind, k, 1):
                        normalize(n - 1, (k - 1) % PER)

            pool.wait_ge(consts_loaded, ALL_CONSTS)
            for k in range(2):
                split_heads(k, k, 0)
            run_turns(pool, turn)

        @block.scalar
        def _(act):
            def exponent(n, k):
                act.wait_ge(low_ready, n + 1)
                wait_above_zero(act, norm_ready, n - 1)
                nc.scalar.activation(probs[:, k % 2], s_low[:, k % 2], ACT.Exp, scale=HEAD_SCALE).then_inc(probs_ready, 1)

            def copy_turned(n, k):
                act.wait_ge(pt_ready, n + 1)
                wait_above_zero(act, pv_ready, n - 1)
                nc.scalar.copy(p_turn[:, k % 2], p_t[k % 2][:]).then_inc(pt_copied, 1)

            def add_bias(u):
                act.wait_ge(h_ready, u + 1)
                wait_above_zero(act, rows_ready, u)
                nc.scalar.activation(h_cols[:], h_t[:], ACT.Identity, bias=cols_s[:, 5:6]).then_inc(h_copied, 1)

            def turn(i, kind):
                for k in range(PER):
                    n = i * PER + k
                    if kind != "tail":
                        exponent(n, k)
                    if runs(kind, k, 2):
                        copy_turned(n - 2, (k - 2) % PER)
                    if kind != "first" and k in (0, 4):
                        add_bias(2 * i - 2 + k // 4)

            act.wait_ge(consts_loaded, ALL_CONSTS)
            run_turns(act, turn)


def window_layout(x, qkv_w, qkv_b, proj_w, proj_b):
    f = np.float32
    nw = SIDE // WIN
    xw = x.reshape(B, nw, WIN, nw // 2, 2, WIN, C)
    xw = xw.transpose(0, 1, 3, 4, 6, 2, 5).reshape(NQUAD, QUAD, 2, C, WTOK)
    xw = xw.transpose(0, 2, 3, 1, 4).reshape(NQUAD, P, QUAD * WTOK)
    swap = np.arange(C) ^ 1
    wq, wk, wv = qkv_w[0:C], qkv_w[C:2 * C], qkv_w[2 * C:3 * C]
    bq, bk, bv = qkv_b[0:C], qkv_b[C:2 * C], qkv_b[2 * C:3 * C]
    wqk = np.zeros((P, 4, P), f)
    for m, w in enumerate((wq, wq[swap], wk, wk[swap])):
        for s in (slice(0, 64), slice(64, 128)):
            wqk[s, m, s] = w.T
    wvx = np.zeros((2, C, 4, 2, 16), f)
    for w in range(2):
        wvx[w, :, :, w, :] = wv.T.reshape(C, 4, 16)
    wpx = np.zeros((4, 2, 16, C), f)
    for w in range(2):
        wpx[:, w] = proj_w.T.reshape(4, 16, C)
    cols = np.zeros((P, 8), f)
    for m, b in enumerate((bq, bq[swap], bk, bk[swap])):
        cols[:, m] = np.concatenate([b, b])
    bvx = np.zeros((4, 2, 16), f)
    for w in range(2):
        bvx[:, w] = bv.reshape(4, 16)
    cols[:, 4] = bvx.reshape(P)
    cols[:, 5] = np.concatenate([proj_b, proj_b])
    half = HD // 2
    freq = (1.0 / 10000.0 ** (np.arange(0, half, 2, dtype=f) / f(half))).astype(f)
    cos, sin = np.zeros((C, WIN, WIN), f), np.zeros((C, WIN, WIN), f)
    for c in range(C):
        d = c % HD
        ang = np.arange(WIN, dtype=f) * freq[(d % half) // 2]
        ang = ang[:, None] + np.zeros((1, WIN), f) if d < half else ang[None, :] + np.zeros((WIN, 1), f)
        cos[c] = np.cos(ang)
        sin[c] = np.sin(ang) if d % 2 else -np.sin(ang)
    trig = np.stack([cos.reshape(C, WTOK), sin.reshape(C, WTOK)], 1)
    trig = np.concatenate([trig, trig]).reshape(P, 2 * WTOK)
    rows = np.arange(P)
    hmask = (((rows % C) // HD)[:, None] == np.arange(NH)[None, :]).astype(f)
    vmask = ((rows // 64)[:, None] == ((rows % 16) // HD)[None, :]).astype(f)
    omask = (((rows % 32) // 16)[:, None] == (rows // 64)[None, :]).astype(f)
    return dict(xw=xw, wqk=wqk.reshape(P, 4 * P), wv=wvx.reshape(P, P), wp=np.tile(wpx.reshape(P, C), (1, 2)), cols=cols, trig=trig,
                hmask=hmask, vmask=vmask, omask=omask, ident=np.eye(P, dtype=f))


TT = 384
CH = TT // P
NT = (SIDE * SIDE + TXT) // P
TILES = NT // CH
KEYS = NT * P
GROUPS = [2] * 13 + [1] * 7
NG = len(GROUPS)
FIRST = [sum(GROUPS[:g]) for g in range(NG)]
LAG = 3
RING = 4
assert NG % RING == 0
NMAX = CH * TILES
NPAIRS = (NMAX + 1) // 2
MAX_PER = [2] * 16 + [1] + [0] * 3
MAX_FROM = [sum(MAX_PER[:g]) for g in range(NG)]
DVE_HIGH = [1, 4, 7, 10, 12, 17, 19]
ACT_HIGH = [g for g in range(NG) if g not in DVE_HIGH]
DVE_LOW = 1 / 4
OUT_AT = 4
Q_AT = 8
KEY_AT = 12
SHIFT_AT, SHIFT_OUT = 17, 18
CENTRE_AT, SQUARE_AT, VAR_AT, POW_AT, NODES_AT = 5, 6, 7, 8, 9
AHEAD = 2
SLOTS = 3
LN_EPS = 1e-5
NORM = C ** -0.5


def above(eng, sem, count):
    if not isinstance(count, int) or count > 0:
        eng.wait_ge(sem, count)


def full_attention(nc, w2x, ident, fold, tokens):
    with ExitStack() as ctx:
        def sb(name, shape, dt=F32):
            return ctx.enter_context(nc.sbuf_tensor(name, shape, dt))

        def ps(name, shape):
            return ctx.enter_context(nc.psum_tensor(name, shape, F32))

        def sem(name):
            return ctx.enter_context(nc.semaphore(name))

        w2x_s = sb("w2x_s", [P, P])
        ident_b = sb("ident_b", [P, P])
        fold_s = sb("fold_s", [P, C + 1])
        half_s = sb("half_s", [P, CH])
        stat = sb("stat", [P, SLOTS, 4, CH])
        centred = sb("centred", [P, SLOTS, CH, C])
        square = sb("square_b", [P, SLOTS, CH, C])
        nodes2 = sb("nodes2", [P, CH, 2, C])
        nodes = sb("nodes", [P, NT, C])
        values_s = sb("values_s", [P, NT, 2 * C], F32R)
        residue = sb("residue", [P, NT])
        keys_t = sb("keys_t", [P, KEYS])
        k_hi = sb("k_hi", [P, KEYS], F32R)
        k_lo = sb("k_lo", [P, KEYS], F32R)
        q_both = sb("q_both", [P, KEYS], F32R)
        q_hi = sb("q_hi", [P, KEYS], F32R)
        q_own = sb("q_own", [P, TT], F32R)
        cmax = sb("cmax", [P, NMAX])
        neg_max = sb("neg_max", [P, CH, C + 1])
        probs = sb("probs_b", [P, RING, 2 * TT])
        p_hi = sb("p_hi", [P, RING, 2 * TT], F32R)
        p_lo = sb("p_lo", [P, RING, 2 * TT], F32R)
        out_cols = sb("out_cols", [P, TT])
        sum_inv = sb("sum_inv", [P, CH, 1])

        s_ps = [ps(f"s_ps{i}", [P, 2, 512]) for i in range(2)]
        max_ps = [ps(f"max_ps{i}", [P, 512]) for i in range(2)]
        o_ps = ps("o_ps", [P, 512])
        turn_ps = ps("turn_ps", [P, 512])

        loaded = sem("b_loaded")
        filled = sem("filled")
        half_ready = sem("half_ready")
        sum_ready = sem("b_sum_ready")
        mean_ready = sem("mean_ready")
        centred_ready = sem("centred_ready")
        square_ready = sem("square_ready")
        square_sum = sem("b_square_sum")
        var_ready = sem("var_ready")
        rstd_ready = sem("rstd_ready")
        nodes_ready = sem("nodes_ready")
        nodes_kept = sem("nodes_kept")
        residue_ready = sem("residue_ready")
        v_high = sem("v_high")
        values_ready = sem("values_ready")
        keys_turned = sem("keys_turned")
        keys_copied = sem("keys_copied")
        k_hi_ready = sem("k_hi_ready")
        k_lo_ready = sem("k_lo_ready")
        q_made = sem("q_made")
        q_rounded = sem("q_rounded")
        q_hi_ready = sem("q_hi_ready")
        q_both_ready = sem("q_both_ready")
        own_ready = sem("own_ready")
        start_made = sem("start_made")
        start_read = sem("start_read")
        max_made = sem("max_made")
        max_read = sem("max_read")
        neg_ready = sem("neg_ready")
        shift_turned = sem("shift_turned")
        shift_ready = sem("shift_ready")
        s_ready = sem("s_ready")
        p_ready = sem("p_ready")
        act_high = sem("act_high")
        dve_high = sem("dve_high")
        dve_low = sem("dve_low")
        pool_low = sem("pool_low")
        pv_done = sem("pv_done")
        out_copied = sem("out_copied")
        out_turned = sem("out_turned")
        inv_ready = sem("b_inv_ready")
        out_added = sem("out_added")

        block = ctx.enter_context(nc.Block())

        MAXIMA = NMAX * (TILES - 1)

        def turns(eng, b, turn):
            turn(b, 0, "first")
            with eng.Fori(1, TILES - 2) as t:
                turn(b, t, "mid")
            turn(b, TILES - 2, "late")
            turn(b, TILES - 1, "last")
            turn(b, TILES, "tail")

        def batches(eng, body):
            body(0, True)
            with eng.Fori(1, B - 1) as b:
                body(b, True)
            body(B - 1, False)

        def high_ready(eng, b, t, g):
            own, done = (DVE_HIGH, dve_high) if g in DVE_HIGH else (ACT_HIGH, act_high)
            eng.wait_ge(done, len(own) * (TILES * b + t) + own.index(g) + 1)

        def has_maxima(kind):
            return kind in ("first", "mid", "late")

        def makes_queries(kind, ahead):
            return kind in ("first", "mid") or (ahead and kind in ("late", "last"))

        def ahead_cols(kind, t):
            at = {"late": 0, "last": TT}.get(kind)
            return ds((t + AHEAD) * TT, TT) if at is None else slice(at, at + TT)

        @block.sync
        def _(sp):
            sp.dma_start(w2x_s[:], w2x).then_inc(loaded, 16)
            sp.dma_start(ident_b[:], ident).then_inc(loaded, 16)
            sp.dma_start(fold_s[:], fold).then_inc(loaded, 16)
            sp.wait_ge(loaded, 48)

        @block.tensor
        def _(pe):
            def turn_keys(nth):
                pe.wait_ge(nodes_ready, nth + 1)
                above(pe, keys_copied, nth)
                for j in range(CH):
                    last = nc.tensor.transpose(turn_ps[:, j * P:(j + 1) * P],
                                               nodes2[:, j].rearrange("p a c -> p (a c)"), ident_b[:])
                last.then_inc(keys_turned, 1)

            def make_queries(nth, cols):
                pe.wait_ge(keys_copied, nth + 1)
                above(pe, q_both_ready, nth)
                above(pe, q_hi_ready, nth)
                nc.tensor.matmul(turn_ps[:, 0:TT], w2x_s[:], keys_t[:, cols],
                                 start=True, stop=True).then_inc(q_made, 1)

            def first_maximum(b):
                above(pe, p_ready, NG * TILES * b)
                pe.wait_ge(own_ready, TILES * b + 1)
                for k in range(NPAIRS):
                    above(pe, start_read, NPAIRS * b + k - 1)
                    for idx in range(2 * k, min(2 * k + 2, NMAX)):
                        c, j = idx // CH, idx % CH
                        if j == 0 or idx == 2 * k:
                            pe.wait_ge(k_hi_ready, TILES * b + c + 1)
                        last = nc.tensor.matmul(s_ps[k % 2][:, idx % 2, 0:TT], q_own[:, j * P:(j + 1) * P],
                                                k_hi[:, c * TT:(c + 1) * TT], start=True, stop=True)
                    last.then_inc(start_made, 1)

            def maximum(b, t, idx):
                made = MAXIMA * b + NMAX * (t - 1) + idx
                c, j = idx // CH, idx % CH
                if idx == 0:
                    pe.wait_ge(own_ready, TILES * b + t + 1)
                above(pe, max_read, made if idx == 0 else made - 1)
                nc.tensor.matmul(max_ps[idx % 2][:, 0:TT], q_own[:, j * P:(j + 1) * P], k_hi[:, c * TT:(c + 1) * TT],
                                 start=True, stop=True).then_inc(max_made, 1)

            def turn_shift(b, t):
                pe.wait_ge(neg_ready, TILES * b + t + 1)
                for j in range(CH):
                    last = nc.tensor.transpose(turn_ps[0:C + 1, j * P:(j + 1) * P], neg_max[:, j, :], ident_b[:])
                last.then_inc(shift_turned, 1)

            def scores(b, t, g, kind):
                at = NG * (TILES * b + t) + g
                if g == 0:
                    pe.wait_ge(shift_ready, TILES * b + t + 1)
                above(pe, p_ready, at if kind == "first" and g == 0 else at - 1)
                q = ds(t * TT, TT)
                for r in range(GROUPS[g]):
                    m = FIRST[g] + r
                    if r == 1 and has_maxima(kind):
                        maximum(b, t + 1, MAX_FROM[g])
                    out = s_ps[g % 2][:, r, 0:TT]
                    nc.tensor.matmul(out, k_hi[:, m * P:(m + 1) * P], q_both[:, q], start=True, stop=False)
                    last = nc.tensor.matmul(out, k_lo[:, m * P:(m + 1) * P], q_hi[:, q], start=False, stop=True)
                last.then_inc(s_ready, 1)

            def gather(b, t, g, now, maxima):
                at = NG * (TILES * b + t) + g
                pe.wait_ge(dve_low, at + 1)
                pe.wait_ge(pool_low, at + 1)
                high_ready(pe, b, t, g)
                if g == 0:
                    above(pe, out_copied, TILES * b + t)
                for r in range(GROUPS[g]):
                    m = FIRST[g] + r
                    for part in (p_hi, p_lo):
                        last = nc.tensor.matmul(o_ps[:, 0:TT], values_s[:, m, :], part[:, g % RING, r * TT:(r + 1) * TT],
                                                start=(m == 0 and part is p_hi), stop=(m == NT - 1 and part is p_lo))
                    if r == 0:
                        for idx in maxima:
                            maximum(b, now + 1, idx)
                last.then_inc(pv_done, 1)

            def turn_out(b, t):
                pe.wait_ge(out_copied, TILES * b + t + 1)
                for j in range(CH):
                    last = nc.tensor.matmul(turn_ps[:, j * (C + 1):(j + 1) * (C + 1)],
                                            out_cols[:, j * P:(j + 1) * P], fold_s[:], start=True, stop=True)
                last.then_inc(out_turned, 1)

            def turn(b, t, kind, ahead):
                for g in range(LAG if kind == "tail" else NG):
                    if kind != "tail":
                        scores(b, t, g, kind)
                    rest = []
                    if has_maxima(kind):
                        rest = list(range(MAX_FROM[g] + (GROUPS[g] == 2), MAX_FROM[g] + MAX_PER[g]))
                        if len(rest) == 2:
                            maximum(b, t + 1, rest.pop(0))
                    if g == SHIFT_AT and has_maxima(kind):
                        if ahead:
                            pe.wait_ge(keys_copied, TILES * (b + 1) + t + 1)
                        elif kind != "late":
                            pe.wait_ge(q_both_ready, TILES * b + t + AHEAD + 1)
                            pe.wait_ge(q_hi_ready, TILES * b + t + AHEAD + 1)
                        else:
                            pe.wait_ge(out_added, CH * (TILES * b + t))
                        turn_shift(b, t + 1)
                    if g < LAG and kind != "first":
                        gather(b, t - 1, g + NG - LAG, t, rest)
                    elif g >= LAG and kind != "tail":
                        gather(b, t, g - LAG, t, rest)
                    else:
                        for idx in rest:
                            maximum(b, t + 1, idx)
                    if g == OUT_AT and kind != "first":
                        turn_out(b, t - 1)
                    if g == Q_AT and makes_queries(kind, ahead):
                        above(pe, out_added, CH * (TILES * b + t))
                        make_queries(TILES * b + t + AHEAD, ahead_cols(kind, t))
                    if g == KEY_AT and ahead:
                        pe.wait_ge(q_both_ready, TILES * b + t + AHEAD + 1)
                        pe.wait_ge(q_hi_ready, TILES * b + t + AHEAD + 1)
                        turn_keys(TILES * (b + 1) + t)

            def batch(b, ahead):
                if not isinstance(b, int) or b > 0:
                    pe.wait_ge(keys_copied, TILES * (b + 1))
                    turn_out(b - 1, TILES - 1)
                first_maximum(b)
                above(pe, out_added, CH * TILES * b)
                turn_shift(b, 0)
                pe.wait_ge(start_read, NPAIRS * (b + 1))
                pe.wait_ge(k_lo_ready, TILES * (b + 1))
                pe.wait_ge(values_ready, b + 1)
                turns(pe, b, lambda b, t, kind: turn(b, t, kind, ahead))

            pe.wait_ge(loaded, 48)
            for t in range(TILES):
                turn_keys(t)
            pe.wait_ge(keys_copied, TILES)
            for t in range(AHEAD):
                make_queries(t, slice(t * TT, (t + 1) * TT))
            pe.wait_ge(q_both_ready, AHEAD)
            pe.wait_ge(q_hi_ready, AHEAD)
            batches(pe, batch)
            pe.wait_ge(out_added, CH * (TILES * B - 1))
            turn_out(B - 1, TILES - 1)

        @block.scalar
        def _(act):
            def squares(nth, slot):
                act.wait_ge(centred_ready, nth + 1)
                nc.scalar.activation(square[:, slot], centred[:, slot], ACT.Square).then_inc(square_ready, 1)

            def keep_nodes(nth, at):
                act.wait_ge(nodes_ready, nth + 1)
                nc.scalar.copy(nodes[:, at, :], nodes2[:, :, 0, :]).then_inc(nodes_kept, 1)

            def copy_keys(nth, cols):
                act.wait_ge(keys_turned, nth + 1)
                nc.scalar.copy(keys_t[:, cols], turn_ps[:, 0:TT]).then_inc(keys_copied, 1)

            def copy_queries(nth, cols):
                act.wait_ge(q_made, nth + 1)
                nc.scalar.copy(q_both[:, cols], turn_ps[:, 0:TT]).then_inc(q_rounded, 1)
                nc.scalar.copy(q_hi[0:C, cols], turn_ps[0:C, 0:TT]).then_inc(q_hi_ready, 1)

            def copy_out(b, t):
                act.wait_ge(pv_done, NG * (TILES * b + t + 1))
                above(act, out_turned, TILES * b + t)
                nc.scalar.copy(out_cols[:], o_ps[:, 0:TT]).then_inc(out_copied, 1)

            def copy_shift(b, t):
                act.wait_ge(shift_turned, TILES * b + t + 1)
                nc.scalar.copy(q_hi[C:C + 1, ds(t * TT, TT)], turn_ps[C:C + 1, 0:TT]).then_inc(shift_ready, 1)

            def turn(b, t, kind, ahead):
                for g in range(LAG if kind == "tail" else NG):
                    at = NG * (TILES * b + t) + g
                    n = GROUPS[g]
                    if kind != "tail":
                        act.wait_ge(s_ready, at + 1)
                        above(act, dve_low, at + 1 - RING)
                        above(act, pool_low, at + 1 - RING)
                        nc.scalar.activation(probs[:, g % RING, 0:n * TT].rearrange("p (r q) -> p r q", r=n),
                                             s_ps[g % 2][:, 0:n, 0:TT], ACT.Exp, scale=NORM).then_inc(p_ready, 1)
                    if g == LAG - 1 and kind != "first":
                        copy_out(b, t - 1)
                    if g == SHIFT_OUT and has_maxima(kind):
                        copy_shift(b, t + 1)
                    if kind != "tail" and g in ACT_HIGH:
                        act.wait_ge(p_ready, at + 1)
                        above(act, pv_done, at + 1 - RING)
                        nc.scalar.copy(p_hi[:, g % RING, 0:n * TT], probs[:, g % RING, 0:n * TT]).then_inc(act_high, 1)
                    nth = TILES * (b + 1) + t
                    if g == Q_AT + 1 and makes_queries(kind, ahead):
                        copy_queries(TILES * b + t + AHEAD, ahead_cols(kind, t))
                    if ahead and kind != "tail":
                        if g == SQUARE_AT:
                            act.wait_ge(square_sum, nth)
                            squares(nth, 0)
                        if g == NODES_AT + 2:
                            act.wait_ge(values_ready, b + 1)
                            keep_nodes(nth, ds(CH * t, CH))
                        if g == KEY_AT + 1:
                            act.wait_ge(k_lo_ready, TILES * (b + 1))
                            copy_keys(nth, ds(TT * t, TT))

            def batch(b, ahead):
                above(act, s_ready, NG * TILES * b)
                for c in range(TILES):
                    cols = slice(c * TT, (c + 1) * TT)
                    act.wait_ge(keys_copied, TILES * b + c + 1)
                    nc.scalar.copy(k_hi[:, cols], keys_t[:, cols]).then_inc(k_hi_ready, 1)
                act.wait_ge(nodes_kept, TILES * (b + 1))
                act.wait_ge(residue_ready, TILES * (b + 1))
                nc.scalar.copy(values_s[:, :, 0:C - 1], nodes[:, :, 0:C - 1])
                nc.scalar.copy(values_s[:, :, C - 1:C], residue[:].rearrange("p (n a) -> p n a", a=1)).then_inc(v_high, 1)
                copy_shift(b, 0)
                turns(act, b, lambda b, t, kind: turn(b, t, kind, ahead))

            for s in range(TILES + 2):
                if s < TILES:
                    above(act, square_sum, s + 1 - SLOTS)
                    squares(s, s % SLOTS)
                if s >= 2:
                    keep_nodes(s - 2, slice(CH * (s - 2), CH * (s - 1)))
                    copy_keys(s - 2, slice(TT * (s - 2), TT * (s - 1)))
            act.wait_ge(filled, 5)
            for t in range(AHEAD):
                copy_queries(t, slice(t * TT, (t + 1) * TT))
            batches(act, batch)

        @block.gpsimd
        def _(pool):
            def power(nth, slot):
                pool.wait_ge(var_ready, nth + 1)
                nc.gpsimd.tensor_tensor(stat[:, slot, 3, :], stat[:, slot, 2, :], half_s[:], ALU.pow).then_inc(rstd_ready, 1)

            def turn(b, t, kind, ahead):
                for g in range(0 if kind == "tail" else NG):
                    w = GROUPS[g] * TT
                    own = slice(int(w * DVE_LOW), w)
                    high_ready(pool, b, t, g)
                    nc.gpsimd.tensor_tensor(p_lo[:, g % RING, own], probs[:, g % RING, own],
                                            p_hi[:, g % RING, own].bitcast(F32), ALU.subtract).then_inc(pool_low, 1)
                    if g == POW_AT - 1 and ahead:
                        pool.wait_ge(nodes_ready, TILES * (b + 1) + t)
                        power(TILES * (b + 1) + t, 0)

            def batch(b, ahead):
                for c in range(TILES):
                    cols = slice(c * TT, (c + 1) * TT)
                    pool.wait_ge(k_hi_ready, TILES * b + c + 1)
                    nc.gpsimd.tensor_tensor(k_lo[0:C, cols], keys_t[0:C, cols], k_hi[0:C, cols].bitcast(F32),
                                            ALU.subtract).then_inc(k_lo_ready, 1)
                pool.wait_ge(v_high, b + 1)
                nc.gpsimd.tensor_tensor(values_s[:, :, C:2 * C - 1], nodes[:, :, 0:C - 1],
                                        values_s[:, :, 0:C - 1].bitcast(F32), ALU.subtract).then_inc(values_ready, 1)
                turns(pool, b, lambda b, t, kind: turn(b, t, kind, ahead))

            nc.gpsimd.memset(half_s[:], -0.5).then_inc(half_ready, 1)
            nc.gpsimd.memset(neg_max[:], 0.0).then_inc(filled, 1)
            nc.gpsimd.memset(values_s[:, :, 2 * C - 1:2 * C].bitcast(F32), 1.0).then_inc(filled, 1)
            pool.wait_ge(half_ready, 1)
            for t in range(TILES):
                above(pool, nodes_ready, t + 1 - SLOTS)
                power(t, t % SLOTS)
            pool.wait_ge(rstd_ready, TILES)
            nc.gpsimd.memset(q_hi[C:P, :].bitcast(F32), 0.0).then_inc(filled, 1)
            pool.wait_ge(filled, 3)
            nc.gpsimd.memset(k_lo[C:P, :].bitcast(F32), 0.0).then_inc(filled, 1)
            pool.wait_ge(filled, 4)
            nc.gpsimd.memset(k_lo[C:C + 1, :].bitcast(F32), 1.0).then_inc(filled, 1)
            pool.wait_ge(filled, 5)
            batches(pool, batch)

        @block.vector
        def _(dve):
            def per_token(slot, row):
                return stat[:, slot, row, :].rearrange("p (n a) -> p n a", a=1)

            def centre(nth, slot, parts):
                for own, at in parts:
                    last = nc.vector.tensor_reduce(stat[:, slot, 0, own], tokens[:, at, :], AX.X, ALU.add)
                last.then_inc(sum_ready, 1)
                dve.wait_ge(sum_ready, nth + 1)
                nc.vector.tensor_scalar(stat[:, slot, 1, :], stat[:, slot, 0, :], 1.0 / C, None, ALU.mult)\
                    .then_inc(mean_ready, 1)
                dve.wait_ge(mean_ready, nth + 1)
                for own, at in parts:
                    n = own.stop - own.start
                    last = nc.vector.tensor_tensor(centred[:, slot, own, :], tokens[:, at, :],
                                                   per_token(slot, 1)[:, own, :].broadcast_to([P, n, C]), ALU.subtract)
                last.then_inc(centred_ready, 1)

            def variance(nth, slot):
                dve.wait_ge(square_ready, nth + 1)
                nc.vector.tensor_reduce(stat[:, slot, 0, :], square[:, slot], AX.X, ALU.add).then_inc(square_sum, 1)
                dve.wait_ge(square_sum, nth + 1)
                nc.vector.tensor_scalar(stat[:, slot, 2, :], stat[:, slot, 0, :], 1.0 / C, LN_EPS, ALU.mult, ALU.add)\
                    .then_inc(var_ready, 1)

            def normalize(nth, slot, at):
                dve.wait_ge(rstd_ready, nth + 1)
                above(dve, keys_turned, nth)
                above(dve, nodes_kept, nth)
                above(dve, residue_ready, nth)
                nc.vector.tensor_tensor(
                    nodes2[:], centred[:, slot].rearrange("p n (a c) -> p n a c", a=1).broadcast_to([P, CH, 2, C]),
                    stat[:, slot, 3, :].rearrange("p (n a c) -> p n a c", a=1, c=1).broadcast_to([P, CH, 2, C]),
                    ALU.mult).then_inc(nodes_ready, 1)
                dve.wait_ge(nodes_ready, nth + 1)
                nc.vector.tensor_reduce(residue[:, at], nodes2[:, :, 0, :], AX.X, ALU.add).then_inc(residue_ready, 1)

            def low_queries(nth, cols):
                dve.wait_ge(q_rounded, nth + 1)
                nc.vector.tensor_tensor(q_both[C:P, cols], turn_ps[C:P, 0:TT], q_both[C:P, cols].bitcast(F32),
                                        ALU.subtract).then_inc(q_both_ready, 1)

            def take_own(nth, cols):
                dve.wait_ge(q_both_ready, nth + 1)
                nc.vector.tensor_copy(q_own[:], q_both[:, cols].bitcast(F32)).then_inc(own_ready, 1)

            def high(b, t, g):
                at = NG * (TILES * b + t) + g
                w = GROUPS[g] * TT
                dve.wait_ge(p_ready, at + 1)
                above(dve, pv_done, at + 1 - RING)
                nc.vector.tensor_copy(p_hi[:, g % RING, 0:w], probs[:, g % RING, 0:w]).then_inc(dve_high, 1)

            def low(b, t, g):
                own = slice(0, int(GROUPS[g] * TT * DVE_LOW))
                high_ready(dve, b, t, g)
                nc.vector.tensor_tensor(p_lo[:, g % RING, own], probs[:, g % RING, own],
                                        p_hi[:, g % RING, own].bitcast(F32), ALU.subtract).then_inc(dve_low, 1)

            def split_at(b, t, g):
                if g < 0:
                    t, g = t - 1, NG - 1
                if g in DVE_HIGH:
                    high(b, t, g)
                low(b, t, g)

            def read_first_maximum(b):
                for k in range(NPAIRS):
                    n = min(2, NMAX - 2 * k)
                    dve.wait_ge(start_made, NPAIRS * b + k + 1)
                    nc.vector.tensor_reduce(cmax[:, 2 * k:2 * k + n], s_ps[k % 2][:, 0:n, 0:TT], AX.X, ALU.max)\
                        .then_inc(start_read, 1)
                dve.wait_ge(start_read, NPAIRS * (b + 1))

            def read_max(b, t, idx):
                made = MAXIMA * b + NMAX * (t - 1) + idx
                dve.wait_ge(max_made, made + 1)
                if idx == 0:
                    dve.wait_ge(neg_ready, TILES * b + t)
                nc.vector.tensor_reduce(cmax[:, idx:idx + 1], max_ps[idx % 2][:, 0:TT], AX.X, ALU.max).then_inc(max_read, 1)

            def negate(b, t):
                above(dve, shift_turned, TILES * b + t)
                nc.vector.tensor_reduce(neg_max[:, :, C:C + 1], cmax[:].rearrange("p (c j) -> p j c", j=CH), AX.X, ALU.max,
                                        negate=True).then_inc(neg_ready, 1)

            def add_out(b, t, kind):
                dve.wait_ge(out_turned, TILES * b + t + 1)
                turned = turn_ps[:, 0:CH * (C + 1)].rearrange("p (j c) -> p j c", j=CH)
                nc.vector.reciprocal(sum_inv[:], turned[:, :, C:C + 1]).then_inc(inv_ready, 1)
                dve.wait_ge(inv_ready, TILES * b + t + 1)
                for j in range(CH):
                    if kind == "tail" and j == CH - 1:
                        at = ds(NPAIR + b, 1)
                    else:
                        at = ds((NT - 1) * b + CH * t + j, 1)
                    nc.vector.scalar_tensor_tensor(out=tokens[:, at, :].rearrange("p a c -> p (a c)"),
                                                   in0=turned[:, j, 0:C], scalar=sum_inv[:, j, :],
                                                   in1=tokens[:, at, :].rearrange("p a c -> p (a c)"),
                                                   op0=ALU.mult, op1=ALU.add).then_inc(out_added, 1)

            def places(b, t, last):
                if last:
                    return [(slice(0, CH - 1), ds((NT - 1) * b + CH * t, CH - 1)), (slice(CH - 1, CH), ds(NPAIR + b, 1))]
                return [(slice(0, CH), ds((NT - 1) * b + CH * t, CH))]

            def turn(b, t, kind, ahead):
                for g in range(1 if kind == "tail" else NG):
                    reads = MAX_PER[g] if has_maxima(kind) else 0
                    for k in range(max(reads, 1)):
                        if k < reads:
                            read_max(b, t + 1, MAX_FROM[g] + k)
                            if MAX_FROM[g] + k == NMAX - 1:
                                dve.wait_ge(max_read, MAXIMA * b + NMAX * (t + 1))
                                negate(b, t + 1)
                        if k == 0 and not (kind == "first" and g == 0):
                            split_at(b, t, g - 1)
                    if g == OUT_AT and kind != "first":
                        add_out(b, t - 1, kind)
                    if kind != "tail" and ahead:
                        nth = TILES * (b + 1) + t
                        if g == CENTRE_AT:
                            dve.wait_ge(nodes_ready, nth)
                            centre(nth, 0, places(b + 1, t, kind == "last"))
                        if g == VAR_AT:
                            variance(nth, 0)
                        if g == NODES_AT:
                            dve.wait_ge(v_high, b + 1)
                            normalize(nth, 0, ds(CH * t, CH))
                    if g == Q_AT + 2 and makes_queries(kind, ahead):
                        low_queries(TILES * b + t + AHEAD, ahead_cols(kind, t))
                    if g == SHIFT_AT and (kind in ("first", "mid") or (kind == "late" and ahead)):
                        take_own(TILES * b + t + AHEAD, ahead_cols(kind, t))

            def batch(b, ahead):
                if not isinstance(b, int) or b > 0:
                    add_out(b - 1, TILES - 1, "tail")
                read_first_maximum(b)
                negate(b, 0)
                take_own(TILES * b + 1, slice(TT, 2 * TT))
                turns(dve, b, lambda b, t, kind: turn(b, t, kind, ahead))

            for s in range(TILES + 2):
                if s < TILES:
                    above(dve, nodes_ready, s + 1 - SLOTS)
                    centre(s, s % SLOTS, places(0, s, s == TILES - 1))
                if 1 <= s <= TILES:
                    variance(s - 1, (s - 1) % SLOTS)
                if s >= 2:
                    normalize(s - 2, (s - 2) % SLOTS, slice(CH * (s - 2), CH * (s - 1)))
            dve.wait_ge(filled, 5)
            for t in range(AHEAD):
                low_queries(t, slice(t * TT, (t + 1) * TT))
            take_own(0, slice(0, TT))
            batches(dve, batch)
            add_out(B - 1, TILES - 1, "tail")


def attention_layout(w):
    w2x = np.zeros((P, P), np.float32)
    w2x[0:C, 0:C] = w
    w2x[0:C, C:P] = w
    fold = np.zeros((P, C + 1), np.float32)
    for c in range(C - 1):
        for row in (c, C + c):
            fold[row, c] = 1.0
            fold[row, C - 1] = -1.0
    fold[C - 1, C - 1] = 1.0
    fold[P - 1, C] = 1.0
    return w2x, fold


U32 = mybir.dt.uint32
E, F = 16, 128
BT = 4
BW = BT * P
NTILES = NPAIR + B
NBLOCK = NTILES // BT
LO = 32


def experts(nc, gate_w, w1, w2, sel, b2, b1, gate_b, rows, ident, tokens, out):
    with ExitStack() as ctx:
        def sb(name, shape, dt=F32):
            return ctx.enter_context(nc.sbuf_tensor(name, shape, dt))

        def ps(name, shape):
            return ctx.enter_context(nc.psum_tensor(name, shape, F32))

        def sem(name):
            return ctx.enter_context(nc.semaphore(name))

        ident_c = sb("ident_c", [P, P])
        gate_w_s = sb("gate_w_s", [P, P])
        w1_s = sb("w1_s", [P, E, F])
        w1_hi = sb("w1_hi", [P, E, F], F32R)
        w1_lo = sb("w1_lo", [P, E, F], F32R)
        w2_s = sb("w2_s", [P, E, 2, C])
        sel_s = sb("sel_s", [P, E, P])
        sel_r = sb("sel_r", [P, E, P], F32R)
        b2_s = sb("b2_s", [P, P])
        b2_hi = sb("b2_hi", [P, P], F32R)
        b2_lo = sb("b2_lo", [P, P], F32R)
        b1_s = sb("b1_s", [P, E])
        gate_b_s = sb("gate_b_s", [P, 1])
        rows_s = sb("rows_s", [P, 2, C])
        places = sb("places", [P, E])

        stat = sb("c_stat", [P, 4, BT])
        centred = sb("c_centred", [P, BT, C])
        square = sb("c_square", [P, BT, C])
        y = sb("y", [P, BT, 2, C])
        y_kept = sb("y_kept", [P, 2, BT, C])
        y_t = sb("y_t", [P, BW])
        y_both = sb("y_both", [P, 2, BW], F32R)
        logit_cols = sb("logit_cols", [P, BW])
        logits = sb("logits", [P, BT, E])
        top = sb("top", [P, BT, 8])
        top_at = sb("top_at", [P, BT, 8], U32)
        at_f = sb("at_f", [P, BT, 2])
        is_top = sb("is_top", [P, 2, BT, E])
        gap = sb("gap", [P, 4, BT])
        gates = sb("gates", [P, BT, P // LO, LO])
        gates_t = sb("gates_t", [P, 2, BW], F32R)
        hidden = sb("hidden", [P, 2, BW])
        gated = sb("gated", [P, 2, BW])
        moe_cols = sb("moe_cols", [P, BW])
        total = sb("total", [P, BT, C])
        f_stat = sb("f_stat", [P, 4, BT])
        f_centred = sb("f_centred", [P, BT, C])
        f_square = sb("f_square", [P, BT, C])
        f_norm = sb("f_norm", [P, BT, C])
        f_scaled = sb("f_scaled", [P, BT, C])
        f_shift = sb("f_shift", [P, BT, C])
        result = sb("result", [P, 2, BT, C])

        z_ps = [ps(f"z_ps{i}", [P, BW]) for i in range(2)]
        gate_ps = [ps(f"gate_ps{i}", [P, BW]) for i in range(2)]
        moe_ps = ps("moe_ps", [P, BW])
        prep_a = ps("prep_a", [P, BW])
        prep_b = ps("prep_b", [P, BW])
        back_ps = ps("back_ps", [P, BW])

        loaded = sem("c_loaded")
        filled = sem("c_filled")
        rounded = sem("c_rounded")
        weights_ready = sem("weights_ready")
        sum_ready = sem("c_sum_ready")
        mean_ready = sem("c_mean_ready")
        centred_ready = sem("c_centred_ready")
        square_ready = sem("c_square_ready")
        square_sum = sem("c_square_sum")
        var_ready = sem("c_var_ready")
        std_ready = sem("c_std_ready")
        rstd_ready = sem("c_rstd_ready")
        y_ready = sem("y_ready")
        y_kept_ready = sem("y_kept_ready")
        y_turned = sem("y_turned")
        y_copied = sem("y_copied")
        y_rounded = sem("y_rounded")
        y_both_ready = sem("y_both_ready")
        logits_made = sem("logits_made")
        logits_biased = sem("logits_biased")
        logits_turned = sem("logits_turned")
        logits_ready = sem("logits_ready")
        top_ready = sem("top_ready")
        top_at_ready = sem("top_at_ready")
        at_ready = sem("at_ready")
        is_top_ready = sem("is_top_ready")
        gap_ready = sem("gap_ready")
        gap_exp = sem("gap_exp")
        gap_sum = sem("gap_sum")
        first_ready = sem("first_ready")
        second_ready = sem("second_ready")
        weighed = sem("weighed")
        gates_ready = sem("gates_ready")
        gates_turned = sem("gates_turned")
        gates_rounded = sem("gates_rounded")
        gates_t_ready = sem("gates_t_ready")
        gate_spread = sem("gate_spread")
        z_ready = sem("z_ready")
        hidden_ready = sem("hidden_ready")
        gated_ready = sem("gated_ready")
        moe_step = sem("moe_step")
        moe_copied = sem("moe_copied")
        moe_turned = sem("moe_turned")
        total_ready = sem("total_ready")
        f_sum_ready = sem("f_sum_ready")
        f_mean_ready = sem("f_mean_ready")
        f_centred_ready = sem("f_centred_ready")
        f_square_ready = sem("f_square_ready")
        f_square_sum = sem("f_square_sum")
        f_var_ready = sem("f_var_ready")
        f_std_ready = sem("f_std_ready")
        f_rstd_ready = sem("f_rstd_ready")
        f_norm_ready = sem("f_norm_ready")
        f_scaled_ready = sem("f_scaled_ready")
        f_shift_ready = sem("f_shift_ready")
        result_ready = sem("result_ready")
        stored = [sem(f"stored{h}") for h in range(2)]

        consts = [(ident_c[:], ident), (gate_w_s[:], gate_w), (w1_s[:].rearrange("p e f -> p (e f)"), w1),
                  (w2_s[:].rearrange("p e a c -> p (e a c)"), w2), (sel_s[:].rearrange("p e c -> p (e c)"), sel),
                  (b2_s[:], b2), (b1_s[:], b1), (gate_b_s[:], gate_b),
                  (rows_s[:].rearrange("p a c -> p (a c)"), rows[:, 0:2 * C]), (places[:], rows[:, 2 * C:2 * C + E])]
        ALL_CONSTS = 16 * len(consts)

        block = ctx.enter_context(nc.Block())

        def run_blocks(eng, step):
            step(0, 0, "first")
            with eng.Fori(0, (NBLOCK - 3) // 2) as i:
                step(2 * i + 1, 1, "mid")
                step(2 * i + 2, 0, "mid")
            step(NBLOCK - 2, 1, "mid")
            step(NBLOCK - 1, 0, "last")
            step(NBLOCK, 1, "tail")

        @block.sync
        def _(sp):
            for dst, src in consts:
                sp.dma_start(dst, src).then_inc(loaded, 16)

            def store(n, half):
                sp.wait_ge(result_ready, n + 1)
                sp.dma_start(out[ds(BT * n, BT)].rearrange("n p c -> p n c"), result[:, half]).then_inc(stored[half], 16)

            with sp.Fori(0, NBLOCK // 2) as i:
                store(2 * i, 0)
                store(2 * i + 1, 1)
            store(NBLOCK - 1, 0)
            sp.wait_ge(stored[0], 16 * (NBLOCK // 2 + 1))
            sp.wait_ge(stored[1], 16 * (NBLOCK // 2))

        @block.tensor
        def _(pe):
            def turn_y(n, half):
                pe.wait_ge(y_ready, n + 1)
                wait_above_zero(pe, top_ready, BT * n)
                for j in range(BT):
                    last = nc.tensor.transpose(prep_a[:, j * P:(j + 1) * P], y[:, j].rearrange("p a c -> p (a c)"),
                                               ident_c[:])
                last.then_inc(y_turned, 1)

            def make_logits(n):
                pe.wait_ge(y_copied, n + 1)
                wait_above_zero(pe, gates_t_ready, n)
                nc.tensor.matmul(prep_b[:], gate_w_s[:], y_t[:], start=True, stop=True).then_inc(logits_made, 1)

            def turn_logits(n):
                pe.wait_ge(logits_biased, n + 1)
                pe.wait_ge(y_both_ready, n + 1)
                for j in range(BT):
                    last = nc.tensor.transpose(prep_a[:, j * P:(j + 1) * P], logit_cols[:, j * P:(j + 1) * P],
                                               ident_c[:])
                last.then_inc(logits_turned, 1)

            def turn_gates(n):
                pe.wait_ge(gates_ready, n + 1)
                for j in range(BT):
                    last = nc.tensor.transpose(prep_b[:, j * P:(j + 1) * P],
                                               gates[:, j].rearrange("p a c -> p (a c)"), ident_c[:])
                last.then_inc(gates_turned, 1)

            def spread(n, half, e):
                wait_above_zero(pe, gated_ready, E * n + e - 1)
                nc.tensor.matmul(gate_ps[e % 2][:], sel_r[:, e, :], gates_t[:, half, :],
                                 start=True, stop=True).then_inc(gate_spread, 1)

            def first_layer(n, half, e):
                wait_above_zero(pe, hidden_ready, E * n + e - 1)
                nc.tensor.matmul(z_ps[e % 2][:], w1_hi[:, e, :], y_both[:, half, :], start=True, stop=False)
                nc.tensor.matmul(z_ps[e % 2][:], w1_lo[:, e, :], y_both[:, half, :],
                                 start=False, stop=True).then_inc(z_ready, 1)

            def second_layer(n, e):
                pe.wait_ge(gated_ready, E * n + e + 1)
                nc.tensor.matmul(moe_ps[:], w2_s[:, e].rearrange("p a c -> p (a c)"), gated[:, e % 2, :], start=False,
                                 stop=(e == E - 1)).then_inc(moe_step, 1)

            def second_bias(n, half):
                wait_above_zero(pe, moe_copied, n)
                nc.tensor.matmul(moe_ps[:], b2_hi[:], gates_t[:, half, :], start=True, stop=False)
                nc.tensor.matmul(moe_ps[:], b2_lo[:], gates_t[:, half, :], start=False, stop=False)

            def turn_back(n):
                pe.wait_ge(moe_copied, n + 1)
                wait_above_zero(pe, total_ready, n)
                for j in range(BT):
                    last = nc.tensor.transpose(back_ps[:, j * P:(j + 1) * P], moe_cols[:, j * P:(j + 1) * P],
                                               ident_c[:])
                last.then_inc(moe_turned, 1)

            def prepare(n, half, e):
                if e == 2:
                    turn_y(n, half)
                if e == 4:
                    make_logits(n)
                if e == 6:
                    turn_logits(n)
                if e == 12:
                    turn_gates(n)

            def step(n, half, kind):
                if kind != "tail":
                    pe.wait_ge(y_both_ready, n + 1)
                    pe.wait_ge(gates_t_ready, n + 1)
                for e in range(E):
                    if kind != "tail":
                        spread(n, half, e)
                        first_layer(n, half, e)
                    if e == 2 and kind != "tail":
                        second_bias(n, half)
                    if e >= 2 and kind != "tail":
                        second_layer(n, e - 2)
                    if e < 2 and kind != "first":
                        second_layer(n - 1, E - 2 + e)
                    if e == 3 and kind != "first":
                        turn_back(n - 1)
                    if kind in ("first", "mid"):
                        prepare(n + 1, 1 - half, e)

            pe.wait_ge(loaded, ALL_CONSTS)
            pe.wait_ge(weights_ready, 3)
            for e in range(E):
                prepare(0, 0, e)
            run_blocks(pe, step)

        @block.scalar
        def _(act):
            def squares(n):
                act.wait_ge(centred_ready, n + 1)
                wait_above_zero(act, square_sum, n)
                nc.scalar.activation(square[:], centred[:], ACT.Square).then_inc(square_ready, 1)

            def deviation(n):
                act.wait_ge(var_ready, n + 1)
                wait_above_zero(act, rstd_ready, n)
                nc.scalar.activation(stat[:, 3, :], stat[:, 2, :], ACT.Sqrt).then_inc(std_ready, 1)

            def copy_y(n, half):
                act.wait_ge(y_turned, n + 1)
                wait_above_zero(act, logits_made, n)
                nc.scalar.copy(y_t[:], prep_a[:]).then_inc(y_copied, 1)
                wait_above_zero(act, z_ready, E * (n - 1))
                nc.scalar.copy(y_both[:, half, :], prep_a[:]).then_inc(y_rounded, 1)

            def add_gate_bias(n):
                act.wait_ge(logits_made, n + 1)
                wait_above_zero(act, logits_turned, n)
                nc.scalar.activation(logit_cols[:], prep_b[:], ACT.Identity, bias=gate_b_s[:])\
                    .then_inc(logits_biased, 1)

            def gap_exponent(n):
                act.wait_ge(gap_ready, n + 1)
                wait_above_zero(act, second_ready, n)
                nc.scalar.activation(gap[:, 1, :], gap[:, 0, :], ACT.Exp).then_inc(gap_exp, 1)

            def round_gates(n, half):
                act.wait_ge(gates_turned, n + 1)
                wait_above_zero(act, gate_spread, E * (n - 1))
                nc.scalar.copy(gates_t[0:2 * LO, half, :], prep_b[0:2 * LO, :]).then_inc(gates_rounded, 1)

            def relu(n, e):
                act.wait_ge(z_ready, E * n + e + 1)
                wait_above_zero(act, gated_ready, E * n + e - 1)
                nc.scalar.activation(hidden[:, e % 2, :], z_ps[e % 2][:], ACT.Relu, bias=b1_s[:, e:e + 1])\
                    .then_inc(hidden_ready, 1)

            def copy_moe(n):
                act.wait_ge(moe_step, E * (n + 1))
                wait_above_zero(act, moe_turned, n)
                nc.scalar.copy(moe_cols[:], moe_ps[:]).then_inc(moe_copied, 1)

            def f_squares(n):
                act.wait_ge(f_centred_ready, n + 1)
                wait_above_zero(act, f_square_sum, n)
                nc.scalar.activation(f_square[:], f_centred[:], ACT.Square).then_inc(f_square_ready, 1)

            def f_deviation(n):
                act.wait_ge(f_var_ready, n + 1)
                wait_above_zero(act, f_rstd_ready, n)
                nc.scalar.activation(f_stat[:, 3, :], f_stat[:, 2, :], ACT.Sqrt).then_inc(f_std_ready, 1)

            def prepare(n, half, e):
                if e == 0:
                    squares(n)
                if e == 1:
                    deviation(n)
                if e == 3:
                    copy_y(n, half)
                if e == 5:
                    add_gate_bias(n)
                if e == 10:
                    gap_exponent(n)
                if e == 13:
                    round_gates(n, half)

            def step(n, half, kind):
                for e in range(E):
                    if kind != "tail":
                        relu(n, e)
                    if kind in ("first", "mid"):
                        prepare(n + 1, 1 - half, e)
                    if kind != "first":
                        if e == 1:
                            copy_moe(n - 1)
                        if e == 5:
                            f_squares(n - 1)
                        if e == 7:
                            f_deviation(n - 1)

            act.wait_ge(loaded, ALL_CONSTS)
            for e in range(E):
                prepare(0, 0, e)
            run_blocks(act, step)

        @block.vector
        def _(dve):
            def spread_rows(ap):
                return ap.rearrange("p (n a) -> p n a", a=1)

            def centre(n):
                at = ds(BT * n, BT)
                nc.vector.tensor_reduce(stat[:, 0, :], tokens[:, at, :], AX.X, ALU.add).then_inc(sum_ready, 1)
                dve.wait_ge(sum_ready, n + 1)
                nc.vector.tensor_scalar(stat[:, 1, :], stat[:, 0, :], 1.0 / C, None, ALU.mult).then_inc(mean_ready, 1)
                dve.wait_ge(mean_ready, n + 1)
                nc.vector.tensor_tensor(centred[:], tokens[:, at, :],
                                        spread_rows(stat[:, 1, :]).broadcast_to([P, BT, C]),
                                        ALU.subtract).then_inc(centred_ready, 1)

            def variance(n):
                dve.wait_ge(square_ready, n + 1)
                nc.vector.tensor_reduce(stat[:, 0, :], square[:], AX.X, ALU.add).then_inc(square_sum, 1)
                dve.wait_ge(square_sum, n + 1)
                nc.vector.tensor_scalar(stat[:, 2, :], stat[:, 0, :], 1.0 / C, LN_EPS, ALU.mult, ALU.add)\
                    .then_inc(var_ready, 1)

            def normalize(n, half):
                dve.wait_ge(std_ready, n + 1)
                nc.vector.reciprocal(stat[:, 1, :], stat[:, 3, :]).then_inc(rstd_ready, 1)
                dve.wait_ge(rstd_ready, n + 1)
                wait_above_zero(dve, y_turned, n)
                wait_above_zero(dve, y_kept_ready, n)
                nc.vector.tensor_tensor(
                    y[:], centred[:].rearrange("p n (a c) -> p n a c", a=1).broadcast_to([P, BT, 2, C]),
                    stat[:, 1, :].rearrange("p (n a c) -> p n a c", a=1, c=1).broadcast_to([P, BT, 2, C]),
                    ALU.mult).then_inc(y_ready, 1)

            def keep_y(n, half):
                dve.wait_ge(y_ready, n + 1)
                nc.vector.tensor_copy(y_kept[:, half], y[:, :, 0, :]).then_inc(y_kept_ready, 1)

            def low_y(n, half):
                dve.wait_ge(y_rounded, n + 1)
                nc.vector.tensor_tensor(y_both[C:P, half, :], prep_a[C:P, :], y_both[C:P, half, :].bitcast(F32),
                                        ALU.subtract).then_inc(y_both_ready, 1)

            def choose(n):
                dve.wait_ge(logits_turned, n + 1)
                in_bank = prep_a[:].rearrange("p (n e) -> p n e", n=BT)[:, :, 0:E]
                nc.vector.tensor_copy(logits[:], in_bank).then_inc(logits_ready, 1)
                for j in range(BT):
                    nc.vector.max(top[:, j, :], in_bank[:, j, :]).then_inc(top_ready, 1)
                dve.wait_ge(logits_ready, n + 1)
                dve.wait_ge(top_ready, BT * (n + 1))
                nc.vector.tensor_tensor(spread_rows(gap[:, 0, :]), top[:, :, 1:2], top[:, :, 0:1],
                                        ALU.subtract).then_inc(gap_ready, 1)
                for j in range(BT):
                    nc.vector.max_index(top_at[:, j, :], top[:, j, :], logits[:, j, :]).then_inc(top_at_ready, 1)

            def mark(n):
                dve.wait_ge(top_at_ready, BT * (n + 1))
                nc.vector.tensor_copy(at_f[:], top_at[:, :, 0:2]).then_inc(at_ready, 1)
                dve.wait_ge(at_ready, n + 1)
                for r in range(2):
                    nc.vector.tensor_tensor(is_top[:, r], places[:].rearrange("p (a e) -> p a e", a=1).broadcast_to([P, BT, E]),
                                            at_f[:, :, r:r + 1].broadcast_to([P, BT, E]), ALU.is_equal)\
                        .then_inc(is_top_ready, 1)

            def weigh(n):
                dve.wait_ge(gap_exp, n + 1)
                nc.vector.tensor_scalar(gap[:, 2, :], gap[:, 1, :], 1.0, None, ALU.add).then_inc(gap_sum, 1)
                dve.wait_ge(gap_sum, n + 1)
                nc.vector.reciprocal(gap[:, 3, :], gap[:, 2, :]).then_inc(first_ready, 1)
                dve.wait_ge(first_ready, n + 1)
                nc.vector.tensor_tensor(gap[:, 2, :], gap[:, 1, :], gap[:, 3, :], ALU.mult).then_inc(second_ready, 1)
                dve.wait_ge(second_ready, n + 1)
                dve.wait_ge(is_top_ready, 2 * (n + 1))
                for r in range(2):
                    nc.vector.tensor_tensor(is_top[:, r], is_top[:, r],
                                            spread_rows(gap[:, 3 - r, :]).broadcast_to([P, BT, E]), ALU.mult)\
                        .then_inc(weighed, 1)
                dve.wait_ge(weighed, 2 * (n + 1))
                nc.vector.tensor_tensor(gates[:, :, 0:2, 0:E],
                                        is_top[:, 0].rearrange("p n (a e) -> p n a e", a=1).broadcast_to([P, BT, 2, E]),
                                        is_top[:, 1].rearrange("p n (a e) -> p n a e", a=1).broadcast_to([P, BT, 2, E]),
                                        ALU.add).then_inc(gates_ready, 1)

            def low_gates(n, half):
                dve.wait_ge(gates_rounded, n + 1)
                nc.vector.tensor_tensor(gates_t[LO:2 * LO, half, :], prep_b[LO:2 * LO, :],
                                        gates_t[LO:2 * LO, half, :].bitcast(F32), ALU.subtract).then_inc(gates_t_ready, 1)

            def gate(n, e):
                dve.wait_ge(hidden_ready, E * n + e + 1)
                dve.wait_ge(gate_spread, E * n + e + 1)
                wait_above_zero(dve, moe_step, E * n + e - 1)
                nc.vector.tensor_tensor(gated[:, e % 2, :], gate_ps[e % 2][:], hidden[:, e % 2, :],
                                        ALU.mult).then_inc(gated_ready, 1)

            def f_centre(n, half):
                dve.wait_ge(moe_turned, n + 1)
                nc.vector.tensor_tensor(total[:], back_ps[:].rearrange("p (n c) -> p n c", n=BT)[:, :, 0:C],
                                        y_kept[:, half], ALU.add).then_inc(total_ready, 1)
                dve.wait_ge(total_ready, n + 1)
                nc.vector.tensor_reduce(f_stat[:, 0, :], total[:], AX.X, ALU.add).then_inc(f_sum_ready, 1)
                dve.wait_ge(f_sum_ready, n + 1)
                nc.vector.tensor_scalar(f_stat[:, 1, :], f_stat[:, 0, :], 1.0 / C, None, ALU.mult).then_inc(f_mean_ready, 1)
                dve.wait_ge(f_mean_ready, n + 1)
                nc.vector.tensor_tensor(f_centred[:], total[:], spread_rows(f_stat[:, 1, :]).broadcast_to([P, BT, C]),
                                        ALU.subtract).then_inc(f_centred_ready, 1)

            def f_variance(n):
                dve.wait_ge(f_square_ready, n + 1)
                nc.vector.tensor_reduce(f_stat[:, 0, :], f_square[:], AX.X, ALU.add).then_inc(f_square_sum, 1)
                dve.wait_ge(f_square_sum, n + 1)
                nc.vector.tensor_scalar(f_stat[:, 2, :], f_stat[:, 0, :], 1.0 / C, LN_EPS, ALU.mult, ALU.add)\
                    .then_inc(f_var_ready, 1)

            def f_normalize(n):
                dve.wait_ge(f_std_ready, n + 1)
                nc.vector.reciprocal(f_stat[:, 1, :], f_stat[:, 3, :]).then_inc(f_rstd_ready, 1)
                dve.wait_ge(f_rstd_ready, n + 1)
                wait_above_zero(dve, f_scaled_ready, n)
                nc.vector.tensor_tensor(f_norm[:], f_centred[:], spread_rows(f_stat[:, 1, :]).broadcast_to([P, BT, C]),
                                        ALU.mult).then_inc(f_norm_ready, 1)

            def prepare(n, half, e):
                if e == 0:
                    centre(n)
                if e == 1:
                    variance(n)
                if e == 2:
                    normalize(n, half)
                if e == 4:
                    low_y(n, half)
                if e == 5:
                    keep_y(n, half)
                if e == 7:
                    choose(n)
                if e == 9:
                    mark(n)
                if e == 11:
                    weigh(n)
                if e == 14:
                    low_gates(n, half)

            def step(n, half, kind):
                for e in range(E):
                    if kind != "tail":
                        gate(n, e)
                    if kind in ("first", "mid"):
                        prepare(n + 1, 1 - half, e)
                    if kind != "first":
                        if e == 4:
                            f_centre(n - 1, 1 - half)
                        if e == 6:
                            f_variance(n - 1)
                        if e == 8:
                            f_normalize(n - 1)

            nc.vector.memset(gates[:], 0.0).then_inc(filled, 1)
            nc.vector.memset(gates_t[:].bitcast(F32), 0.0).then_inc(filled, 1)
            dve.wait_ge(loaded, ALL_CONSTS)
            dve.wait_ge(filled, 2)
            nc.vector.tensor_copy(w1_hi[:], w1_s[:]).then_inc(rounded, 1)
            nc.vector.tensor_copy(b2_hi[:], b2_s[:]).then_inc(rounded, 1)
            nc.vector.tensor_copy(sel_r[:], sel_s[:]).then_inc(weights_ready, 1)
            dve.wait_ge(rounded, 2)
            nc.vector.tensor_tensor(w1_lo[:], w1_s[:], w1_hi[:].bitcast(F32), ALU.subtract).then_inc(weights_ready, 1)
            nc.vector.tensor_tensor(b2_lo[:], b2_s[:], b2_hi[:].bitcast(F32), ALU.subtract).then_inc(weights_ready, 1)
            for e in range(E):
                prepare(0, 0, e)
            run_blocks(dve, step)

        @block.gpsimd
        def _(pool):
            def finish(n, half, nth):
                pool.wait_ge(f_norm_ready, n + 1)
                wait_above_zero(pool, result_ready, n)
                gamma = rows_s[:, 0:1, :].broadcast_to([P, BT, C])
                beta = rows_s[:, 1:2, :].broadcast_to([P, BT, C])
                nc.gpsimd.tensor_tensor(f_scaled[:], f_norm[:], gamma, ALU.mult).then_inc(f_scaled_ready, 1)
                nc.gpsimd.tensor_tensor(f_shift[:], tokens[:, ds(BT * n, BT), :], beta, ALU.add).then_inc(f_shift_ready, 1)
                pool.wait_ge(f_scaled_ready, n + 1)
                pool.wait_ge(f_shift_ready, n + 1)
                wait_above_zero(pool, stored[half], 16 * nth)
                nc.gpsimd.tensor_tensor(result[:, half], f_scaled[:], f_shift[:], ALU.add).then_inc(result_ready, 1)

            pool.wait_ge(loaded, ALL_CONSTS)
            with pool.Fori(0, NBLOCK // 2) as i:
                finish(2 * i, 0, i)
                finish(2 * i + 1, 1, i)
            finish(NBLOCK - 1, 0, NBLOCK // 2)


def expert_layout(gate_w, gate_b, w1, b1, w2, b2, gamma, beta):
    f = np.float32
    gw = np.zeros((P, P), f)
    gw[0:C, 0:E] = gate_w
    gb = np.zeros((P, 1), f)
    gb[0:E, 0] = gate_b
    w1t = w1.transpose(1, 0, 2).reshape(C, E * F)
    sel = np.zeros((P, E, P), f)
    b2x = np.zeros((P, C), f)
    for e in range(E):
        sel[e, e] = sel[LO + e, e] = 1.0
    b2x[0:E] = b2
    b2x[LO:LO + E] = b2
    rows = np.concatenate([gamma, beta, np.arange(E, dtype=f)])
    return dict(gate_w=gw, w1=np.concatenate([w1t, w1t]), w2=np.tile(w2.transpose(1, 0, 2)[:, :, None], (1, 1, 2, 1)).reshape(F, 2 * E * C),
                sel=sel.reshape(P, E * P), b2=np.tile(b2x, (1, 2)), b1=np.ascontiguousarray(b1.T), gate_b=gb,
                rows=np.tile(rows, (P, 1)))


def fused_layer(nc, xw, txt, wqk, wv, wp, cols, trig, hmask, vmask, omask, ident, w2x, fold,
                gate_w, w1, w2, sel, b2, b1, gate_b, rows, out):
    with nc.sbuf_tensor("tokens", [P, NPAIR + B, C], F32) as tokens:
        window_attention(nc, xw, txt, wqk, wv, wp, cols, trig, hmask, vmask, omask, ident, tokens)
        full_attention(nc, w2x, ident, fold, tokens)
        experts(nc, gate_w, w1, w2, sel, b2, b1, gate_b, rows, ident, tokens, out)


def kernel(x, txt, L0_tok_qkv_w, L0_tok_qkv_b, L0_tok_proj_w, L0_tok_proj_b, L0_attn_W, L0_ffn_gate_w,
           L0_ffn_gate_b, L0_ffn_w1, L0_ffn_b1, L0_ffn_w2, L0_ffn_b2, L0_ffn_gamma, L0_ffn_beta):
    import concourse.bacc as bacc
    from concourse.bass_utils import run_bass_kernel_spmd

    a = [np.asarray(v) for v in (x, L0_tok_qkv_w, L0_tok_qkv_b, L0_tok_proj_w, L0_tok_proj_b)]
    laid = window_layout(*a)
    laid["txt"] = np.asarray(txt)
    laid["w2x"], laid["fold"] = attention_layout(np.asarray(L0_attn_W))
    laid.update(expert_layout(*[np.asarray(v) for v in (
        L0_ffn_gate_w, L0_ffn_gate_b, L0_ffn_w1, L0_ffn_b1, L0_ffn_w2, L0_ffn_b2, L0_ffn_gamma, L0_ffn_beta)]))
    order = ["xw", "txt", "wqk", "wv", "wp", "cols", "trig", "hmask", "vmask", "omask", "ident", "w2x", "fold",
             "gate_w", "w1", "w2", "sel", "b2", "b1", "gate_b", "rows"]

    nc = bacc.Bacc("TRN2", target_bir_lowering=False, num_devices=1)
    arrays, args = {}, []
    for name in order:
        v = np.ascontiguousarray(laid[name])
        arrays[f"in_{name}_dram"] = v
        args.append(nc.dram_tensor(f"in_{name}_dram", v.shape, mybir.dt.from_np(v.dtype), kind="ExternalInput").ap())
    args.append(nc.dram_tensor("out_0_dram", (NPAIR + B, P, C), F32, kind="ExternalOutput").ap())
    fused_layer(nc, *args)
    got = run_bass_kernel_spmd(nc, [arrays], core_ids=[0]).results[0]["out_0_dram"]

    nw = SIDE // WIN
    img = got[:NPAIR].reshape(B, nw, nw // 2, 2, WIN, WIN, C).transpose(0, 1, 4, 2, 3, 5, 6)
    return np.concatenate([img.reshape(B, SIDE * SIDE, C), got[NPAIR:]], axis=1)
```

```python
from contextlib import ExitStack

import numpy as np
import concourse.bass as bass
from concourse import mybir

F32 = mybir.dt.float32
F32R = mybir.dt.float32r
ALU = mybir.AluOpType
ACT = mybir.ActivationFunctionType
AX = mybir.AxisListType
ds = bass.ds

P = 128
B, SIDE, C = 4, 64, 64
WIN = 8
NH, HD = 8, 8
WTOK = WIN * WIN
NPAIR = B * (SIDE // WIN) ** 2 // 2
QUAD = 4
NQUAD = NPAIR // QUAD
PER = 2 * QUAD
TXT = 128
HEAD_SCALE = HD ** -0.5


def wait_above_zero(eng, sem, count):
    if not isinstance(count, int) or count > 0:
        eng.wait_ge(sem, count)


HELD = 4
TURN_LAG, VALUE_LAG = 3, 4


def run_turns(eng, turn):
    turns = NPAIR // PER
    turn(0, "first")
    turn(1, "mid")
    with eng.Fori(2, turns - 1) as i:
        turn(i, "mid")
    turn(turns - 1, "last")
    turn(turns, "tail")


def runs(kind, k, lag):
    return k >= lag if kind == "first" else k < lag if kind == "tail" else True


def window_attention(nc, xw, txt, wqk, wv, wp, cols, trig, hmask, ident, tokens):
    with ExitStack() as ctx:
        def sb(name, shape, dt=F32):
            return ctx.enter_context(nc.sbuf_tensor(name, shape, dt))

        def ps(name, shape):
            return ctx.enter_context(nc.psum_tensor(name, shape, F32))

        def sem(name):
            return ctx.enter_context(nc.semaphore(name))

        wqk_s = sb("wqk_s", [P, 4, P])
        wv_s = sb("wv_s", [P, P])
        wp_s = sb("wp_s", [P, P])
        cols_s = sb("cols_s", [P, 12])
        trig_s = sb("trig_s", [P, 2, WTOK])
        hmask_s = sb("hmask_s", [P, NH])
        ident_s = sb("ident_s", [P, P])
        x_s = sb("x_s", [P, 2, QUAD, 2, WTOK])
        turned = sb("turned", [P, 4, QUAD * WTOK])
        k_rot = sb("k_rot", [P, 2, QUAD, WTOK])
        q_diag = sb("q_diag", [P, 2, QUAD, P])
        k_heads = sb("k_heads", [P, 2, QUAD, NH, WTOK])
        v_heads = sb("v_heads", [P, 2, QUAD, P])
        s_max = sb("s_max", [P, HELD, NH])
        s_low = sb("s_low", [P, HELD, NH, WTOK])
        probs = sb("probs", [P, HELD, NH, WTOK])
        p_sum = sb("p_sum", [P, HELD, NH])
        p_inv = sb("p_inv", [P, HELD, NH])
        p_norm = sb("p_norm", [P, HELD, NH, WTOK])
        p_turn = sb("p_turn", [P, 2, 4, P])
        o_own = sb("o_own", [P, QUAD, P])
        h_cols = sb("h_cols", [P, QUAD, P])

        proj_a = ps("proj_a", [P, 2, QUAD * WTOK])
        proj_b = ps("proj_b", [P, 2, QUAD * WTOK])
        scores = [ps(f"scores{i}", [P, NH, WTOK]) for i in range(2)]
        p_t = [ps(f"p_t{i}", [P, 4, P]) for i in range(2)]
        o_t = ps("o_t", [P, QUAD, P])
        h_t = ps("h_t", [P, QUAD, P])
        v_ps = proj_a[:].rearrange("p a b -> p (a b)").rearrange("p (q c) -> p q c", q=QUAD)
        rows_ps = proj_b[:].rearrange("p a b -> p (a b)").rearrange("p (q c) -> p q c", q=QUAD)

        consts_loaded = sem("consts_loaded")
        x_loaded = [sem(f"x_loaded{half}") for half in range(2)]
        text_loaded = sem("text_loaded")
        diag_zero = sem("diag_zero")
        qk_projected = sem("qk_projected")
        v_projected = sem("v_projected")
        turned_ready = sem("turned_ready")
        rotated = sem("rotated")
        k_ready = sem("k_ready")
        v_ready = sem("v_ready")
        scores_ready = sem("scores_ready")
        max_ready = sem("max_ready")
        low_ready = sem("low_ready")
        probs_ready = sem("probs_ready")
        sum_ready = sem("sum_ready")
        inv_ready = sem("inv_ready")
        norm_ready = sem("norm_ready")
        pt_ready = sem("pt_ready")
        pt_copied = sem("pt_copied")
        pv_ready = sem("pv_ready")
        o_ready = sem("o_ready")
        h_ready = sem("h_ready")
        h_copied = sem("h_copied")
        rows_ready = sem("rows_ready")
        rows_copied = sem("rows_copied")

        consts = [(wqk_s[:].rearrange("p a b -> p (a b)"), wqk), (wv_s[:], wv), (wp_s[:], wp), (cols_s[:], cols),
                  (trig_s[:].rearrange("p a b -> p (a b)"), trig), (hmask_s[:], hmask), (ident_s[:], ident)]
        ALL_CONSTS = 16 * len(consts)

        block = ctx.enter_context(nc.Block())

        @block.sync
        def _(sp):
            def load_x(u, half):
                for copy in range(2):
                    sp.dma_start(x_s[:, half, :, copy, :],
                                 xw[ds(u, 1)].rearrange("a p (q t) -> (a p) q t", q=QUAD)).then_inc(x_loaded[half], 16)

            load_x(0, 0)
            for dst, src in consts:
                sp.dma_start(dst, src).then_inc(consts_loaded, 16)
            load_x(1, 1)
            sp.dma_start(tokens[:, NPAIR:NPAIR + B, :], txt.rearrange("b p c -> p b c")).then_inc(text_loaded, 16)

            def refill(i):
                sp.wait_ge(v_projected, 2 * i + 1)
                load_x(2 * i + 2, 0)
                sp.wait_ge(v_projected, 2 * i + 2)
                load_x(2 * i + 3, 1)

            with sp.Fori(0, NQUAD // 2 - 1) as i:
                refill(i)
            sp.wait_ge(text_loaded, 16)

        @block.tensor
        def _(pe):
            def project_qk(u, half, nth):
                pe.wait_ge(x_loaded[half], 32 * nth + 32)
                wait_above_zero(pe, v_ready, u)
                wait_above_zero(pe, rows_copied, u - 3)
                for m in range(4):
                    bank = proj_a if m < 2 else proj_b
                    last = nc.tensor.matmul(bank[:, m % 2, :], wqk_s[:, m, :],
                                            x_s[:, half, :, 0, :], start=True, stop=True)
                last.then_inc(qk_projected, 1)

            def project_v(u, half):
                pe.wait_ge(turned_ready, 4 * u + 4)
                for p in range(QUAD):
                    last = nc.tensor.matmul(v_ps[:, p, :], x_s[:, half, p].rearrange("p a t -> p (a t)"), wv_s[:],
                                            start=True, stop=True)
                last.then_inc(v_projected, 1)

            def score(n, k):
                pe.wait_ge(k_ready, n + 1)
                pe.wait_ge(rotated, 3 * ((n - k) // QUAD + k // QUAD) + 3)
                wait_above_zero(pe, low_ready, n - 1)
                half, p = k // QUAD, k % QUAD
                nc.tensor.matmul(scores[k % 2][:].rearrange("p h t -> p (h t)"), q_diag[:, half, p, :],
                                 k_heads[:, half, p].rearrange("p h t -> p (h t)"),
                                 start=True, stop=True).then_inc(scores_ready, 1)

            def turn_probs(n, k):
                pe.wait_ge(norm_ready, n + 1)
                wait_above_zero(pe, pt_copied, n - 1)
                for j in range(4):
                    last = nc.tensor.transpose(p_t[k % 2][:, j, :],
                                               p_norm[:, k % HELD, 2 * j:2 * j + 2, :].rearrange("p h t -> p (h t)"),
                                               ident_s[:])
                last.then_inc(pt_ready, 1)

            def values(n, k, u):
                pe.wait_ge(pt_copied, n + 1)
                half, p = k // QUAD, k % QUAD
                if p == 0:
                    pe.wait_ge(v_ready, u + 1)
                    wait_above_zero(pe, o_ready, u)
                for j in range(4):
                    last = nc.tensor.matmul(o_t[32 * j:32 * j + 32, p, :], v_heads[:, half, p, 32 * j:32 * j + 32],
                                            p_turn[:, k % 2, j, :], start=True, stop=True)
                last.then_inc(pv_ready, 1)

            def project_out(u):
                pe.wait_ge(o_ready, u + 1)
                wait_above_zero(pe, h_copied, u)
                nc.tensor.matmul(h_t[:].rearrange("p q t -> p (q t)"), wp_s[:],
                                 o_own[:].rearrange("p q t -> p (q t)"), start=True, stop=True).then_inc(h_ready, 1)

            def to_rows(u, k, kind):
                pe.wait_ge(h_copied, u + 1)
                if kind in ("first", "mid") or kind == "last" and k == 2:
                    pe.wait_ge(turned_ready, 4 * (u + 3) + 4)
                wait_above_zero(pe, rows_copied, u)
                for p in range(QUAD):
                    last = nc.tensor.transpose(rows_ps[:, p, :], h_cols[:, p, :], ident_s[:])
                last.then_inc(rows_ready, 1)

            def turn(i, kind):
                for k in range(PER):
                    n = i * PER + k
                    if kind != "tail":
                        score(n, k)
                    if k == 0 and kind != "tail":
                        project_qk(2 * i + 1, 1, i)
                    if k == QUAD and kind in ("first", "mid"):
                        project_qk(2 * i + 2, 0, i + 1)
                    if runs(kind, k, TURN_LAG):
                        turn_probs(n - TURN_LAG, (k - TURN_LAG) % PER)
                    if runs(kind, k, VALUE_LAG):
                        values(n - VALUE_LAG, (k - VALUE_LAG) % PER, 2 * i + (k - VALUE_LAG) // QUAD)
                    if k == 3 and kind != "tail":
                        project_v(2 * i + 1, 1)
                    if k == 7 and kind in ("first", "mid"):
                        project_v(2 * i + 2, 0)
                    if kind != "first" and k in (1, 5):
                        project_out(2 * i - 2 + k // 4)
                    if kind != "first" and k in (2, 6):
                        to_rows(2 * i - 2 + k // 4, k, kind)

            pe.wait_ge(consts_loaded, ALL_CONSTS)
            project_qk(0, 0, 0)
            project_v(0, 0)
            run_turns(pe, turn)

        @block.vector
        def _(dve):
            def rotate(u, half):
                dve.wait_ge(qk_projected, u + 1)
                wait_above_zero(dve, rotated, 3 * u)
                for m in range(4):
                    bank = proj_a if m < 2 else proj_b
                    nc.vector.scalar_tensor_tensor(
                        out=turned[:, m, :].rearrange("p (q t) -> p q t", q=QUAD),
                        in0=bank[:, m % 2, :].rearrange("p (q t) -> p q t", q=QUAD),
                        scalar=cols_s[:, m:m + 1],
                        in1=trig_s[:, m % 2:m % 2 + 1, :].broadcast_to([P, QUAD, WTOK]),
                        op0=ALU.add, op1=ALU.mult).then_inc(turned_ready, 1)
                dve.wait_ge(turned_ready, 4 * u + 4)
                wait_above_zero(dve, scores_ready, QUAD * (u - 1))
                wait_above_zero(dve, k_ready, QUAD * (u - 1))
                q1 = turned[:, 0, :].rearrange("p (q t) -> p q t", q=QUAD)
                q2 = turned[:, 1, :].rearrange("p (q t) -> p q t", q=QUAD)
                for w in range(2):
                    r = slice(64 * w, 64 * w + 64)
                    nc.vector.tensor_tensor(q_diag[r, half, :, r], q1[r], q2[r], ALU.add).then_inc(rotated, 1)
                nc.vector.tensor_tensor(k_rot[:, half].rearrange("p q t -> p (q t)"), turned[:, 2, :],
                                        turned[:, 3, :], ALU.add).then_inc(rotated, 1)

            def lower(n, k):
                dve.wait_ge(scores_ready, n + 1)
                wait_above_zero(dve, low_ready, n - 1)
                nc.vector.tensor_reduce(s_max[:, k % HELD, :], scores[k % 2][:], AX.X, ALU.max).then_inc(max_ready, 1)
                dve.wait_ge(max_ready, n + 1)
                wait_above_zero(dve, probs_ready, n + 1 - HELD)
                nc.vector.tensor_tensor(s_low[:, k % HELD], scores[k % 2][:],
                                        s_max[:, k % HELD, :].rearrange("p (h a) -> p h a", a=1).broadcast_to([P, NH, WTOK]),
                                        ALU.subtract).then_inc(low_ready, 1)

            def invert(n, k):
                dve.wait_ge(probs_ready, n + 1)
                wait_above_zero(dve, inv_ready, n - 1)
                nc.vector.tensor_reduce(p_sum[:, k % HELD, :], probs[:, k % HELD], AX.X, ALU.add).then_inc(sum_ready, 1)
                dve.wait_ge(sum_ready, n + 1)
                wait_above_zero(dve, norm_ready, n - 1)
                nc.vector.reciprocal(p_inv[:, k % HELD, :], p_sum[:, k % HELD, :]).then_inc(inv_ready, 1)

            def turn(i, kind):
                for k in range(PER):
                    n = i * PER + k
                    if kind != "tail":
                        lower(n, k)
                    if runs(kind, k, 1):
                        invert(n - 1, (k - 1) % PER)
                    if k == 0 and kind != "tail":
                        rotate(2 * i + 1, 1)
                    if k == QUAD and kind in ("first", "mid"):
                        rotate(2 * i + 2, 0)

            nc.vector.memset(q_diag[:], 0.0).then_inc(diag_zero, 1)
            dve.wait_ge(diag_zero, 1)
            dve.wait_ge(consts_loaded, ALL_CONSTS)
            rotate(0, 0)
            run_turns(dve, turn)

        @block.gpsimd
        def _(pool):
            def split_heads(n, k, u):
                half, p = k // QUAD, k % QUAD
                if p == 0:
                    pool.wait_ge(rotated, 3 * u + 3)
                wait_above_zero(pool, scores_ready, n - PER + 1)
                nc.gpsimd.tensor_tensor(k_heads[:, half, p], k_rot[:, half, p:p + 1, :].broadcast_to([P, NH, WTOK]),
                                        hmask_s[:].rearrange("p (h a) -> p h a", a=1).broadcast_to([P, NH, WTOK]),
                                        ALU.mult).then_inc(k_ready, 1)

            def normalize(n, k):
                pool.wait_ge(inv_ready, n + 1)
                wait_above_zero(pool, pt_ready, n + 1 - HELD)
                nc.gpsimd.tensor_tensor(p_norm[:, k % HELD], probs[:, k % HELD],
                                        p_inv[:, k % HELD, :].rearrange("p (h a) -> p h a", a=1).broadcast_to([P, NH, WTOK]),
                                        ALU.mult).then_inc(norm_ready, 1)

            def turn(i, kind):
                for k in range(PER):
                    n = i * PER + k
                    if kind != "tail":
                        if not (kind == "last" and k >= PER - 2):
                            split_heads(n + 2, (k + 2) % PER, 2 * i + (k + 2) // QUAD)
                    if runs(kind, k, 1):
                        normalize(n - 1, (k - 1) % PER)

            pool.wait_ge(consts_loaded, ALL_CONSTS)
            for k in range(2):
                split_heads(k, k, 0)
            run_turns(pool, turn)

        @block.scalar
        def _(act):
            def exponent(n, k):
                act.wait_ge(low_ready, n + 1)
                wait_above_zero(act, norm_ready, n + 1 - HELD)
                nc.scalar.activation(probs[:, k % HELD], s_low[:, k % HELD], ACT.Exp, scale=HEAD_SCALE).then_inc(probs_ready, 1)

            def copy_turned(n, k):
                act.wait_ge(pt_ready, n + 1)
                wait_above_zero(act, pv_ready, n - 1)
                nc.scalar.copy(p_turn[:, k % 2], p_t[k % 2][:]).then_inc(pt_copied, 1)

            def mask_v(u, half):
                act.wait_ge(v_projected, u + 1)
                wait_above_zero(act, pv_ready, QUAD * (u - 1))
                for w in range(2):
                    out = v_heads[:, half].rearrange("p q (g a d) -> p (q g) a d", a=2, d=HD)
                    own = v_ps.rearrange("p q (g a d) -> p (q g) a d", a=2, d=HD)
                    last = nc.scalar.activation(out[:, :, w, :], own[:, :, w, :], ACT.Copy, scale=cols_s[:, 9 + w:10 + w])
                last.then_inc(v_ready, 1)

            def own_window(u):
                act.wait_ge(pv_ready, QUAD * (u + 1))
                wait_above_zero(act, h_ready, u)
                for w in range(2):
                    t = slice(WTOK * w, WTOK * w + WTOK)
                    last = nc.scalar.activation(o_own[:, :, t], o_t[:, :, t], ACT.Identity, bias=cols_s[:, 4 + 2 * w:5 + 2 * w],
                                                scale=cols_s[:, 7 + w:8 + w])
                last.then_inc(o_ready, 1)

            def keep_rows(u):
                act.wait_ge(rows_ready, u + 1)
                nc.scalar.copy(tokens[:, ds(QUAD * u, QUAD), :], rows_ps[:, :, 0:C]).then_inc(rows_copied, 1)

            def add_bias(u):
                act.wait_ge(h_ready, u + 1)
                wait_above_zero(act, rows_ready, u)
                nc.scalar.activation(h_cols[:], h_t[:], ACT.Identity, bias=cols_s[:, 5:6]).then_inc(h_copied, 1)

            def turn(i, kind):
                for k in range(PER):
                    n = i * PER + k
                    if kind != "first" and k in (0, 4):
                        own_window(2 * i - 2 + k // 4)
                    if kind != "first" and k in (3, 7):
                        keep_rows(2 * i - 2 + k // 4)
                    if kind != "tail":
                        exponent(n, k)
                    if runs(kind, k, TURN_LAG):
                        copy_turned(n - TURN_LAG, (k - TURN_LAG) % PER)
                    if kind != "first" and k in (1, 5):
                        add_bias(2 * i - 2 + k // 4)
                    if k == 3 and kind != "tail":
                        mask_v(2 * i + 1, 1)
                    if k == 7 and kind in ("first", "mid"):
                        mask_v(2 * i + 2, 0)

            act.wait_ge(consts_loaded, ALL_CONSTS)
            mask_v(0, 0)
            run_turns(act, turn)


def window_layout(x, qkv_w, qkv_b, proj_w, proj_b):
    f = np.float32
    nw = SIDE // WIN
    xw = x.reshape(B, nw, WIN, nw // 2, 2, WIN, C)
    xw = xw.transpose(0, 1, 3, 4, 6, 2, 5).reshape(NQUAD, QUAD, 2, C, WTOK)
    xw = xw.transpose(0, 2, 3, 1, 4).reshape(NQUAD, P, QUAD * WTOK)
    swap = np.arange(C) ^ 1
    wq, wk, wv = qkv_w[0:C], qkv_w[C:2 * C], qkv_w[2 * C:3 * C]
    bq, bk, bv = qkv_b[0:C], qkv_b[C:2 * C], qkv_b[2 * C:3 * C]
    wqk = np.zeros((P, 4, P), f)
    for m, w in enumerate((wq, wq[swap], wk, wk[swap])):
        for s in (slice(0, 64), slice(64, 128)):
            wqk[s, m, s] = w.T
    wvx = np.zeros((2, C, 4, 2, 16), f)
    for w in range(2):
        wvx[w, :, :, w, :] = wv.T.reshape(C, 4, 16)
    wpx = np.zeros((4, 2, 16, C), f)
    for w in range(2):
        wpx[:, w] = proj_w.T.reshape(4, 16, C)
    cols = np.zeros((P, 12), f)
    for m, b in enumerate((bq, bq[swap], bk, bk[swap])):
        cols[:, m] = np.concatenate([b, b])
    bvx = np.zeros((4, 2, 16), f)
    for w in range(2):
        bvx[:, w] = bv.reshape(4, 16)
    rows = np.arange(P)
    for w in range(2):
        own = (rows % 32) // 16 == w
        cols[own, 4 + 2 * w] = bvx.reshape(P)[own]
        cols[own, 7 + w] = 1.0
        cols[rows // 64 == w, 9 + w] = 1.0
    cols[:, 5] = np.concatenate([proj_b, proj_b])
    half = HD // 2
    freq = (1.0 / 10000.0 ** (np.arange(0, half, 2, dtype=f) / f(half))).astype(f)
    cos, sin = np.zeros((C, WIN, WIN), f), np.zeros((C, WIN, WIN), f)
    for c in range(C):
        d = c % HD
        ang = np.arange(WIN, dtype=f) * freq[(d % half) // 2]
        ang = ang[:, None] + np.zeros((1, WIN), f) if d < half else ang[None, :] + np.zeros((WIN, 1), f)
        cos[c] = np.cos(ang)
        sin[c] = np.sin(ang) if d % 2 else -np.sin(ang)
    trig = np.stack([cos.reshape(C, WTOK), sin.reshape(C, WTOK)], 1)
    trig = np.concatenate([trig, trig]).reshape(P, 2 * WTOK)
    hmask = (((rows % C) // HD)[:, None] == np.arange(NH)[None, :]).astype(f)
    return dict(xw=xw, wqk=wqk.reshape(P, 4 * P), wv=wvx.reshape(P, P), wp=np.tile(wpx.reshape(P, C), (1, 2)), cols=cols, trig=trig,
                hmask=hmask, ident=np.eye(P, dtype=f))


TT = 384
CH = TT // P
NT = (SIDE * SIDE + TXT) // P
TILES = NT // CH
KEYS = NT * P
GROUPS = [2, 2, 1] * 4 + [2] * 5 + [1] * 3
NG = len(GROUPS)
FIRST = [sum(GROUPS[:g]) for g in range(NG)]
LAG = 3
RING = 4
assert NG % RING == 0
NMAX = CH * TILES
NPAIRS = (NMAX + 1) // 2
MAX_PER = [2, 2, 1] * 4 + [3, 3, 3, 2, 2] + [0] * 3
MAX_FROM = [sum(MAX_PER[:g]) for g in range(NG)]
DVE_HIGH = [2, 8, 11, 17, 18, 19]
ACT_HIGH = [g for g in range(NG) if g not in DVE_HIGH]
DVE_LOW = 1 / 5
OUT_AT = 4
Q_AT = 8
KEY_AT = 12
SHIFT_AT, SHIFT_OUT = 17, 18
CENTRE_AT, SQUARE_AT, VAR_AT, POW_AT, NODES_AT = 5, 6, 7, 8, 9
AHEAD = 2
SLOTS = 3
LN_EPS = 1e-5
NORM = C ** -0.5


def full_attention(nc, w2x, ident, fold, tokens):
    with ExitStack() as ctx:
        def sb(name, shape, dt=F32):
            return ctx.enter_context(nc.sbuf_tensor(name, shape, dt))

        def ps(name, shape):
            return ctx.enter_context(nc.psum_tensor(name, shape, F32))

        def sem(name):
            return ctx.enter_context(nc.semaphore(name))

        w2x_s = sb("w2x_s", [P, P])
        ident_b = sb("ident_b", [P, P])
        fold_s = sb("fold_s", [P, C + 1])
        half_s = sb("half_s", [P, CH])
        stat = sb("stat", [P, SLOTS, 4, CH])
        centred = sb("centred", [P, SLOTS, CH, C])
        square = sb("square_b", [P, SLOTS, CH, C])
        nodes2 = sb("nodes2", [P, CH, 2, C])
        nodes = sb("nodes", [P, NT, C])
        values_s = sb("values_s", [P, NT, 2 * C], F32R)
        residue = sb("residue", [P, NT])
        keys_t = sb("keys_t", [P, KEYS])
        k_hi = sb("k_hi", [P, KEYS], F32R)
        k_lo = sb("k_lo", [P, KEYS], F32R)
        q_both = sb("q_both", [P, KEYS], F32R)
        q_hi = sb("q_hi", [P, KEYS], F32R)
        q_own = sb("q_own", [P, TT], F32R)
        cmax = sb("cmax", [P, NMAX])
        neg_max = sb("neg_max", [P, CH, C + 1])
        probs = sb("probs_b", [P, RING, 2 * TT])
        p_hi = sb("p_hi", [P, RING, 2 * TT], F32R)
        p_lo = sb("p_lo", [P, RING, 2 * TT], F32R)
        out_cols = sb("out_cols", [P, TT])
        sum_inv = sb("sum_inv", [P, CH, 1])

        s_ps = [ps(f"s_ps{i}", [P, 2, 512]) for i in range(2)]
        max_ps = [ps(f"max_ps{i}", [P, 512]) for i in range(2)]
        o_ps = ps("o_ps", [P, 512])
        turn_ps = ps("turn_ps", [P, 512])

        loaded = sem("b_loaded")
        filled = sem("filled")
        half_ready = sem("half_ready")
        sum_ready = sem("b_sum_ready")
        mean_ready = sem("mean_ready")
        centred_ready = sem("centred_ready")
        square_ready = sem("square_ready")
        square_sum = sem("b_square_sum")
        var_ready = sem("var_ready")
        rstd_ready = sem("rstd_ready")
        nodes_ready = sem("nodes_ready")
        nodes_kept = sem("nodes_kept")
        residue_ready = sem("residue_ready")
        v_high = sem("v_high")
        values_ready = sem("values_ready")
        keys_turned = sem("keys_turned")
        keys_copied = sem("keys_copied")
        k_hi_ready = sem("k_hi_ready")
        k_lo_ready = sem("k_lo_ready")
        q_made = sem("q_made")
        q_rounded = sem("q_rounded")
        q_hi_ready = sem("q_hi_ready")
        q_both_ready = sem("q_both_ready")
        own_ready = sem("own_ready")
        start_made = sem("start_made")
        start_read = sem("start_read")
        max_made = sem("max_made")
        max_read = sem("max_read")
        neg_ready = sem("neg_ready")
        shift_turned = sem("shift_turned")
        shift_ready = sem("shift_ready")
        s_ready = sem("s_ready")
        p_ready = sem("p_ready")
        act_high = sem("act_high")
        dve_high = sem("dve_high")
        dve_low = sem("dve_low")
        pool_low = sem("pool_low")
        pv_done = sem("pv_done")
        out_copied = sem("out_copied")
        out_turned = sem("out_turned")
        inv_ready = sem("b_inv_ready")
        out_added = sem("out_added")

        block = ctx.enter_context(nc.Block())

        MAXIMA = NMAX * (TILES - 1)

        def turns(eng, b, turn):
            turn(b, 0, "first")
            start = 1
            if isinstance(b, int) and b == 0:
                turn(b, 1, "mid")
                start = 2
            with eng.Fori(start, TILES - 2) as t:
                turn(b, t, "mid")
            turn(b, TILES - 2, "late")
            turn(b, TILES - 1, "last")
            turn(b, TILES, "tail")

        def batches(eng, body):
            body(0, True)
            with eng.Fori(1, B - 1) as b:
                body(b, True)
            body(B - 1, False)

        def high_ready(eng, b, t, g):
            own, done = (DVE_HIGH, dve_high) if g in DVE_HIGH else (ACT_HIGH, act_high)
            eng.wait_ge(done, len(own) * (TILES * b + t) + own.index(g) + 1)

        def has_maxima(kind):
            return kind in ("first", "mid", "late")

        def makes_queries(kind, ahead):
            return kind in ("first", "mid") or (ahead and kind in ("late", "last"))

        def ahead_cols(kind, t):
            at = {"late": 0, "last": TT}.get(kind)
            return ds((t + AHEAD) * TT, TT) if at is None else slice(at, at + TT)

        @block.sync
        def _(sp):
            sp.dma_start(w2x_s[:], w2x).then_inc(loaded, 16)
            sp.dma_start(ident_b[:], ident).then_inc(loaded, 16)
            sp.dma_start(fold_s[:], fold).then_inc(loaded, 16)
            sp.wait_ge(loaded, 48)

        @block.tensor
        def _(pe):
            def turn_keys(nth):
                pe.wait_ge(nodes_ready, nth + 1)
                wait_above_zero(pe, keys_copied, nth)
                for j in range(CH):
                    last = nc.tensor.transpose(turn_ps[:, j * P:(j + 1) * P],
                                               nodes2[:, j].rearrange("p a c -> p (a c)"), ident_b[:])
                last.then_inc(keys_turned, 1)

            def make_queries(nth, cols):
                pe.wait_ge(keys_copied, nth + 1)
                wait_above_zero(pe, q_both_ready, nth)
                wait_above_zero(pe, q_hi_ready, nth)
                nc.tensor.matmul(turn_ps[:, 0:TT], w2x_s[:], keys_t[:, cols],
                                 start=True, stop=True).then_inc(q_made, 1)

            def first_maximum(b):
                wait_above_zero(pe, p_ready, NG * TILES * b)
                pe.wait_ge(own_ready, TILES * b + 1)
                for k in range(NPAIRS):
                    wait_above_zero(pe, start_read, NPAIRS * b + k - 1)
                    for idx in range(2 * k, min(2 * k + 2, NMAX)):
                        c, j = idx // CH, idx % CH
                        if j == 0 or idx == 2 * k:
                            pe.wait_ge(k_hi_ready, TILES * b + c + 1)
                        last = nc.tensor.matmul(s_ps[k % 2][:, idx % 2, 0:TT], q_own[:, j * P:(j + 1) * P],
                                                k_hi[:, c * TT:(c + 1) * TT], start=True, stop=True)
                    last.then_inc(start_made, 1)

            def maximum(b, t, idx):
                made = MAXIMA * b + NMAX * (t - 1) + idx
                c, j = idx // CH, idx % CH
                if idx == 0:
                    pe.wait_ge(own_ready, TILES * b + t + 1)
                wait_above_zero(pe, max_read, made if idx == 0 else made - 1)
                nc.tensor.matmul(max_ps[idx % 2][:, 0:TT], q_own[:, j * P:(j + 1) * P], k_hi[:, c * TT:(c + 1) * TT],
                                 start=True, stop=True).then_inc(max_made, 1)

            def turn_shift(b, t):
                pe.wait_ge(neg_ready, TILES * b + t + 1)
                for j in range(CH):
                    last = nc.tensor.transpose(turn_ps[0:C + 1, j * P:(j + 1) * P], neg_max[:, j, :], ident_b[:])
                last.then_inc(shift_turned, 1)

            def scores(b, t, g, kind):
                at = NG * (TILES * b + t) + g
                if g == 0:
                    pe.wait_ge(shift_ready, TILES * b + t + 1)
                wait_above_zero(pe, p_ready, at if kind == "first" and g == 0 else at - 1)
                q = ds(t * TT, TT)
                for r in range(GROUPS[g]):
                    m = FIRST[g] + r
                    if r == 1 and has_maxima(kind):
                        maximum(b, t + 1, MAX_FROM[g])
                    out = s_ps[g % 2][:, r, 0:TT]
                    nc.tensor.matmul(out, k_hi[:, m * P:(m + 1) * P], q_both[:, q], start=True, stop=False)
                    last = nc.tensor.matmul(out, k_lo[:, m * P:(m + 1) * P], q_hi[:, q], start=False, stop=True)
                last.then_inc(s_ready, 1)

            def gather(b, t, g, now, maxima):
                at = NG * (TILES * b + t) + g
                pe.wait_ge(dve_low, at + 1)
                pe.wait_ge(pool_low, at + 1)
                high_ready(pe, b, t, g)
                if g == 0:
                    wait_above_zero(pe, out_copied, TILES * b + t)
                for r in range(GROUPS[g]):
                    m = FIRST[g] + r
                    for part in (p_hi, p_lo):
                        last = nc.tensor.matmul(o_ps[:, 0:TT], values_s[:, m, :], part[:, g % RING, r * TT:(r + 1) * TT],
                                                start=(m == 0 and part is p_hi), stop=(m == NT - 1 and part is p_lo))
                    if r == 0:
                        for idx in maxima:
                            maximum(b, now + 1, idx)
                last.then_inc(pv_done, 1)

            def turn_out(b, t):
                pe.wait_ge(out_copied, TILES * b + t + 1)
                for j in range(CH):
                    last = nc.tensor.matmul(turn_ps[:, j * (C + 1):(j + 1) * (C + 1)],
                                            out_cols[:, j * P:(j + 1) * P], fold_s[:], start=True, stop=True)
                last.then_inc(out_turned, 1)

            def turn(b, t, kind, ahead):
                for g in range(LAG if kind == "tail" else NG):
                    if kind != "tail":
                        scores(b, t, g, kind)
                    rest = []
                    if has_maxima(kind):
                        rest = list(range(MAX_FROM[g] + (GROUPS[g] == 2), MAX_FROM[g] + MAX_PER[g]))
                        if len(rest) == 2:
                            maximum(b, t + 1, rest.pop(0))
                    if g == SHIFT_AT and has_maxima(kind):
                        if ahead:
                            pe.wait_ge(keys_copied, TILES * (b + 1) + t + 1)
                        elif kind != "late":
                            pe.wait_ge(q_both_ready, TILES * b + t + AHEAD + 1)
                            pe.wait_ge(q_hi_ready, TILES * b + t + AHEAD + 1)
                        else:
                            pe.wait_ge(out_added, CH * (TILES * b + t))
                        turn_shift(b, t + 1)
                    if g < LAG and kind != "first":
                        gather(b, t - 1, g + NG - LAG, t, rest)
                    elif g >= LAG and kind != "tail":
                        gather(b, t, g - LAG, t, rest)
                    else:
                        for idx in rest:
                            maximum(b, t + 1, idx)
                    if g == OUT_AT and kind != "first":
                        turn_out(b, t - 1)
                    if g == Q_AT and makes_queries(kind, ahead):
                        wait_above_zero(pe, out_added, CH * (TILES * b + t))
                        make_queries(TILES * b + t + AHEAD, ahead_cols(kind, t))
                    if g == KEY_AT and ahead:
                        pe.wait_ge(q_both_ready, TILES * b + t + AHEAD + 1)
                        pe.wait_ge(q_hi_ready, TILES * b + t + AHEAD + 1)
                        turn_keys(TILES * (b + 1) + t)

            def batch(b, ahead):
                if not isinstance(b, int) or b > 0:
                    pe.wait_ge(keys_copied, TILES * (b + 1))
                    turn_out(b - 1, TILES - 1)
                first_maximum(b)
                wait_above_zero(pe, out_added, CH * TILES * b)
                turn_shift(b, 0)
                pe.wait_ge(start_read, NPAIRS * (b + 1))
                pe.wait_ge(k_lo_ready, TILES * (b + 1))
                pe.wait_ge(values_ready, b + 1)
                turns(pe, b, lambda b, t, kind: turn(b, t, kind, ahead))

            pe.wait_ge(loaded, 48)
            for t in range(TILES):
                turn_keys(t)
            pe.wait_ge(keys_copied, TILES)
            for t in range(AHEAD):
                make_queries(t, slice(t * TT, (t + 1) * TT))
            pe.wait_ge(q_both_ready, AHEAD)
            pe.wait_ge(q_hi_ready, AHEAD)
            batches(pe, batch)
            pe.wait_ge(out_added, CH * (TILES * B - 1))
            turn_out(B - 1, TILES - 1)

        @block.scalar
        def _(act):
            def squares(nth, slot):
                act.wait_ge(centred_ready, nth + 1)
                nc.scalar.activation(square[:, slot], centred[:, slot], ACT.Square).then_inc(square_ready, 1)

            def keep_nodes(nth, at):
                act.wait_ge(nodes_ready, nth + 1)
                nc.scalar.copy(nodes[:, at, :], nodes2[:, :, 0, :]).then_inc(nodes_kept, 1)

            def copy_keys(nth, cols):
                act.wait_ge(keys_turned, nth + 1)
                nc.scalar.copy(keys_t[:, cols], turn_ps[:, 0:TT]).then_inc(keys_copied, 1)

            def copy_queries(nth, cols):
                act.wait_ge(q_made, nth + 1)
                nc.scalar.copy(q_both[:, cols], turn_ps[:, 0:TT]).then_inc(q_rounded, 1)
                nc.scalar.copy(q_hi[0:C, cols], turn_ps[0:C, 0:TT]).then_inc(q_hi_ready, 1)

            def copy_out(b, t):
                act.wait_ge(pv_done, NG * (TILES * b + t + 1))
                wait_above_zero(act, out_turned, TILES * b + t)
                nc.scalar.copy(out_cols[:], o_ps[:, 0:TT]).then_inc(out_copied, 1)

            def copy_shift(b, t):
                act.wait_ge(shift_turned, TILES * b + t + 1)
                nc.scalar.copy(q_hi[C:C + 1, ds(t * TT, TT)], turn_ps[C:C + 1, 0:TT]).then_inc(shift_ready, 1)

            def turn(b, t, kind, ahead):
                for g in range(LAG if kind == "tail" else NG):
                    at = NG * (TILES * b + t) + g
                    n = GROUPS[g]
                    if kind != "tail":
                        act.wait_ge(s_ready, at + 1)
                        wait_above_zero(act, dve_low, at + 1 - RING)
                        wait_above_zero(act, pool_low, at + 1 - RING)
                        nc.scalar.activation(probs[:, g % RING, 0:n * TT].rearrange("p (r q) -> p r q", r=n),
                                             s_ps[g % 2][:, 0:n, 0:TT], ACT.Exp, scale=NORM).then_inc(p_ready, 1)
                    if g == LAG - 1 and kind != "first":
                        copy_out(b, t - 1)
                    if g == SHIFT_OUT and has_maxima(kind):
                        copy_shift(b, t + 1)
                    if kind != "tail" and g in ACT_HIGH:
                        act.wait_ge(p_ready, at + 1)
                        wait_above_zero(act, pv_done, at + 1 - RING)
                        nc.scalar.copy(p_hi[:, g % RING, 0:n * TT], probs[:, g % RING, 0:n * TT]).then_inc(act_high, 1)
                    nth = TILES * (b + 1) + t
                    if g == Q_AT + 1 and makes_queries(kind, ahead):
                        copy_queries(TILES * b + t + AHEAD, ahead_cols(kind, t))
                    if ahead and kind != "tail":
                        if g == SQUARE_AT:
                            act.wait_ge(square_sum, nth)
                            squares(nth, 0)
                        if g == NODES_AT + 2:
                            act.wait_ge(values_ready, b + 1)
                            keep_nodes(nth, ds(CH * t, CH))
                        if g == KEY_AT + 1:
                            act.wait_ge(k_lo_ready, TILES * (b + 1))
                            copy_keys(nth, ds(TT * t, TT))

            def batch(b, ahead):
                wait_above_zero(act, s_ready, NG * TILES * b)
                for c in range(TILES):
                    cols = slice(c * TT, (c + 1) * TT)
                    act.wait_ge(keys_copied, TILES * b + c + 1)
                    nc.scalar.copy(k_hi[:, cols], keys_t[:, cols]).then_inc(k_hi_ready, 1)
                act.wait_ge(nodes_kept, TILES * (b + 1))
                act.wait_ge(residue_ready, TILES * (b + 1))
                nc.scalar.copy(values_s[:, :, 0:C - 1], nodes[:, :, 0:C - 1])
                nc.scalar.copy(values_s[:, :, C - 1:C], residue[:].rearrange("p (n a) -> p n a", a=1)).then_inc(v_high, 1)
                copy_shift(b, 0)
                turns(act, b, lambda b, t, kind: turn(b, t, kind, ahead))

            for s in range(TILES + 2):
                if s < TILES:
                    wait_above_zero(act, square_sum, s + 1 - SLOTS)
                    squares(s, s % SLOTS)
                if s >= 2:
                    keep_nodes(s - 2, slice(CH * (s - 2), CH * (s - 1)))
                    copy_keys(s - 2, slice(TT * (s - 2), TT * (s - 1)))
            act.wait_ge(filled, 5)
            for t in range(AHEAD):
                copy_queries(t, slice(t * TT, (t + 1) * TT))
            batches(act, batch)

        @block.gpsimd
        def _(pool):
            def power(nth, slot):
                pool.wait_ge(var_ready, nth + 1)
                nc.gpsimd.tensor_tensor(stat[:, slot, 3, :], stat[:, slot, 2, :], half_s[:], ALU.pow).then_inc(rstd_ready, 1)

            def turn(b, t, kind, ahead):
                for g in range(0 if kind == "tail" else NG):
                    w = GROUPS[g] * TT
                    own = slice(int(w * DVE_LOW), w)
                    high_ready(pool, b, t, g)
                    nc.gpsimd.tensor_tensor(p_lo[:, g % RING, own], probs[:, g % RING, own],
                                            p_hi[:, g % RING, own].bitcast(F32), ALU.subtract).then_inc(pool_low, 1)
                    if g == POW_AT - 1 and ahead:
                        pool.wait_ge(nodes_ready, TILES * (b + 1) + t)
                        power(TILES * (b + 1) + t, 0)

            def batch(b, ahead):
                for c in range(TILES):
                    cols = slice(c * TT, (c + 1) * TT)
                    pool.wait_ge(k_hi_ready, TILES * b + c + 1)
                    nc.gpsimd.tensor_tensor(k_lo[0:C, cols], keys_t[0:C, cols], k_hi[0:C, cols].bitcast(F32),
                                            ALU.subtract).then_inc(k_lo_ready, 1)
                pool.wait_ge(v_high, b + 1)
                nc.gpsimd.tensor_tensor(values_s[:, :, C:2 * C - 1], nodes[:, :, 0:C - 1],
                                        values_s[:, :, 0:C - 1].bitcast(F32), ALU.subtract).then_inc(values_ready, 1)
                turns(pool, b, lambda b, t, kind: turn(b, t, kind, ahead))

            nc.gpsimd.memset(half_s[:], -0.5).then_inc(half_ready, 1)
            nc.gpsimd.memset(neg_max[:], 0.0).then_inc(filled, 1)
            nc.gpsimd.memset(values_s[:, :, 2 * C - 1:2 * C].bitcast(F32), 1.0).then_inc(filled, 1)
            pool.wait_ge(half_ready, 1)
            for t in range(TILES):
                wait_above_zero(pool, nodes_ready, t + 1 - SLOTS)
                power(t, t % SLOTS)
            pool.wait_ge(rstd_ready, TILES)
            nc.gpsimd.memset(q_hi[C:P, :].bitcast(F32), 0.0).then_inc(filled, 1)
            pool.wait_ge(filled, 3)
            nc.gpsimd.memset(k_lo[C:P, :].bitcast(F32), 0.0).then_inc(filled, 1)
            pool.wait_ge(filled, 4)
            nc.gpsimd.memset(k_lo[C:C + 1, :].bitcast(F32), 1.0).then_inc(filled, 1)
            pool.wait_ge(filled, 5)
            batches(pool, batch)

        @block.vector
        def _(dve):
            def per_token(slot, row):
                return stat[:, slot, row, :].rearrange("p (n a) -> p n a", a=1)

            def centre(nth, slot, parts):
                for own, at in parts:
                    last = nc.vector.tensor_reduce(stat[:, slot, 0, own], tokens[:, at, :], AX.X, ALU.add)
                last.then_inc(sum_ready, 1)
                dve.wait_ge(sum_ready, nth + 1)
                nc.vector.tensor_scalar(stat[:, slot, 1, :], stat[:, slot, 0, :], 1.0 / C, None, ALU.mult)\
                    .then_inc(mean_ready, 1)
                dve.wait_ge(mean_ready, nth + 1)
                for own, at in parts:
                    n = own.stop - own.start
                    last = nc.vector.tensor_tensor(centred[:, slot, own, :], tokens[:, at, :],
                                                   per_token(slot, 1)[:, own, :].broadcast_to([P, n, C]), ALU.subtract)
                last.then_inc(centred_ready, 1)

            def variance(nth, slot):
                dve.wait_ge(square_ready, nth + 1)
                nc.vector.tensor_reduce(stat[:, slot, 0, :], square[:, slot], AX.X, ALU.add).then_inc(square_sum, 1)
                dve.wait_ge(square_sum, nth + 1)
                nc.vector.tensor_scalar(stat[:, slot, 2, :], stat[:, slot, 0, :], 1.0 / C, LN_EPS, ALU.mult, ALU.add)\
                    .then_inc(var_ready, 1)

            def normalize(nth, slot, at):
                dve.wait_ge(rstd_ready, nth + 1)
                wait_above_zero(dve, keys_turned, nth)
                wait_above_zero(dve, nodes_kept, nth)
                wait_above_zero(dve, residue_ready, nth)
                nc.vector.tensor_tensor(
                    nodes2[:], centred[:, slot].rearrange("p n (a c) -> p n a c", a=1).broadcast_to([P, CH, 2, C]),
                    stat[:, slot, 3, :].rearrange("p (n a c) -> p n a c", a=1, c=1).broadcast_to([P, CH, 2, C]),
                    ALU.mult).then_inc(nodes_ready, 1)
                dve.wait_ge(nodes_ready, nth + 1)
                nc.vector.tensor_reduce(residue[:, at], nodes2[:, :, 0, :], AX.X, ALU.add).then_inc(residue_ready, 1)

            def low_queries(nth, cols):
                dve.wait_ge(q_rounded, nth + 1)
                nc.vector.tensor_tensor(q_both[C:P, cols], turn_ps[C:P, 0:TT], q_both[C:P, cols].bitcast(F32),
                                        ALU.subtract).then_inc(q_both_ready, 1)

            def take_own(nth, cols):
                dve.wait_ge(q_both_ready, nth + 1)
                nc.vector.tensor_copy(q_own[:], q_both[:, cols].bitcast(F32)).then_inc(own_ready, 1)

            def high(b, t, g):
                at = NG * (TILES * b + t) + g
                w = GROUPS[g] * TT
                dve.wait_ge(p_ready, at + 1)
                wait_above_zero(dve, pv_done, at + 1 - RING)
                nc.vector.tensor_copy(p_hi[:, g % RING, 0:w], probs[:, g % RING, 0:w]).then_inc(dve_high, 1)

            def low(b, t, g):
                own = slice(0, int(GROUPS[g] * TT * DVE_LOW))
                high_ready(dve, b, t, g)
                nc.vector.tensor_tensor(p_lo[:, g % RING, own], probs[:, g % RING, own],
                                        p_hi[:, g % RING, own].bitcast(F32), ALU.subtract).then_inc(dve_low, 1)

            def split_at(b, t, g):
                if g < 0:
                    t, g = t - 1, NG - 1
                if g in DVE_HIGH:
                    high(b, t, g)
                low(b, t, g)

            def read_first_maximum(b):
                for k in range(NPAIRS):
                    n = min(2, NMAX - 2 * k)
                    dve.wait_ge(start_made, NPAIRS * b + k + 1)
                    nc.vector.tensor_reduce(cmax[:, 2 * k:2 * k + n], s_ps[k % 2][:, 0:n, 0:TT], AX.X, ALU.max)\
                        .then_inc(start_read, 1)
                dve.wait_ge(start_read, NPAIRS * (b + 1))

            def read_max(b, t, idx):
                made = MAXIMA * b + NMAX * (t - 1) + idx
                dve.wait_ge(max_made, made + 1)
                if idx == 0:
                    dve.wait_ge(neg_ready, TILES * b + t)
                nc.vector.tensor_reduce(cmax[:, idx:idx + 1], max_ps[idx % 2][:, 0:TT], AX.X, ALU.max).then_inc(max_read, 1)

            def negate(b, t):
                wait_above_zero(dve, shift_turned, TILES * b + t)
                nc.vector.tensor_reduce(neg_max[:, :, C:C + 1], cmax[:].rearrange("p (c j) -> p j c", j=CH), AX.X, ALU.max,
                                        negate=True).then_inc(neg_ready, 1)

            def add_out(b, t, kind):
                dve.wait_ge(out_turned, TILES * b + t + 1)
                turned = turn_ps[:, 0:CH * (C + 1)].rearrange("p (j c) -> p j c", j=CH)
                nc.vector.reciprocal(sum_inv[:], turned[:, :, C:C + 1]).then_inc(inv_ready, 1)
                dve.wait_ge(inv_ready, TILES * b + t + 1)
                for j in range(CH):
                    if kind == "tail" and j == CH - 1:
                        at = ds(NPAIR + b, 1)
                    else:
                        at = ds((NT - 1) * b + CH * t + j, 1)
                    nc.vector.scalar_tensor_tensor(out=tokens[:, at, :].rearrange("p a c -> p (a c)"),
                                                   in0=turned[:, j, 0:C], scalar=sum_inv[:, j, :],
                                                   in1=tokens[:, at, :].rearrange("p a c -> p (a c)"),
                                                   op0=ALU.mult, op1=ALU.add).then_inc(out_added, 1)

            def places(b, t, last):
                if last:
                    return [(slice(0, CH - 1), ds((NT - 1) * b + CH * t, CH - 1)), (slice(CH - 1, CH), ds(NPAIR + b, 1))]
                return [(slice(0, CH), ds((NT - 1) * b + CH * t, CH))]

            def turn(b, t, kind, ahead):
                for g in range(1 if kind == "tail" else NG):
                    reads = MAX_PER[g] if has_maxima(kind) else 0
                    if g == 0 and not (kind == "first" and g == 0):
                        split_at(b, t, g - 1)
                    for k in range(max(reads, 1)):
                        if k < reads:
                            read_max(b, t + 1, MAX_FROM[g] + k)
                            if MAX_FROM[g] + k == NMAX - 1:
                                dve.wait_ge(max_read, MAXIMA * b + NMAX * (t + 1))
                                negate(b, t + 1)
                        if k == 0 and g > 0:
                            split_at(b, t, g - 1)
                    if g == OUT_AT and kind != "first":
                        add_out(b, t - 1, kind)
                    if kind != "tail" and ahead:
                        nth = TILES * (b + 1) + t
                        if g == CENTRE_AT:
                            dve.wait_ge(nodes_ready, nth)
                            centre(nth, 0, places(b + 1, t, kind == "last"))
                        if g == VAR_AT:
                            variance(nth, 0)
                        if g == NODES_AT:
                            dve.wait_ge(v_high, b + 1)
                            normalize(nth, 0, ds(CH * t, CH))
                    if g == Q_AT + 2 and makes_queries(kind, ahead):
                        low_queries(TILES * b + t + AHEAD, ahead_cols(kind, t))
                    if g == SHIFT_AT and (kind in ("first", "mid") or (kind == "late" and ahead)):
                        take_own(TILES * b + t + AHEAD, ahead_cols(kind, t))

            def batch(b, ahead):
                if not isinstance(b, int) or b > 0:
                    add_out(b - 1, TILES - 1, "tail")
                read_first_maximum(b)
                negate(b, 0)
                take_own(TILES * b + 1, slice(TT, 2 * TT))
                turns(dve, b, lambda b, t, kind: turn(b, t, kind, ahead))

            for s in range(TILES + 2):
                if s < TILES:
                    wait_above_zero(dve, nodes_ready, s + 1 - SLOTS)
                    centre(s, s % SLOTS, places(0, s, s == TILES - 1))
                if 1 <= s <= TILES:
                    variance(s - 1, (s - 1) % SLOTS)
                if s >= 2:
                    normalize(s - 2, (s - 2) % SLOTS, slice(CH * (s - 2), CH * (s - 1)))
            dve.wait_ge(filled, 5)
            for t in range(AHEAD):
                low_queries(t, slice(t * TT, (t + 1) * TT))
            take_own(0, slice(0, TT))
            batches(dve, batch)
            add_out(B - 1, TILES - 1, "tail")


def attention_layout(w):
    w2x = np.zeros((P, P), np.float32)
    w2x[0:C, 0:C] = w
    w2x[0:C, C:P] = w
    fold = np.zeros((P, C + 1), np.float32)
    for c in range(C - 1):
        for row in (c, C + c):
            fold[row, c] = 1.0
            fold[row, C - 1] = -1.0
    fold[C - 1, C - 1] = 1.0
    fold[P - 1, C] = 1.0
    return w2x, fold


U32 = mybir.dt.uint32
E, F = 16, 128
BT = 4
BW = BT * P
NTILES = NPAIR + B
NBLOCK = NTILES // BT
LO = 32
LAG2 = 4
TURN_BACK = 7
RING2 = 8
DVE_LOWS = [3, 8, 11, 13]
POOL_LOWS = [e for e in range(E) if e not in DVE_LOWS]
DVE_HIGHS = [0, 2, 12, 15]
ACT_HIGHS = [e for e in range(E) if e not in DVE_HIGHS]


def experts(nc, gate_w, w1, w2, sel, b2, b1, gate_b, rows, pick, ident, tokens, out):
    with ExitStack() as ctx:
        def sb(name, shape, dt=F32):
            return ctx.enter_context(nc.sbuf_tensor(name, shape, dt))

        def ps(name, shape):
            return ctx.enter_context(nc.psum_tensor(name, shape, F32))

        def sem(name):
            return ctx.enter_context(nc.semaphore(name))

        ident_c = sb("ident_c", [P, P])
        gate_w_s = sb("gate_w_s", [P, P])
        w1_s = sb("w1_s", [P, E, F])
        w1_hi = sb("w1_hi", [P, E, F], F32R)
        w1_lo = sb("w1_lo", [P, E, F], F32R)
        w2_s = sb("w2_s", [P, E, 2, C])
        w2_r = sb("w2_r", [P, E, 2, C], F32R)
        half_c = sb("half_c", [P, BT])
        pick_s = sb("pick_s", [P, P])
        pick_r = sb("pick_r", [P, P], F32R)
        sel_s = sb("sel_s", [P, E, P])
        sel_r = sb("sel_r", [P, E, P], F32R)
        b2_s = sb("b2_s", [P, P])
        b2_r = sb("b2_r", [P, P], F32R)
        b1_s = sb("b1_s", [P, E])
        gate_b_s = sb("gate_b_s", [P, 1])
        rows_s = sb("rows_s", [P, 2, C])
        places = sb("places", [P, E])

        stat = sb("c_stat", [P, 4, BT])
        centred = sb("c_centred", [P, BT, C])
        square = sb("c_square", [P, BT, C])
        y = sb("y", [P, BT, 2, C])
        y_t = sb("y_t", [P, BW])
        y_both = sb("y_both", [P, 2, BW], F32R)
        logit_cols = sb("logit_cols", [P, BW])
        logits = sb("logits", [P, BT, E])
        top = sb("top", [P, BT, 8])
        top_at = sb("top_at", [P, BT, 8], U32)
        at_f = sb("at_f", [P, BT, 2])
        is_top = sb("is_top", [P, 2, BT, E])
        gap = sb("gap", [P, 4, BT])
        gates = sb("gates", [P, BT, P // LO, LO])
        gates_t = sb("gates_t", [P, 2, BW], F32R)
        hidden = sb("hidden", [P, 4, BW])      
        gated = sb("gated", [P, RING2, BW])
        h_hi = sb("h_hi", [P, RING2, BW], F32R)
        h_lo = sb("h_lo", [P, RING2, BW], F32R)
        moe_cols = sb("moe_cols", [P, BW])
        f_stat = sb("f_stat", [P, 4, BT])
        f_centred = sb("f_centred", [P, BT, C])
        f_square = sb("f_square", [P, BT, C])
        f_norm = sb("f_norm", [P, BT, C])
        f_scaled = sb("f_scaled", [P, BT, C])
        f_shift = sb("f_shift", [P, BT, C])
        result = sb("result", [P, 2, BT, C])

        z_ps = [ps(f"z_ps{i}", [P, BW]) for i in range(2)]
        gate_ps = [ps(f"gate_ps{i}", [P, BW]) for i in range(2)]
        moe_ps = [ps(f"moe_ps{i}", [P, BW]) for i in range(2)]
        prep_a = ps("prep_a", [P, BW])
        prep_b = ps("prep_b", [P, BW])

        small_loaded = sem("small_loaded")
        loaded = sem("c_loaded")
        filled = sem("c_filled")
        rounded = sem("c_rounded")
        weights_ready = sem("weights_ready")
        sum_ready = sem("c_sum_ready")
        mean_ready = sem("c_mean_ready")
        centred_ready = sem("c_centred_ready")
        square_ready = sem("c_square_ready")
        square_sum = sem("c_square_sum")
        var_ready = sem("c_var_ready")
        rstd_ready = sem("c_rstd_ready")
        y_ready = sem("y_ready")
        y_turned = sem("y_turned")
        y_copied = sem("y_copied")
        y_rounded = sem("y_rounded")
        y_both_ready = sem("y_both_ready")
        logits_made = sem("logits_made")
        logits_biased = sem("logits_biased")
        logits_turned = sem("logits_turned")
        logits_ready = sem("logits_ready")
        top_ready = sem("top_ready")
        top_at_ready = sem("top_at_ready")
        at_ready = sem("at_ready")
        is_top_ready = sem("is_top_ready")
        gap_ready = sem("gap_ready")
        gap_exp = sem("gap_exp")
        gap_sum = sem("gap_sum")
        first_ready = sem("first_ready")
        second_ready = sem("second_ready")
        weighed = sem("weighed")
        gates_ready = sem("gates_ready")
        gates_turned = sem("gates_turned")
        gates_rounded = sem("gates_rounded")
        gates_t_ready = sem("gates_t_ready")
        gate_spread = sem("gate_spread")
        z_ready = sem("z_ready")
        hidden_ready = sem("hidden_ready")
        act_highs = sem("act_highs")
        dve_highs = sem("dve_highs")
        dve_lows = sem("dve_lows")
        pool_lows = sem("pool_lows")
        half_set = sem("half_set")
        gated_ready = sem("gated_ready")
        moe_step = sem("moe_step")
        moe_copied = sem("moe_copied")
        moe_turned = sem("moe_turned")
        f_sum_ready = sem("f_sum_ready")
        f_mean_ready = sem("f_mean_ready")
        f_centred_ready = sem("f_centred_ready")
        f_square_ready = sem("f_square_ready")
        f_square_sum = sem("f_square_sum")
        f_var_ready = sem("f_var_ready")
        f_rstd_ready = sem("f_rstd_ready")
        f_norm_ready = sem("f_norm_ready")
        f_scaled_ready = sem("f_scaled_ready")
        f_shift_ready = sem("f_shift_ready")
        result_ready = sem("result_ready")
        stored = [sem(f"stored{h}") for h in range(2)]

        small = [(ident_c[:], ident), (gate_w_s[:], gate_w), (gate_b_s[:], gate_b),
                 (rows_s[:].rearrange("p a c -> p (a c)"), rows[:, 0:2 * C]), (places[:], rows[:, 2 * C:2 * C + E])]
        consts = [(w1_s[:].rearrange("p e f -> p (e f)"), w1), (w2_s[:].rearrange("p e a c -> p (e a c)"), w2),
                  (b1_s[:], b1), (b2_s[:], b2), (pick_s[:], pick), (sel_s[:].rearrange("p e c -> p (e c)"), sel)]
        ALL_SMALL, ALL_CONSTS = 16 * len(small), 16 * len(consts)

        block = ctx.enter_context(nc.Block())

        def run_blocks(eng, step):
            step(0, 0, "first")
            step(1, 1, "mid")
            step(2, 0, "mid")
            with eng.Fori(1, (NBLOCK - 3) // 2) as i:
                step(2 * i + 1, 1, "mid")
                step(2 * i + 2, 0, "mid")
            step(NBLOCK - 2, 1, "late")
            step(NBLOCK - 1, 0, "last")
            step(NBLOCK, 1, "tail")

        @block.sync
        def _(sp):
            for dst, src in small:
                sp.dma_start(dst, src).then_inc(small_loaded, 16)
            for dst, src in consts:
                sp.dma_start(dst, src).then_inc(loaded, 16)

            def store(n, half):
                sp.wait_ge(result_ready, n + 1)
                sp.dma_start(out[ds(BT * n, BT)].rearrange("n p c -> p n c"), result[:, half]).then_inc(stored[half], 16)

            with sp.Fori(0, NBLOCK // 2) as i:
                store(2 * i, 0)
                store(2 * i + 1, 1)
            store(NBLOCK - 1, 0)
            sp.wait_ge(stored[0], 16 * (NBLOCK // 2 + 1))
            sp.wait_ge(stored[1], 16 * (NBLOCK // 2))

        def high_ready(eng, n, e):
            own, done = (DVE_HIGHS, dve_highs) if e in DVE_HIGHS else (ACT_HIGHS, act_highs)
            eng.wait_ge(done, len(own) * n + own.index(e) + 1)

        def low_ready(eng, n, e):
            own, done = (DVE_LOWS, dve_lows) if e in DVE_LOWS else (POOL_LOWS, pool_lows)
            eng.wait_ge(done, len(own) * n + own.index(e) + 1)

        @block.tensor
        def _(pe):
            def turn_y(n):
                pe.wait_ge(y_ready, n + 1)
                for j in range(BT):
                    last = nc.tensor.transpose(prep_a[:, j * P:(j + 1) * P], y[:, j].rearrange("p a c -> p (a c)"),
                                               ident_c[:])
                last.then_inc(y_turned, 1)

            def make_logits(n):
                pe.wait_ge(y_copied, n + 1)
                wait_above_zero(pe, gates_t_ready, n)
                nc.tensor.matmul(prep_b[:], gate_w_s[:], y_t[:], start=True, stop=True).then_inc(logits_made, 1)

            def turn_logits(n):
                pe.wait_ge(logits_biased, n + 1)
                pe.wait_ge(y_both_ready, n + 1)
                for j in range(BT):
                    last = nc.tensor.transpose(prep_a[:, j * P:(j + 1) * P], logit_cols[:, j * P:(j + 1) * P],
                                               ident_c[:])
                last.then_inc(logits_turned, 1)

            def turn_gates(n):
                pe.wait_ge(gates_ready, n + 1)
                for j in range(BT):
                    last = nc.tensor.transpose(prep_b[:, j * P:(j + 1) * P],
                                               gates[:, j].rearrange("p a c -> p (a c)"), ident_c[:])
                last.then_inc(gates_turned, 1)

            def spread(n, half, e):
                wait_above_zero(pe, gated_ready, E * n + e - 1)
                nc.tensor.matmul(gate_ps[e % 2][:], sel_r[:, e, :], gates_t[:, half, :],
                                 start=True, stop=True).then_inc(gate_spread, 1)

            def first_layer(n, half, e):
                wait_above_zero(pe, hidden_ready, E * n + e - 1)
                nc.tensor.matmul(z_ps[e % 2][:], w1_hi[:, e, :], y_both[:, half, :], start=True, stop=False)
                nc.tensor.matmul(z_ps[e % 2][:], w1_lo[:, e, :], y_both[:, half, :],
                                 start=False, stop=True).then_inc(z_ready, 1)

            def second_layer(n, half, e):
                low_ready(pe, n, e)
                for part in (h_hi, h_lo):
                    last = nc.tensor.matmul(moe_ps[half][:], w2_r[:, e].rearrange("p a c -> p (a c)"), part[:, e % RING2, :],
                                            start=False, stop=(e == E - 1 and part is h_lo))
                last.then_inc(moe_step, 1)

            def second_bias(n, half):
                wait_above_zero(pe, moe_copied, n - 1)
                nc.tensor.matmul(moe_ps[half][:], b2_r[:], gates_t[:, half, :], start=True, stop=False)
                nc.tensor.matmul(moe_ps[half][:], pick_r[:], y_both[:, half, :], start=False, stop=False)

            def turn_back(n):
                pe.wait_ge(moe_copied, n + 1)
                for j in range(BT):
                    last = nc.tensor.matmul(prep_a[:, j * C:(j + 1) * C], moe_cols[:, j * P:(j + 1) * P],
                                            pick_s[:, 0:C], start=True, stop=True)
                last.then_inc(moe_turned, 1)

            def prepare(n, half, e):
                if e == 2:
                    make_logits(n)
                if e == 4:
                    turn_logits(n)
                if e == 9:
                    turn_gates(n)

            def step(n, half, kind):
                prepares = kind in ("first", "mid", "late")
                if kind != "tail":
                    pe.wait_ge(y_both_ready, n + 1)
                    pe.wait_ge(gates_t_ready, n + 1)
                for e in range(TURN_BACK + 1 if kind == "tail" else E):
                    if kind != "tail":
                        first_layer(n, half, e)
                        spread(n, half, e)
                    if e < LAG2 and kind != "first":
                        second_layer(n - 1, 1 - half, E - LAG2 + e)
                    if e == LAG2 and kind != "tail":
                        second_bias(n, half)
                    if e >= LAG2 and kind != "tail":
                        second_layer(n, half, e - LAG2)
                    if e == TURN_BACK and kind != "first":
                        if prepares:
                            pe.wait_ge(top_ready, BT * (n + 2))
                        else:
                            pe.wait_ge(f_centred_ready, n - 1)
                        turn_back(n - 1)
                    if prepares:
                        prepare(n + 1, 1 - half, e)
                    if e == E - 1 and kind in ("first", "mid"):
                        pe.wait_ge(top_ready, BT * (n + 2))
                        wait_above_zero(pe, f_centred_ready, n)
                        turn_y(n + 2)

            pe.wait_ge(small_loaded, ALL_SMALL)
            turn_y(0)
            for e in range(E):
                prepare(0, 0, e)
            pe.wait_ge(top_ready, BT)
            turn_y(1)
            pe.wait_ge(loaded, ALL_CONSTS)
            pe.wait_ge(weights_ready, 5)
            run_blocks(pe, step)

        @block.scalar
        def _(act):
            def squares(n):
                act.wait_ge(centred_ready, n + 1)
                wait_above_zero(act, square_sum, n)
                nc.scalar.activation(square[:], centred[:], ACT.Square).then_inc(square_ready, 1)

            def write_y(n, tiles):
                act.wait_ge(rstd_ready, n + 1)
                wait_above_zero(act, y_turned, n)
                for j in tiles:
                    last = nc.scalar.activation(y[:, j], centred[:, j:j + 1, :].broadcast_to([P, 2, C]), ACT.Copy,
                                                scale=stat[:, 3, j:j + 1])
                if BT - 1 in tiles:
                    last.then_inc(y_ready, 1)

            def copy_y(n):
                act.wait_ge(y_turned, n + 1)
                wait_above_zero(act, logits_made, n)
                nc.scalar.copy(y_t[:], prep_a[:]).then_inc(y_copied, 1)

            def round_y(n, half):
                act.wait_ge(y_turned, n + 1)
                wait_above_zero(act, z_ready, E * (n - 1))
                nc.scalar.copy(y_both[:, half, :], prep_a[:]).then_inc(y_rounded, 1)

            def add_gate_bias(n):
                act.wait_ge(logits_made, n + 1)
                wait_above_zero(act, logits_turned, n)
                nc.scalar.activation(logit_cols[:], prep_b[:], ACT.Identity, bias=gate_b_s[:])\
                    .then_inc(logits_biased, 1)

            def gap_exponent(n):
                act.wait_ge(gap_ready, n + 1)
                wait_above_zero(act, second_ready, n)
                nc.scalar.activation(gap[:, 1, :], gap[:, 0, :], ACT.Exp).then_inc(gap_exp, 1)

            def round_gates(n, half):
                act.wait_ge(gates_turned, n + 1)
                wait_above_zero(act, gate_spread, E * (n - 1))
                nc.scalar.copy(gates_t[0:2 * LO, half, :], prep_b[0:2 * LO, :]).then_inc(gates_rounded, 1)

            def relu(n, e):
                act.wait_ge(z_ready, E * n + e + 1)
                wait_above_zero(act, gated_ready, E * n + e - 3)
                nc.scalar.activation(hidden[:, e % 4, :], z_ps[e % 2][:], ACT.Relu, bias=b1_s[:, e:e + 1])\
                    .then_inc(hidden_ready, 1)

            def high(n, e):
                act.wait_ge(gated_ready, E * n + e + 1)
                wait_above_zero(act, moe_step, E * n + e + 1 - RING2)
                nc.scalar.copy(h_hi[:, e % RING2, :], gated[:, e % RING2, :]).then_inc(act_highs, 1)

            def copy_moe(n, half):
                act.wait_ge(moe_step, E * (n + 1))
                wait_above_zero(act, moe_turned, n)
                nc.scalar.copy(moe_cols[:], moe_ps[half][:]).then_inc(moe_copied, 1)

            def f_squares(n):
                act.wait_ge(f_centred_ready, n + 1)
                wait_above_zero(act, f_square_sum, n)
                nc.scalar.activation(f_square[:], f_centred[:], ACT.Square).then_inc(f_square_ready, 1)

            def prepare(n, half, e):
                if e == 0:
                    copy_y(n)
                if e == 1:
                    round_y(n, half)
                if e == 3:
                    add_gate_bias(n)
                if e == 6:
                    gap_exponent(n)
                if e == 10:
                    round_gates(n, half)

            def step(n, half, kind):
                for e in range(E):
                    if kind != "tail":
                        relu(n, e)
                    if (e - 1) % E in ACT_HIGHS:
                        if e > 0 and kind != "tail":
                            high(n, e - 1)
                        if e == 0 and kind != "first":
                            high(n - 1, E - 1)
                    if kind in ("first", "mid", "late"):
                        prepare(n + 1, 1 - half, e)
                    if kind != "first":
                        if e == LAG2 + 1:
                            copy_moe(n - 1, 1 - half)
                        if e == 9:
                            f_squares(n - 1)
                    if kind in ("first", "mid"):
                        if e == 4:
                            squares(n + 2)
                        if e == 13:
                            write_y(n + 2, (0, 1))
                        if e == 14:
                            write_y(n + 2, (2, 3))

            squares(0)
            write_y(0, range(BT))
            for e in range(E):
                if e == 3:
                    act.wait_ge(small_loaded, ALL_SMALL)
                prepare(0, 0, e)
            squares(1)
            write_y(1, range(BT))
            act.wait_ge(loaded, ALL_CONSTS)
            nc.scalar.copy(w1_hi[:], w1_s[:]).then_inc(rounded, 1)
            nc.scalar.copy(w2_r[:, :, 0, :], w2_s[:, :, 0, :]).then_inc(rounded, 1)
            nc.scalar.copy(b2_r[:, 0:C], b2_s[:, 0:C]).then_inc(rounded, 1)
            run_blocks(act, step)

        @block.vector
        def _(dve):
            def spread_rows(ap):
                return ap.rearrange("p (n a) -> p n a", a=1)

            def centre(n):
                at = ds(BT * n, BT)
                wait_above_zero(dve, y_ready, n)
                nc.vector.tensor_reduce(stat[:, 0, :], tokens[:, at, :], AX.X, ALU.add).then_inc(sum_ready, 1)
                dve.wait_ge(sum_ready, n + 1)
                nc.vector.tensor_scalar(stat[:, 1, :], stat[:, 0, :], 1.0 / C, None, ALU.mult).then_inc(mean_ready, 1)
                dve.wait_ge(mean_ready, n + 1)
                nc.vector.tensor_tensor(centred[:], tokens[:, at, :],
                                        spread_rows(stat[:, 1, :]).broadcast_to([P, BT, C]),
                                        ALU.subtract).then_inc(centred_ready, 1)

            def variance(n):
                dve.wait_ge(square_ready, n + 1)
                nc.vector.tensor_reduce(stat[:, 0, :], square[:], AX.X, ALU.add).then_inc(square_sum, 1)
                dve.wait_ge(square_sum, n + 1)
                nc.vector.tensor_scalar(stat[:, 2, :], stat[:, 0, :], 1.0 / C, LN_EPS, ALU.mult, ALU.add)\
                    .then_inc(var_ready, 1)

            def low_y(n, half):
                dve.wait_ge(y_rounded, n + 1)
                nc.vector.tensor_tensor(y_both[C:P, half, :], prep_a[C:P, :], y_both[C:P, half, :].bitcast(F32),
                                        ALU.subtract).then_inc(y_both_ready, 1)

            def choose(n):
                dve.wait_ge(logits_turned, n + 1)
                in_bank = prep_a[:].rearrange("p (n e) -> p n e", n=BT)[:, :, 0:E]
                nc.vector.tensor_copy(logits[:], in_bank).then_inc(logits_ready, 1)
                for j in range(BT):
                    nc.vector.max(top[:, j, :], in_bank[:, j, :]).then_inc(top_ready, 1)
                dve.wait_ge(logits_ready, n + 1)
                dve.wait_ge(top_ready, BT * (n + 1))
                nc.vector.tensor_tensor(spread_rows(gap[:, 0, :]), top[:, :, 1:2], top[:, :, 0:1],
                                        ALU.subtract).then_inc(gap_ready, 1)
                for j in range(BT):
                    nc.vector.max_index(top_at[:, j, :], top[:, j, :], logits[:, j, :]).then_inc(top_at_ready, 1)

            def mark(n):
                dve.wait_ge(top_at_ready, BT * (n + 1))
                nc.vector.tensor_copy(at_f[:], top_at[:, :, 0:2]).then_inc(at_ready, 1)
                dve.wait_ge(at_ready, n + 1)
                for r in range(2):
                    nc.vector.tensor_tensor(is_top[:, r], places[:].rearrange("p (a e) -> p a e", a=1).broadcast_to([P, BT, E]),
                                            at_f[:, :, r:r + 1].broadcast_to([P, BT, E]), ALU.is_equal)\
                        .then_inc(is_top_ready, 1)

            def weigh(n):
                dve.wait_ge(gap_exp, n + 1)
                nc.vector.tensor_scalar(gap[:, 2, :], gap[:, 1, :], 1.0, None, ALU.add).then_inc(gap_sum, 1)
                dve.wait_ge(gap_sum, n + 1)
                nc.vector.reciprocal(gap[:, 3, :], gap[:, 2, :]).then_inc(first_ready, 1)
                dve.wait_ge(first_ready, n + 1)
                nc.vector.tensor_tensor(gap[:, 2, :], gap[:, 1, :], gap[:, 3, :], ALU.mult).then_inc(second_ready, 1)
                dve.wait_ge(second_ready, n + 1)
                dve.wait_ge(is_top_ready, 2 * (n + 1))
                for r in range(2):
                    nc.vector.tensor_tensor(is_top[:, r], is_top[:, r],
                                            spread_rows(gap[:, 3 - r, :]).broadcast_to([P, BT, E]), ALU.mult)\
                        .then_inc(weighed, 1)
                dve.wait_ge(weighed, 2 * (n + 1))
                nc.vector.tensor_tensor(gates[:, :, 0:2, 0:E],
                                        is_top[:, 0].rearrange("p n (a e) -> p n a e", a=1).broadcast_to([P, BT, 2, E]),
                                        is_top[:, 1].rearrange("p n (a e) -> p n a e", a=1).broadcast_to([P, BT, 2, E]),
                                        ALU.add).then_inc(gates_ready, 1)

            def low_gates(n, half):
                dve.wait_ge(gates_rounded, n + 1)
                nc.vector.tensor_tensor(gates_t[LO:2 * LO, half, :], prep_b[LO:2 * LO, :],
                                        gates_t[LO:2 * LO, half, :].bitcast(F32), ALU.subtract).then_inc(gates_t_ready, 1)

            def gate(n, e):
                dve.wait_ge(hidden_ready, E * n + e + 1)
                dve.wait_ge(gate_spread, E * n + e + 1)
                wait_above_zero(dve, moe_step, E * n + e + 1 - RING2)
                nc.vector.tensor_tensor(gated[:, e % RING2, :], gate_ps[e % 2][:], hidden[:, e % 4, :],
                                        ALU.mult).then_inc(gated_ready, 1)

            def high(n, e):
                dve.wait_ge(gated_ready, E * n + e + 1)
                nc.vector.tensor_copy(h_hi[:, e % RING2, :], gated[:, e % RING2, :]).then_inc(dve_highs, 1)

            def low(n, e):
                high_ready(dve, n, e)
                nc.vector.tensor_tensor(h_lo[:, e % RING2, :], gated[:, e % RING2, :], h_hi[:, e % RING2, :].bitcast(F32),
                                        ALU.subtract).then_inc(dve_lows, 1)

            def f_centre(n, half):
                dve.wait_ge(moe_turned, n + 1)
                total = prep_a[:, 0:BT * C].rearrange("p (n c) -> p n c", n=BT)
                nc.vector.tensor_reduce(f_stat[:, 0, :], total, AX.X, ALU.add).then_inc(f_sum_ready, 1)
                dve.wait_ge(f_sum_ready, n + 1)
                nc.vector.tensor_scalar(f_stat[:, 1, :], f_stat[:, 0, :], 1.0 / C, None, ALU.mult).then_inc(f_mean_ready, 1)
                dve.wait_ge(f_mean_ready, n + 1)
                nc.vector.tensor_tensor(f_centred[:], total, spread_rows(f_stat[:, 1, :]).broadcast_to([P, BT, C]),
                                        ALU.subtract).then_inc(f_centred_ready, 1)

            def f_normalize(n):
                dve.wait_ge(f_rstd_ready, n + 1)
                wait_above_zero(dve, f_scaled_ready, n)
                nc.vector.tensor_tensor(f_norm[:], f_centred[:], spread_rows(f_stat[:, 3, :]).broadcast_to([P, BT, C]),
                                        ALU.mult).then_inc(f_norm_ready, 1)

            def f_variance(n):
                dve.wait_ge(f_square_ready, n + 1)
                nc.vector.tensor_reduce(f_stat[:, 0, :], f_square[:], AX.X, ALU.add).then_inc(f_square_sum, 1)
                dve.wait_ge(f_square_sum, n + 1)
                nc.vector.tensor_scalar(f_stat[:, 2, :], f_stat[:, 0, :], 1.0 / C, LN_EPS, ALU.mult, ALU.add)\
                    .then_inc(f_var_ready, 1)

            def prepare(n, half, e):
                if e == 2:
                    low_y(n, half)
                if e == 5:
                    choose(n)
                if e == 6:
                    mark(n)
                if e == 7:
                    weigh(n)
                if e == 11:
                    low_gates(n, half)

            def step(n, half, kind):
                for e in range(E):
                    if kind != "tail":
                        gate(n, e)
                    if kind != "tail" and e in DVE_HIGHS:
                        high(n, e)
                    if (e - 1) % E in DVE_LOWS:
                        if e > 0 and kind != "tail":
                            low(n, e - 1)
                        if e == 0 and kind != "first":
                            low(n - 1, E - 1)
                    if kind in ("first", "mid", "late"):
                        prepare(n + 1, 1 - half, e)
                    if kind != "first":
                        if e == 8:
                            f_centre(n - 1, 1 - half)
                        if e == 10:
                            f_variance(n - 1)
                        if e == 13:
                            f_normalize(n - 1)
                    if kind in ("first", "mid"):
                        if e == 3:
                            centre(n + 2)
                        if e == 8:
                            variance(n + 2)

            centre(0)
            variance(0)
            dve.wait_ge(small_loaded, ALL_SMALL)
            dve.wait_ge(filled, 2)
            for e in range(E):
                prepare(0, 0, e)
            centre(1)
            variance(1)
            dve.wait_ge(loaded, ALL_CONSTS)
            nc.vector.tensor_copy(sel_r[:], sel_s[:]).then_inc(weights_ready, 1)
            nc.vector.tensor_copy(pick_r[:], pick_s[:]).then_inc(weights_ready, 1)
            dve.wait_ge(rounded, 3)
            nc.vector.tensor_tensor(w1_lo[:], w1_s[:], w1_hi[:].bitcast(F32), ALU.subtract).then_inc(weights_ready, 1)
            nc.vector.tensor_tensor(w2_r[:, :, 1, :], w2_s[:, :, 1, :], w2_r[:, :, 0, :].bitcast(F32),
                                    ALU.subtract).then_inc(weights_ready, 1)
            nc.vector.tensor_tensor(b2_r[:, C:P], b2_s[:, C:P], b2_r[:, 0:C].bitcast(F32),
                                    ALU.subtract).then_inc(weights_ready, 1)
            run_blocks(dve, step)

        @block.gpsimd
        def _(pool):
            def finish(n, half):
                pool.wait_ge(f_norm_ready, n + 1)
                wait_above_zero(pool, result_ready, n)
                gamma = rows_s[:, 0:1, :].broadcast_to([P, BT, C])
                beta = rows_s[:, 1:2, :].broadcast_to([P, BT, C])
                nc.gpsimd.tensor_tensor(f_scaled[:], f_norm[:], gamma, ALU.mult).then_inc(f_scaled_ready, 1)
                nc.gpsimd.tensor_tensor(f_shift[:], tokens[:, ds(BT * n, BT), :], beta, ALU.add).then_inc(f_shift_ready, 1)
                pool.wait_ge(f_scaled_ready, n + 1)
                pool.wait_ge(f_shift_ready, n + 1)
                wait_above_zero(pool, stored[half], 8 * (n - half))
                nc.gpsimd.tensor_tensor(result[:, half], f_scaled[:], f_shift[:], ALU.add).then_inc(result_ready, 1)

            def power(n, from_var, row, done):
                pool.wait_ge(from_var, n + 1)
                nc.gpsimd.tensor_tensor(row[:, 3, :], row[:, 2, :], half_c[:], ALU.pow).then_inc(done, 1)

            def low(n, e):
                high_ready(pool, n, e)
                nc.gpsimd.tensor_tensor(h_lo[:, e % RING2, :], gated[:, e % RING2, :], h_hi[:, e % RING2, :].bitcast(F32),
                                        ALU.subtract).then_inc(pool_lows, 1)

            def token_power(n):
                wait_above_zero(pool, y_ready, n)
                power(n, var_ready, stat, rstd_ready)

            def step(n, half, kind):
                for e in range(E):
                    if (e - 1) % E in POOL_LOWS:
                        if e > 0 and kind != "tail":
                            low(n, e - 1)
                        if e == 0 and kind != "first":
                            low(n - 1, E - 1)
                    if kind in ("first", "mid") and e == 9:
                        token_power(n + 2)
                    if kind != "first":
                        if e == 11:
                            wait_above_zero(pool, f_norm_ready, n - 1)
                            power(n - 1, f_var_ready, f_stat, f_rstd_ready)
                        if e == 14:
                            finish(n - 1, 1 - half)

            nc.gpsimd.memset(half_c[:], -0.5).then_inc(half_set, 1)
            nc.gpsimd.memset(gates[:], 0.0).then_inc(filled, 1)
            nc.gpsimd.memset(gates_t[:].bitcast(F32), 0.0).then_inc(filled, 1)
            pool.wait_ge(half_set, 1)
            pool.wait_ge(small_loaded, ALL_SMALL)
            for n in range(2):
                token_power(n)
            run_blocks(pool, step)


def expert_layout(gate_w, gate_b, w1, b1, w2, b2, gamma, beta):
    f = np.float32
    gw = np.zeros((P, P), f)
    gw[0:C, 0:E] = gate_w
    gb = np.zeros((P, 1), f)
    gb[0:E, 0] = gate_b
    w1t = w1.transpose(1, 0, 2).reshape(C, E * F)
    sel = np.zeros((P, E, P), f)
    b2x = np.zeros((P, C), f)
    for e in range(E):
        sel[e, e] = sel[LO + e, e] = 1.0
    b2x[0:E] = b2
    b2x[LO:LO + E] = b2
    rows = np.concatenate([gamma, beta, np.arange(E, dtype=f)])
    pick = np.zeros((P, P), f)
    for c in range(C):
        pick[c, c] = pick[C + c, c] = 1.0
    return dict(gate_w=gw, pick=pick, w1=np.concatenate([w1t, w1t]), w2=np.tile(w2.transpose(1, 0, 2)[:, :, None], (1, 1, 2, 1)).reshape(F, 2 * E * C),
                sel=sel.reshape(P, E * P), b2=np.tile(b2x, (1, 2)), b1=np.ascontiguousarray(b1.T), gate_b=gb,
                rows=np.tile(rows, (P, 1)))


def fused_layer(nc, xw, txt, wqk, wv, wp, cols, trig, hmask, ident, w2x, fold,
                gate_w, w1, w2, sel, b2, b1, gate_b, rows, pick, out):
    with nc.sbuf_tensor("tokens", [P, NPAIR + B, C], F32) as tokens:
        window_attention(nc, xw, txt, wqk, wv, wp, cols, trig, hmask, ident, tokens)
        full_attention(nc, w2x, ident, fold, tokens)
        experts(nc, gate_w, w1, w2, sel, b2, b1, gate_b, rows, pick, ident, tokens, out)


def kernel(x, txt, L0_tok_qkv_w, L0_tok_qkv_b, L0_tok_proj_w, L0_tok_proj_b, L0_attn_W, L0_ffn_gate_w,
           L0_ffn_gate_b, L0_ffn_w1, L0_ffn_b1, L0_ffn_w2, L0_ffn_b2, L0_ffn_gamma, L0_ffn_beta):
    import concourse.bacc as bacc
    from concourse.bass_utils import run_bass_kernel_spmd

    a = [np.asarray(v) for v in (x, L0_tok_qkv_w, L0_tok_qkv_b, L0_tok_proj_w, L0_tok_proj_b)]
    laid = window_layout(*a)
    laid["txt"] = np.asarray(txt)
    laid["w2x"], laid["fold"] = attention_layout(np.asarray(L0_attn_W))
    laid.update(expert_layout(*[np.asarray(v) for v in (
        L0_ffn_gate_w, L0_ffn_gate_b, L0_ffn_w1, L0_ffn_b1, L0_ffn_w2, L0_ffn_b2, L0_ffn_gamma, L0_ffn_beta)]))
    order = ["xw", "txt", "wqk", "wv", "wp", "cols", "trig", "hmask", "ident", "w2x", "fold",
             "gate_w", "w1", "w2", "sel", "b2", "b1", "gate_b", "rows", "pick"]

    nc = bacc.Bacc("TRN2", target_bir_lowering=False, num_devices=1)
    arrays, args = {}, []
    for name in order:
        v = np.ascontiguousarray(laid[name])
        arrays[f"in_{name}_dram"] = v
        args.append(nc.dram_tensor(f"in_{name}_dram", v.shape, mybir.dt.from_np(v.dtype), kind="ExternalInput").ap())
    args.append(nc.dram_tensor("out_0_dram", (NPAIR + B, P, C), F32, kind="ExternalOutput").ap())
    fused_layer(nc, *args)
    got = run_bass_kernel_spmd(nc, [arrays], core_ids=[0]).results[0]["out_0_dram"]

    nw = SIDE // WIN
    img = got[:NPAIR].reshape(B, nw, nw // 2, 2, WIN, WIN, C).transpose(0, 1, 4, 2, 3, 5, 6)
    return np.concatenate([img.reshape(B, SIDE * SIDE, C), got[NPAIR:]], axis=1)
```
